# Optimizing a Trainium2 kernel written in Bass

```python
import numpy as np
import jax
import jax.numpy as jnp

def _softmax(x, axis=-1):
    return jax.nn.softmax(x, axis=axis)

def _gelu(x):
    return jax.nn.gelu(x, approximate=True)

def _silu(x):
    return jax.nn.silu(x)

def _sigmoid(x):
    return jax.nn.sigmoid(x)

def _layernorm(x, axis=-1, eps=1e-05):
    m = jnp.mean(x, axis=axis, keepdims=True)
    v = jnp.var(x, axis=axis, keepdims=True)
    return (x - m) / jnp.sqrt(v + eps)

def _scatter_add(tgt, idx, src, axis=0):
    return tgt.at[idx].add(src)

def _segment_sum(src, seg, n):
    return jax.ops.segment_sum(src, seg, n)
kernel_name = 'mk_recurrent_d1_jaxref_r4_e06a55'

def setup_inputs(seed: int=0):
    np.random.seed(seed)
    _w = jnp.asarray

    def _L0_attn_setup():
        import jax, jax.numpy as jnp
        import numpy as np
        D_MODEL = 256
        NUM_HEADS = 16
        D_K = D_MODEL // NUM_HEADS
        MAX_LEN = 256
        BATCH = 8
        SEQ = 256
        key = jax.random.key(seed)
        ks = jax.random.split(key, 12)
        s = 0.02
        inp = {'x': jax.random.normal(ks[0], (BATCH, SEQ, D_MODEL), dtype=jnp.float32), 'Wq': jax.random.normal(ks[1], (D_MODEL, D_MODEL), dtype=jnp.float32) * s, 'bq': jnp.zeros((D_MODEL,), dtype=jnp.float32), 'Wk': jax.random.normal(ks[2], (D_MODEL, D_MODEL), dtype=jnp.float32) * s, 'bk': jnp.zeros((D_MODEL,), dtype=jnp.float32), 'Wv': jax.random.normal(ks[3], (D_MODEL, D_MODEL), dtype=jnp.float32) * s, 'bv': jnp.zeros((D_MODEL,), dtype=jnp.float32), 'Wo': jax.random.normal(ks[4], (D_MODEL, D_MODEL), dtype=jnp.float32) * s, 'bo': jnp.zeros((D_MODEL,), dtype=jnp.float32), 'relative_k': jax.random.normal(ks[5], (2 * MAX_LEN - 1, D_K), dtype=jnp.float32), 'relative_v': jax.random.normal(ks[6], (2 * MAX_LEN - 1, D_K), dtype=jnp.float32)}
        return inp
    _L0_attn_in = _L0_attn_setup()

    def _L0_ffn_setup():
        import jax, jax.numpy as jnp
        import numpy as np
        D = 256
        H = 4
        HD = D // H
        E = 8
        FF = 1024
        CAP_FACTOR = 1.0

        def _ln(x, g, b, eps=1e-05):
            mu = jnp.mean(x, -1, keepdims=True)
            v = jnp.mean((x - mu) ** 2, -1, keepdims=True)
            return (x - mu) * jax.lax.rsqrt(v + eps) * g + b

        def _mha(x, w, b, ow, ob):
            L, N, _ = x.shape
            qkv = x @ w.T + b
            q, k, v = jnp.split(qkv, 3, axis=-1)
            rh = lambda t: t.reshape(L, N, H, HD).transpose(1, 2, 0, 3)
            q, k, v = (rh(q), rh(k), rh(v))
            scores = jnp.einsum('nhld,nhmd->nhlm', q, k) / np.float32(np.sqrt(HD))
            attn = jax.nn.softmax(scores, axis=-1)
            o = jnp.einsum('nhlm,nhmd->nhld', attn, v).transpose(2, 0, 1, 3).reshape(L, N, D)
            return o @ ow.T + ob

        def _moe(x, wg, w1, b1, w2, b2):
            L, N, _ = x.shape
            S = L * N
            cap = int(CAP_FACTOR * S) // E
            xf = x.reshape(S, D)
            gates = jax.nn.softmax(xf @ wg, axis=-1)
            idx = jnp.argmax(gates, axis=-1)
            mask1 = jax.nn.one_hot(idx, E, dtype=x.dtype)
            loc = jnp.sum((jnp.cumsum(mask1, 0) - 1.0) * mask1, -1).astype(jnp.int32)
            keep = loc < cap
            gate_val = jnp.take_along_axis(gates, idx[:, None], -1)[:, 0]
            slot = jnp.where(keep, idx.astype(jnp.int32) * cap + loc, E * cap)
            disp = jnp.zeros((E * cap, D), x.dtype).at[slot].set(xf, mode='drop')
            disp = disp.reshape(E, cap, D)
            h = jnp.einsum('ecd,edf->ecf', disp, w1) + b1[:, None, :]
            y = (jnp.einsum('ecf,efd->ecd', h, w2) + b2[:, None, :]).reshape(E * cap, D)
            out = jnp.where(keep[:, None], gate_val[:, None] * y[jnp.minimum(slot, E * cap - 1)], 0.0)
            return out.reshape(L, N, D)
        key = jax.random.key(seed)
        ks = jax.random.split(key, 8)
        L, N = (256, 16)
        s = 0.02
        return {'x': jax.random.normal(ks[0], (L, N, D), jnp.float32), 'in_proj_w': jax.random.normal(ks[1], (3 * D, D), jnp.float32) * s, 'in_proj_b': jnp.zeros((3 * D,), jnp.float32), 'out_proj_w': jax.random.normal(ks[2], (D, D), jnp.float32) * s, 'out_proj_b': jnp.zeros((D,), jnp.float32), 'ln1_g': jnp.ones((D,), jnp.float32), 'ln1_b': jnp.zeros((D,), jnp.float32), 'ln2_g': jnp.ones((D,), jnp.float32), 'ln2_b': jnp.zeros((D,), jnp.float32), 'wg': jax.random.normal(ks[3], (D, E), jnp.float32) * s, 'w1': jax.random.normal(ks[4], (E, D, FF), jnp.float32) * s, 'b1': jnp.zeros((E, FF), jnp.float32), 'w2': jax.random.normal(ks[5], (E, FF, D), jnp.float32) * s, 'b2': jnp.zeros((E, D), jnp.float32)}
    _L0_ffn_in = _L0_ffn_setup()
    _d = {'L0_attn_x': _L0_attn_in['x'], 'L0_attn_Wq': _L0_attn_in['Wq'], 'L0_attn_bq': _L0_attn_in['bq'], 'L0_attn_Wk': _L0_attn_in['Wk'], 'L0_attn_bk': _L0_attn_in['bk'], 'L0_attn_Wv': _L0_attn_in['Wv'], 'L0_attn_bv': _L0_attn_in['bv'], 'L0_attn_Wo': _L0_attn_in['Wo'], 'L0_attn_bo': _L0_attn_in['bo'], 'L0_attn_relative_k': _L0_attn_in['relative_k'], 'L0_attn_relative_v': _L0_attn_in['relative_v'], 'L0_ffn_in_proj_w': _L0_ffn_in['in_proj_w'], 'L0_ffn_in_proj_b': _L0_ffn_in['in_proj_b'], 'L0_ffn_out_proj_w': _L0_ffn_in['out_proj_w'], 'L0_ffn_out_proj_b': _L0_ffn_in['out_proj_b'], 'L0_ffn_ln1_g': _L0_ffn_in['ln1_g'], 'L0_ffn_ln1_b': _L0_ffn_in['ln1_b'], 'L0_ffn_ln2_g': _L0_ffn_in['ln2_g'], 'L0_ffn_ln2_b': _L0_ffn_in['ln2_b'], 'L0_ffn_wg': _L0_ffn_in['wg'], 'L0_ffn_w1': _L0_ffn_in['w1'], 'L0_ffn_b1': _L0_ffn_in['b1'], 'L0_ffn_w2': _L0_ffn_in['w2'], 'L0_ffn_b2': _L0_ffn_in['b2']}
    _x0 = _d['L0_attn_x']
    _d['L0_attn_x'] = jax.random.normal(jax.random.fold_in(jax.random.key(seed), 1), (2, 2048, 256), dtype=_x0.dtype)
    del _x0
    return _d

def reference(L0_attn_x, L0_attn_Wq, L0_attn_bq, L0_attn_Wk, L0_attn_bk, L0_attn_Wv, L0_attn_bv, L0_attn_Wo, L0_attn_bo, L0_attn_relative_k, L0_attn_relative_v, L0_ffn_in_proj_w, L0_ffn_in_proj_b, L0_ffn_out_proj_w, L0_ffn_out_proj_b, L0_ffn_ln1_g, L0_ffn_ln1_b, L0_ffn_ln2_g, L0_ffn_ln2_b, L0_ffn_wg, L0_ffn_w1, L0_ffn_b1, L0_ffn_w2, L0_ffn_b2):

    def _L0_attn_ref(x, Wq, bq, Wk, bk, Wv, bv, Wo, bo, relative_k, relative_v):
        import jax, jax.numpy as jnp
        import numpy as np
        D_MODEL = 256
        NUM_HEADS = 16
        D_K = D_MODEL // NUM_HEADS
        MAX_LEN = 256
        BATCH = 8
        SEQ = 256
        B, L, D = x.shape
        H, dk = (NUM_HEADS, D_K)
        Q = (x @ Wq.T + bq).reshape(B, L, H, dk).transpose(0, 2, 1, 3)
        K = (x @ Wk.T + bk).reshape(B, L, H, dk).transpose(0, 2, 1, 3)
        V = (x @ Wv.T + bv).reshape(B, L, H, dk).transpose(0, 2, 1, 3)
        rel_pos = jnp.arange(L)[None, :] - jnp.arange(L)[:, None] + (MAX_LEN - 1)
        rel_k = relative_k[rel_pos]
        rel_v = relative_v[rel_pos]
        scale = 1.0 / np.sqrt(dk).astype(np.float32)
        scores = jnp.einsum('bhld,bhrd->bhlr', Q, K) * scale
        scores = scores + jnp.einsum('bhld,lrd->bhlr', Q, rel_k)
        attn = jax.nn.softmax(scores, axis=-1)
        out = jnp.einsum('bhlr,bhrd->bhld', attn, V)
        out = out + jnp.einsum('bhlr,lrd->bhld', attn, rel_v)
        out = out.transpose(0, 2, 1, 3).reshape(B, L, D)
        return out @ Wo.T + bo

    def _L0_ffn_ref(x, in_proj_w, in_proj_b, out_proj_w, out_proj_b, ln1_g, ln1_b, ln2_g, ln2_b, wg, w1, b1, w2, b2):
        import jax, jax.numpy as jnp
        import numpy as np
        D = 256
        H = 4
        HD = D // H
        E = 8
        FF = 1024
        CAP_FACTOR = 1.0

        def _ln(x, g, b, eps=1e-05):
            mu = jnp.mean(x, -1, keepdims=True)
            v = jnp.mean((x - mu) ** 2, -1, keepdims=True)
            return (x - mu) * jax.lax.rsqrt(v + eps) * g + b

        def _mha(x, w, b, ow, ob):
            L, N, _ = x.shape
            qkv = x @ w.T + b
            q, k, v = jnp.split(qkv, 3, axis=-1)
            rh = lambda t: t.reshape(L, N, H, HD).transpose(1, 2, 0, 3)
            q, k, v = (rh(q), rh(k), rh(v))
            scores = jnp.einsum('nhld,nhmd->nhlm', q, k) / np.float32(np.sqrt(HD))
            attn = jax.nn.softmax(scores, axis=-1)
            o = jnp.einsum('nhlm,nhmd->nhld', attn, v).transpose(2, 0, 1, 3).reshape(L, N, D)
            return o @ ow.T + ob

        def _moe(x, wg, w1, b1, w2, b2):
            L, N, _ = x.shape
            S = L * N
            cap = int(CAP_FACTOR * S) // E
            xf = x.reshape(S, D)
            gates = jax.nn.softmax(xf @ wg, axis=-1)
            idx = jnp.argmax(gates, axis=-1)
            mask1 = jax.nn.one_hot(idx, E, dtype=x.dtype)
            loc = jnp.sum((jnp.cumsum(mask1, 0) - 1.0) * mask1, -1).astype(jnp.int32)
            keep = loc < cap
            gate_val = jnp.take_along_axis(gates, idx[:, None], -1)[:, 0]
            slot = jnp.where(keep, idx.astype(jnp.int32) * cap + loc, E * cap)
            disp = jnp.zeros((E * cap, D), x.dtype).at[slot].set(xf, mode='drop')
            disp = disp.reshape(E, cap, D)
            h = jnp.einsum('ecd,edf->ecf', disp, w1) + b1[:, None, :]
            y = (jnp.einsum('ecf,efd->ecd', h, w2) + b2[:, None, :]).reshape(E * cap, D)
            out = jnp.where(keep[:, None], gate_val[:, None] * y[jnp.minimum(slot, E * cap - 1)], 0.0)
            return out.reshape(L, N, D)
        y1 = _ln(x + _mha(x, in_proj_w, in_proj_b, out_proj_w, out_proj_b), ln1_g, ln1_b)
        y2 = _ln(y1 + _moe(y1, wg, w1, b1, w2, b2), ln2_g, ln2_b)
        return y2
    x = L0_attn_x
    xn = _layernorm(x, axis=-1)
    s = _L0_attn_ref(xn, L0_attn_Wq, L0_attn_bq, L0_attn_Wk, L0_attn_bk, L0_attn_Wv, L0_attn_bv, L0_attn_Wo, L0_attn_bo, L0_attn_relative_k, L0_attn_relative_v)
    g = _silu(_L0_ffn_ref(xn, L0_ffn_in_proj_w, L0_ffn_in_proj_b, L0_ffn_out_proj_w, L0_ffn_out_proj_b, L0_ffn_ln1_g, L0_ffn_ln1_b, L0_ffn_ln2_g, L0_ffn_ln2_b, L0_ffn_wg, L0_ffn_w1, L0_ffn_b1, L0_ffn_w2, L0_ffn_b2))
    x = x + s * g
    return x

_drawn_inputs = setup_inputs


def setup_inputs(seed=0):
    import zlib

    import numpy as np

    out = dict(_drawn_inputs(seed))
    spreads = {'L0_attn_bq': (0.0, 0.599),
     'L0_attn_bk': (0.0, 0.8),
     'L0_attn_bv': (0.0, 0.39),
     'L0_attn_bo': (0.0, 0.1),
     'L0_ffn_in_proj_b': (0.0, 0.8),
     'L0_ffn_out_proj_b': (0.0, 0.697),
     'L0_ffn_ln1_g': (1.0, 0.6),
     'L0_ffn_ln1_b': (0.0, 0.762),
     'L0_ffn_ln2_g': (1.0, 0.6),
     'L0_ffn_ln2_b': (0.0, 0.792),
     'L0_ffn_b1': (0.0, 0.8),
     'L0_ffn_b2': (0.0, 0.8)}
    factors = {'L0_attn_Wk': 8.0,
     'L0_attn_Wv': 8.0,
     'L0_ffn_in_proj_w': 7.124,
     'L0_ffn_out_proj_w': 6.42,
     'L0_ffn_wg': 8.0,
     'L0_ffn_w1': 8.0,
     'L0_ffn_w2': 8.0}
    for name, (base, spread) in spreads.items():
        noise = np.random.default_rng([zlib.crc32(name.encode()), seed]).standard_normal(out[name].shape)
        drawn = base * np.exp(spread * noise) if base else spread * noise
        out[name] = jnp.asarray(drawn.astype(out[name].dtype))
    for name, factor in factors.items():
        out[name] = (out[name] * factor).astype(out[name].dtype)
    return out
```

```python
from contextlib import ExitStack

import concourse.bass as bass
from concourse import mybir

F32 = mybir.dt.float32
BF16 = mybir.dt.bfloat16
FP16 = mybir.dt.float16
U32 = mybir.dt.uint32
I32 = mybir.dt.int32
ALU = mybir.AluOpType
ACT = mybir.ActivationFunctionType
AX_X = mybir.AxisListType.X
ds = bass.ds

P = 128
B, L, D = 2, 2048, 256
TOK = B * L
NT = TOK // P
H, DK = 16, 16
HH = H // 2
NC = B * 2
NI = L // P
W = HH * P
MAXLEN = 256
REL = 2 * MAXLEN - 1
EPS = 1e-5
FH, FHD = 4, 64
E, FF, CAP = 8, 1024, TOK // 8
CH = 4
NCH = NT // CH

BAND, HI, LO = 0, 1, 2
KS = [0, 1, 2, -1, -2, -3, -4, -5, -6, 3, 4, 5, 6, 7, 8, 9]
NB = 9
LOWEST = -6 * P - (P - 1)
HIGHEST = 2 * P + (P - 1)
SPAN = HIGHEST - LOWEST + 1
TSW = SPAN - 7
TVU = SPAN - P + 1
TERMS = 6
PARTS = 3
QROWS = TERMS * DK
ROWS = QROWS + PARTS
PAIRS = [(0, 0), (0, 1), (1, 0)]

C_ID, C_FOLD, C_PICK, C_DEN, C_MASK, C_MASKV, C_TRI, C_ONE, C_HEAD, C_IOTA, C_CAPE = 0, 128, 368, 560, 752, 760, 768, 896, 1024, 1032, 1040
C_N = 1048

START = 1


def start_counts(nc, sems):
    with nc.Block() as block:
        @block.sync
        def _(sp):
            for s in sems.values():
                sp.sem_inc(s, START)


def phase_project(nc, ins, dr, sem, sb, ps):
    xn_all, qkv_all = dr["xn_all"], dr["qkv_all"]
    wq, wk, wv, wi = sb("wq", [P, 2, D]), sb("wk", [P, 2, D]), sb("wv", [P, 2, D]), sb("wi", [P, 2, 3 * D])
    bqk = sb("bqk", [P, 4])
    bv, bi = sb("bv", [P, D]), sb("bi", [P, 3 * D])
    cst = sb("cst1", [P, C_N])
    tc2 = sb("tc2", [P, 2])
    selc = sb("selc", [P, 2, HH])
    xc = sb("xc", [P, 2, CH, D])
    stat, mv = sb("stat", [P, CH, 6]), sb("mv", [P, CH, 2])
    std, rstd = sb("std", [P, CH]), sb("rstd", [P, CH])
    xnc = sb("xnc", [P, CH, D])
    pause = sb("pause", [P, 1])
    xT = sb("xT", [P, 2, CH * P])
    qf = sb("qf", [P, 2, CH * P])
    res = sb("res", [P, CH * P])
    pair = sb("pair", [P, 2, 2, CH * P], FP16)
    part = sb("part", [P, 2, PARTS, CH * P], BF16)
    cres = sb("cres", [2 * HH, CH * P])
    cf = sb("cf", [2 * HH, CH * P])
    cpart = sb("cpart", [2 * HH, PARTS, CH * P], BF16)
    vs = sb("vs", [P, CH, D])
    tp = ps("tp", [P, 2, CH * P])
    pq = ps("pq", [P, 2, CH * P])
    pc = ps("pc", [P, CH * P])
    pv = ps("pv", [P, D])
    pi = ps("pi", [P, 2, 512])

    S = {n: sem("a_" + n) for n in (
        "weights xload stats aggr eps std rstd normed kept tp_done xT proj qf p0 r1 p1 p2 hi lo cmm cf c0 cr1 c1 c2 vmm vout "
        "imm iout qstore0 qstore1 cstore vstore selc tabl tabl2").split()}

    start_counts(nc, S)
    with nc.Block() as block:
        @block.sync
        def _(sp):
            for t, s in ((wq, "wqT"), (wk, "wkT"), (wv, "wvT"), (wi, "wiT")):
                sp.dma_start(t[:], ins[s].rearrange("(k p) n -> p k n", p=P)).then_inc(S["weights"], 16)
            sp.dma_start(bqk[:], ins["bqk"]).then_inc(S["weights"], 16)
            sp.dma_start(bv[:], ins["bv"].partition_broadcast(P)).then_inc(S["weights"], 16)
            sp.dma_start(bi[:], ins["bi"].partition_broadcast(P)).then_inc(S["weights"], 16)
            sp.dma_start(cst[:], ins["consts"]).then_inc(S["weights"], 16)
            for n, row in ((0, REL - 1), (1, 0)):
                src = bass.AP(ins["rk"].tensor, row * DK, [[1, DK], [0, HH], [1, 1]])
                sp.dma_start(tc2[:, n:n + 1], src).then_inc(S["weights"], 16)
            tk, rkT = dr["tk"], ins["rkT"]
            lo, mid = 129, 129 + REL
            sp.dma_start(tk[:, lo:mid], rkT).then_inc(S["tabl"], 16)
            sp.dma_start(tk[:, mid:mid + REL], rkT).then_inc(S["tabl"], 16)
            sp.dma_start(tk[:, 0:lo], bass.AP(rkT.tensor, 0, [[REL, DK], [0, lo], [1, 1]])).then_inc(S["tabl"], 16)
            sp.dma_start(tk[:, mid + REL:SPAN],
                         bass.AP(rkT.tensor, REL - 1, [[REL, DK], [0, P], [1, 1]])).then_inc(S["tabl"], 16)
            tv, rv = dr["tv"], ins["rv"]
            sp.dma_start(tv[0:lo, :], bass.AP(rv.tensor, 0, [[0, lo], [1, DK]])).then_inc(S["tabl"], 16)
            sp.dma_start(tv[lo:mid, :], rv).then_inc(S["tabl"], 16)
            sp.dma_start(tv[mid:mid + REL, :], rv).then_inc(S["tabl"], 16)
            sp.dma_start(tv[mid + REL:SPAN, :],
                         bass.AP(rv.tensor, (REL - 1) * DK, [[0, P], [1, DK]])).then_inc(S["tabl"], 16)
            xv = ins["x"].rearrange("(c a p) n -> p c a n", a=CH, p=P)
            with sp.Fori(0, NCH // 2) as h:
                for u in range(2):
                    ch = h * 2 + u
                    sp.wait_ge(S["kept"], START + h * 2)
                    sp.dma_start(xc[:, u], xv[:, ds(ch, 1)].rearrange("p c a n -> p (c a) n")).then_inc(S["xload"], 16)
                    for n in range(4):
                        ready = ch * 4 + n + 1
                        sp.wait_ge(S["p2"], START + ready)
                        dst = dr["qs"] if n < 2 else dr["ks"]
                        row = (ch // 4) * (2 * NI) + (n % 2) * NI + (ch % 4) * CH
                        for q in range(PARTS):
                            d = dst[ds(row, CH), q * W * DK:(q + 1) * W * DK].rearrange("i (p l) -> p i l", l=P)
                            sp.dma_start(d, part[:, n % 2, q, :].rearrange("p (i l) -> p i l", l=P)).then_inc(S[f"qstore{n % 2}"], 16)
                        if n < 2:
                            for q in range(2):
                                d = dr["qp"][ds(row, CH), q, :].rearrange("i (p l) -> p i l", l=P)
                                sp.dma_start(d, pair[:, n, q, :].rearrange("p (i l) -> p i l", l=P)).then_inc(S[f"qstore{n % 2}"], 16)
                            sp.wait_ge(S["c2"], START + ch * 2 + n + 1)
                            for q in range(PARTS):
                                for cl in range(2):
                                    d = dr["cs"][ds(row, CH), cl, q, :, :].rearrange("i h l -> h i l")
                                    sp.dma_start(d, cpart[cl * HH:(cl + 1) * HH, q, :].rearrange("h (i l) -> h i l", l=P)).then_inc(S["cstore"], 16)
                    sp.wait_ge(S["vout"], START + ch * CH + CH)
                    sp.dma_start(dr["v"].rearrange("(c a p) n -> p c a n", a=CH, p=P)[:, ds(ch, 1)].rearrange("p c a n -> p (c a) n"),
                                 vs[:]).then_inc(S["vstore"], 16)
            sp.wait_ge(S["tabl"], START + 16 * 8)
            for n in range(2):
                sp.wait_ge(S[f"qstore{n}"], START + 128 * NCH)
            sp.wait_ge(S["cstore"], START + 16 * 12 * NCH)
            sp.wait_ge(S["vstore"], START + 16 * NCH)

        @block.vector
        def _(dve):
            dve.wait_ge(S["weights"], START + 16 * 10)
            for n in range(2):
                nc.vector.tensor_scalar(selc[:, n, :], cst[:, C_HEAD:C_HEAD + HH], tc2[:, n:n + 1], None, ALU.mult).then_inc(S["selc"], 1)
            with dve.Fori(0, NCH // 2) as h:
                for u in range(2):
                    ch = h * 2 + u
                    dve.wait_ge(S["xload"], START + ch * 16 + 16)
                    for a in range(CH):
                        nc.vector.bn_stats(stat[:, a, :], xc[:, u, a, :]).then_inc(S["stats"], 1)
                    dve.wait_ge(S["stats"], START + ch * CH + CH)
                    nc.vector.memset(pause[:], 0.0)
                    for a in range(CH):
                        nc.vector.bn_aggr(mv[:, a, :], stat[:, a, :]).then_inc(S["aggr"], 1)
                    dve.wait_ge(S["aggr"], START + ch * CH + CH)
                    nc.vector.tensor_scalar(std[:], mv[:, :, 1], EPS, None, ALU.add).then_inc(S["eps"], 1)
                    dve.wait_ge(S["std"], START + ch + 1)
                    nc.vector.reciprocal(rstd[:], std[:]).then_inc(S["rstd"], 1)
                    dve.wait_ge(S["rstd"], START + ch + 1)
                    dve.wait_ge(S["tp_done"], START + ch)
                    dve.wait_ge(S["kept"], START + ch)
                    for a in range(CH):
                        nc.vector.tensor_scalar(xnc[:, a, :], xc[:, u, a, :], mv[:, a, 0:1], rstd[:, a:a + 1],
                                                ALU.subtract, ALU.mult).then_inc(S["normed"], 1)
                    for n in range(4):
                        k = ch * 4 + n
                        dve.wait_ge(S["proj"], START + k + 1)
                        dve.wait_ge(S[f"qstore{n % 2}"], START + ch * 128 + (80 if n >= 2 else 0))
                        dve.wait_ge(S["p2"], START + k)
                        if n < 2:
                            nc.vector.tensor_scalar(qf[:, n % 2, :], pq[:, n % 2, :], bqk[:, n:n + 1], None, ALU.add).then_inc(S["qf"], 1)
                        else:
                            nc.vector.tensor_scalar(qf[:, n % 2, :], pq[:, n % 2, :], bqk[:, n:n + 1], DK ** -0.5,
                                                    ALU.add, ALU.mult).then_inc(S["qf"], 1)
                        dve.wait_ge(S["p0"], START + k + 1)
                        nc.vector.tensor_tensor(res[:], qf[:, n % 2, :], part[:, n % 2, 0, :], ALU.subtract).then_inc(S["r1"], 1)
                        if n < 2:
                            dve.wait_ge(S["hi"], START + ch * 2 + n + 1)
                            nc.vector.tensor_tensor(pair[:, n, 1, :], qf[:, n, :], pair[:, n, 0, :], ALU.subtract).then_inc(S["lo"], 1)
                        dve.wait_ge(S["p1"], START + k + 1)
                        nc.vector.tensor_tensor(part[:, n % 2, 2, :], res[:], part[:, n % 2, 1, :], ALU.subtract).then_inc(S["p2"], 1)
                        if n < 2:
                            k = ch * 2 + n
                            dve.wait_ge(S["cmm"], START + k + 1)
                            dve.wait_ge(S["cstore"], START + k * 96)
                            dve.wait_ge(S["c2"], START + k)
                            nc.vector.tensor_copy(cf[:], pc[0:2 * HH, :]).then_inc(S["cf"], 1)
                            dve.wait_ge(S["cf"], START + k + 1)
                            nc.vector.tensor_copy(cpart[:, 0, :], cf[:]).then_inc(S["c0"], 1)
                            dve.wait_ge(S["c0"], START + k + 1)
                            nc.vector.tensor_tensor(cres[:], cf[:], cpart[:, 0, :], ALU.subtract).then_inc(S["cr1"], 1)
                            dve.wait_ge(S["cr1"], START + k + 1)
                            nc.vector.tensor_copy(cpart[:, 1, :], cres[:]).then_inc(S["c1"], 1)
                            dve.wait_ge(S["c1"], START + k + 1)
                            nc.vector.tensor_tensor(cpart[:, 2, :], cres[:], cpart[:, 1, :], ALU.subtract).then_inc(S["c2"], 1)
                    dve.wait_ge(S["vstore"], START + ch * 16)
                    for a in range(CH):
                        dve.wait_ge(S["vmm"], START + ch * CH + a + 1)
                        nc.vector.tensor_tensor(vs[:, a, :], pv[:], bv[:], ALU.add).then_inc(S["vout"], 1)
                        dve.wait_ge(S["imm"], START + ch * CH + a + 1)
                        out = qkv_all[:, ds(ch * CH + a, 1), :].rearrange("p a n -> p (a n)")
                        nc.vector.tensor_tensor(out[:, 0:512], pi[:, 0, :], bi[:, 0:512], ALU.add)
                        nc.vector.tensor_tensor(out[:, 512:768], pi[:, 1, 0:256], bi[:, 512:768], ALU.add).then_inc(S["iout"], 1)

        @block.scalar
        def _(act):
            with act.Fori(0, NCH) as ch:
                act.wait_ge(S["eps"], START + ch + 1)
                nc.scalar.activation(std[:], std[:], ACT.Sqrt).then_inc(S["std"], 1)
                act.wait_ge(S["tp_done"], START + ch + 1)
                act.wait_ge(S["imm"], START + ch * CH)
                for k in range(2):
                    nc.scalar.activation(xT[:, k, :], tp[:, k, :], ACT.Copy).then_inc(S["xT"], 1)
                for n in range(4):
                    act.wait_ge(S["qf"], START + ch * 4 + n + 1)
                    nc.scalar.activation(part[:, n % 2, 0, :], qf[:, n % 2, :], ACT.Copy).then_inc(S["p0"], 1)
                    if n < 2:
                        nc.scalar.activation(pair[:, n, 0, :], qf[:, n, :], ACT.Copy).then_inc(S["hi"], 1)
                    act.wait_ge(S["r1"], START + ch * 4 + n + 1)
                    nc.scalar.activation(part[:, n % 2, 1, :], res[:], ACT.Copy).then_inc(S["p1"], 1)

        @block.gpsimd
        def _(pool):
            with pool.Fori(0, NCH) as ch:
                pool.wait_ge(S["normed"], START + ch * CH + CH)
                nc.gpsimd.tensor_copy(xn_all[:, ds(ch * CH, CH), :], xnc[:]).then_inc(S["kept"], 1)

        @block.tensor
        def _(pe):
            pe.wait_ge(S["weights"], START + 16 * 10)
            pe.wait_ge(S["selc"], START + 2)
            ident = cst[:, C_ID:C_ID + P]
            with pe.Fori(0, NCH) as ch:
                pe.wait_ge(S["normed"], START + ch * CH + CH)
                pe.wait_ge(S["xT"], START + ch * 2)
                for k in range(2):
                    for a in range(CH):
                        last = nc.tensor.transpose(tp[:, k, a * P:(a + 1) * P], xnc[:, a, k * P:(k + 1) * P], ident)
                last.then_inc(S["tp_done"], 1)
                pe.wait_ge(S["xT"], START + ch * 2 + 2)
                for n in range(4):
                    w, half = (wq, n) if n < 2 else (wk, n - 2)
                    pe.wait_ge(S["qf"], START + ch * 4 + (n - 1 if n > 1 else 0))
                    for k in range(2):
                        last = nc.tensor.matmul(pq[:, n % 2, :], w[:, k, half * P:(half + 1) * P], xT[:, k, :],
                                                start=(k == 0), stop=(k == 1))
                    last.then_inc(S["proj"], 1)
                    if n < 2:
                        pe.wait_ge(S["qf"], START + ch * 4 + n + 1)
                        pe.wait_ge(S["cf"], START + ch * 2 + n)
                        nc.tensor.matmul(pc[0:2 * HH, :], selc[:].rearrange("p c h -> p (c h)"), qf[:, n % 2, :],
                                         start=True, stop=True).then_inc(S["cmm"], 1)
                for a in range(CH):
                    pe.wait_ge(S["vout"], START + ch * CH + a)
                    for k in range(2):
                        last = nc.tensor.matmul(pv[:], xT[:, k, a * P:(a + 1) * P], wv[:, k, :], start=(k == 0), stop=(k == 1))
                    last.then_inc(S["vmm"], 1)
                    pe.wait_ge(S["iout"], START + ch * CH + a)
                    for c in range(2):
                        n = 512 if c == 0 else 256
                        for k in range(2):
                            last = nc.tensor.matmul(pi[:, c, 0:n], xT[:, k, a * P:(a + 1) * P], wi[:, k, c * 512:c * 512 + n],
                                                    start=(k == 0), stop=(k == 1))
                    last.then_inc(S["imm"], 1)


def phase_pairs(nc, ins, dr, sem, sb, ps):
    xn_all, qkv_all, y1_all, logits = dr["xn_all"], dr["qkv_all"], dr["y1_all"], dr["logits"]
    wo, wg = sb("wo2", [P, 2, D]), sb("wg2", [P, 2, E])
    bo, g1, b1 = sb("bo2", [P, D]), sb("g1", [P, D]), sb("b1_", [P, D])
    cst = sb("cst2", [P, P])
    zero = sb("zero", [P, D])
    prod = sb("prod", [P, 2, 2, D])
    s = sb("s", [P, 2, 2, FH])
    m = sb("m", [P, 2, FH])
    r = sb("r", [P, 2, FH])
    pv_ = sb("pvp", [P, 2, 2, D])
    o = sb("o", [P, 2, D])
    oT = sb("oT", [P, 2, 2, P])
    z = sb("z", [P, 2, D])
    stat, mv = sb("stat2", [P, 2, 6]), sb("mv2", [P, 2, 2])
    std, rstd = sb("std2", [P, 2]), sb("rstd2", [P, 2])
    y1 = sb("y1", [P, 2, D])
    pause = sb("pause2", [P, 1])
    y1T = sb("y1T", [P, 2, 2, P])
    tp = ps("tp2", [P, 2, 2, P])
    po = ps("po", [P, 2, D])
    ty = ps("ty", [P, 2, 2, P])
    pl = ps("pl", [P, 2, E])

    S = {n: sem("b_" + n) for n in (
        "weights prod0 prod1 s0 s1 max diff exp sum rec prob vprod o tp oT proj z0 z1 stats aggr eps std rstd n0 n1 y1 kept "
        "ty y1T logit lout zset zeroed").split()}

    start_counts(nc, S)
    with nc.Block() as block:
        @block.sync
        def _(sp):
            sp.dma_start(wo[:], ins["woT"].rearrange("(k p) n -> p k n", p=P)).then_inc(S["weights"], 16)
            sp.dma_start(wg[:], ins["wg"].rearrange("(k p) n -> p k n", p=P)).then_inc(S["weights"], 16)
            for t, n in ((bo, "bo_f"), (g1, "g1"), (b1, "b1ln")):
                sp.dma_start(t[:], ins[n].partition_broadcast(P)).then_inc(S["weights"], 16)
            sp.dma_start(cst[:], ins["consts"][:, C_ID:C_ID + P]).then_inc(S["weights"], 16)
            sp.wait_ge(S["zset"], START + 1)
            for t in range(NT):
                sp.dma_start(dr["disp"][t * P:(t + 1) * P, :], zero[:]).then_inc(S["zeroed"], 16)
            sp.wait_ge(S["zeroed"], START + 16 * NT)

        @block.vector
        def _(dve):
            nc.vector.memset(zero[:], 0.0).then_inc(S["zset"], 1)
            dve.wait_ge(S["weights"], START + 16 * 6)
            kv = qkv_all[:].rearrange("p (b t) n -> p b t n", b=2)
            with dve.Fori(0, NI) as t:
                for b in range(2):
                    q = kv[:, b, ds(t, 1), 0:D]
                    for c in range(2):
                        nc.vector.tensor_tensor(prod[:, b, c, :].unsqueeze(1), q, kv[:, c, ds(t, 1), D:2 * D], ALU.mult).then_inc(S[f"prod{b}"], 1)
                for b in range(2):
                    dve.wait_ge(S[f"prod{b}"], START + t * 2 + 2)
                    dve.wait_ge(S["vprod"], START + t * 4)
                    nc.vector.tensor_reduce(s[:, b].rearrange("p c h -> p (c h)"),
                                            prod[:, b].rearrange("p c (h d) -> p (c h) d", h=FH), AX_X, ALU.add).then_inc(S[f"s{b}"], 1)
                for b in range(2):
                    dve.wait_ge(S[f"s{b}"], START + t + 1)
                nc.vector.tensor_tensor(m[:], s[:, :, 0, :], s[:, :, 1, :], ALU.max).then_inc(S["max"], 1)
                dve.wait_ge(S["max"], START + t + 1)
                for c in range(2):
                    nc.vector.tensor_tensor(s[:, :, c, :], s[:, :, c, :], m[:], ALU.subtract).then_inc(S["diff"], 1)
                dve.wait_ge(S["exp"], START + t + 1)
                nc.vector.tensor_tensor(m[:], s[:, :, 0, :], s[:, :, 1, :], ALU.add).then_inc(S["sum"], 1)
                dve.wait_ge(S["sum"], START + t + 1)
                nc.vector.reciprocal(r[:], m[:]).then_inc(S["rec"], 1)
                dve.wait_ge(S["rec"], START + t + 1)
                for c in range(2):
                    nc.vector.tensor_tensor(s[:, :, c, :], s[:, :, c, :], r[:], ALU.mult).then_inc(S["prob"], 1)
                dve.wait_ge(S["proj"], START + t + 1)
                nc.vector.tensor_tensor(z[:], po[:], bo[:].unsqueeze(1).to_broadcast([P, 2, D]), ALU.add).then_inc(S["z0"], 1)
                dve.wait_ge(S["z0"], START + t + 1)
                xv = xn_all[:].rearrange("p (b t) n -> p b t n", b=2)
                for b in range(2):
                    nc.vector.tensor_tensor(z[:, b:b + 1, :], z[:, b:b + 1, :], xv[:, b, ds(t, 1), :], ALU.add).then_inc(S["z1"], 1)
                for b in range(2):
                    dve.wait_ge(S["z1"], START + t * 2 + b + 1)
                    nc.vector.bn_stats(stat[:, b, :], z[:, b, :]).then_inc(S["stats"], 1)
                dve.wait_ge(S["stats"], START + t * 2 + 2)
                nc.vector.memset(pause[:], 0.0)
                for b in range(2):
                    nc.vector.bn_aggr(mv[:, b, :], stat[:, b, :]).then_inc(S["aggr"], 1)
                dve.wait_ge(S["aggr"], START + t * 2 + 2)
                nc.vector.tensor_scalar(std[:], mv[:, :, 1], EPS, None, ALU.add).then_inc(S["eps"], 1)
                dve.wait_ge(S["std"], START + t + 1)
                nc.vector.reciprocal(rstd[:], std[:]).then_inc(S["rstd"], 1)
                dve.wait_ge(S["rstd"], START + t + 1)
                for b in range(2):
                    nc.vector.tensor_scalar(z[:, b, :], z[:, b, :], mv[:, b, 0:1], rstd[:, b:b + 1],
                                            ALU.subtract, ALU.mult).then_inc(S["n0"], 1)
                dve.wait_ge(S["n0"], START + t * 2 + 2)
                nc.vector.tensor_tensor(z[:], z[:], g1[:].unsqueeze(1).to_broadcast([P, 2, D]), ALU.mult).then_inc(S["n1"], 1)
                dve.wait_ge(S["n1"], START + t + 1)
                dve.wait_ge(S["kept"], START + t * 2)
                dve.wait_ge(S["ty"], START + t)
                nc.vector.tensor_tensor(y1[:], z[:], b1[:].unsqueeze(1).to_broadcast([P, 2, D]), ALU.add).then_inc(S["y1"], 1)
                dve.wait_ge(S["logit"], START + t + 1)
                lv = logits[:].rearrange("p (b t) e -> p b t e", b=2)
                for b in range(2):
                    nc.vector.tensor_copy(lv[:, b, ds(t, 1), :], pl[:, b:b + 1, :]).then_inc(S["lout"], 1)

        @block.gpsimd
        def _(pool):
            kv = qkv_all[:].rearrange("p (b t) n -> p b t n", b=2)
            with pool.Fori(0, NI) as t:
                pool.wait_ge(S["prob"], START + t * 2 + 2)
                for b in range(2):
                    for c in range(2):
                        nc.gpsimd.tensor_tensor(pv_[:, b, c, :].rearrange("p (h d) -> p h d", h=FH),
                                                kv[:, c, ds(t, 1), 2 * D:3 * D].rearrange("p t (h d) -> p (t h) d", h=FH),
                                                s[:, b, c, :].unsqueeze(2).to_broadcast([P, FH, FHD]), ALU.mult).then_inc(S["vprod"], 1)
                pool.wait_ge(S["vprod"], START + t * 4 + 4)
                pool.wait_ge(S["tp"], START + t)
                nc.gpsimd.tensor_tensor(o[:], pv_[:, :, 0, :], pv_[:, :, 1, :], ALU.add).then_inc(S["o"], 1)
                pool.wait_ge(S["y1"], START + t + 1)
                yv = y1_all[:].rearrange("p (b t) n -> p b t n", b=2)
                for b in range(2):
                    nc.gpsimd.tensor_copy(yv[:, b, ds(t, 1), :], y1[:, b:b + 1, :]).then_inc(S["kept"], 1)

        @block.scalar
        def _(act):
            with act.Fori(0, NI) as t:
                act.wait_ge(S["diff"], START + t * 2 + 2)
                nc.scalar.activation(s[:], s[:], ACT.Exp, scale=FHD ** -0.5).then_inc(S["exp"], 1)
                act.wait_ge(S["tp"], START + t + 1)
                act.wait_ge(S["proj"], START + t)
                nc.scalar.activation(oT[:], tp[:], ACT.Copy).then_inc(S["oT"], 1)
                act.wait_ge(S["eps"], START + t + 1)
                nc.scalar.activation(std[:], std[:], ACT.Sqrt).then_inc(S["std"], 1)
                act.wait_ge(S["ty"], START + t + 1)
                act.wait_ge(S["logit"], START + t)
                nc.scalar.activation(y1T[:], ty[:], ACT.Copy).then_inc(S["y1T"], 1)

        @block.tensor
        def _(pe):
            pe.wait_ge(S["weights"], START + 16 * 6)
            with pe.Fori(0, NI) as t:
                pe.wait_ge(S["o"], START + t + 1)
                pe.wait_ge(S["oT"], START + t)
                for b in range(2):
                    for k in range(2):
                        last = nc.tensor.transpose(tp[:, b, k, :], o[:, b, k * P:(k + 1) * P], cst[:])
                last.then_inc(S["tp"], 1)
                pe.wait_ge(S["oT"], START + t + 1)
                pe.wait_ge(S["z0"], START + t)
                for b in range(2):
                    for k in range(2):
                        last = nc.tensor.matmul(po[:, b, :], oT[:, b, k, :], wo[:, k, :], start=(k == 0), stop=(k == 1))
                last.then_inc(S["proj"], 1)
                pe.wait_ge(S["y1"], START + t + 1)
                pe.wait_ge(S["y1T"], START + t)
                for b in range(2):
                    for k in range(2):
                        last = nc.tensor.transpose(ty[:, b, k, :], y1[:, b, k * P:(k + 1) * P], cst[:])
                last.then_inc(S["ty"], 1)
                pe.wait_ge(S["y1T"], START + t + 1)
                pe.wait_ge(S["lout"], START + t * 2)
                for b in range(2):
                    for k in range(2):
                        last = nc.tensor.matmul(pl[:, b, :], y1T[:, b, k, :], wg[:, k, :], start=(k == 0), stop=(k == 1))
                last.then_inc(S["logit"], 1)


def phase_route(nc, ins, dr, sem, sb, ps):
    y1_all, logits, gate, slot_u, back_u = dr["y1_all"], dr["logits"], dr["gate"], dr["slot_u"], dr["back_u"]
    n = [P, NT, E]
    cst = sb("cst3", [P, C_N])
    mx, rec = sb("mx", [P, NT]), sb("rec", [P, NT])
    ex, hot, rank = sb("ex", n), sb("hot", n), sb("rank", n)
    pre, tot = sb("pre", n), sb("tot", [P, E, 2 * NT])
    tot2 = sb("tot2", [P, E, 2 * NT])
    loc, idx, keep, slot = sb("loc", [P, NT]), sb("idx", [P, NT]), sb("keep", [P, NT]), sb("slot", [P, NT])
    tmp = sb("tmp", [P, NT])
    pp, pt = ps("pp", n), ps("pt", n)
    s_cst, s_v, s_exp, s_hot, s_cum, s_sc = sem("c_cst"), sem("c_steps"), sem("c_exp"), sem("c_hot"), sem("c_cum"), sem("c_scattered")
    s_slot = sem("c_slots")

    with nc.Block() as block:
        @block.sync
        def _(sp):
            sp.dma_start(cst[:], ins["consts"]).then_inc(s_cst, 16)

        @block.scalar
        def _(act):
            act.wait_ge(s_v, 2)
            nc.scalar.activation(ex[:], ex[:], ACT.Exp).then_inc(s_exp, 1)

        @block.tensor
        def _(pe):
            pe.wait_ge(s_cst, 16)
            pe.wait_ge(s_hot, 1)
            nc.tensor.matmul(pp[:], cst[:, C_TRI:C_TRI + P], hot[:], start=True, stop=True)
            nc.tensor.matmul(pt[:], cst[:, C_ONE:C_ONE + P], hot[:], start=True, stop=True).then_inc(s_cum, 1)

        @block.vector
        def _(dve):
            step = [0]

            def done(ins_):
                step[0] += 1
                ins_.then_inc(s_v, 1)
                dve.wait_ge(s_v, step[0])

            def wide(t):
                return t[:].unsqueeze(2).to_broadcast(n)

            done(nc.vector.tensor_reduce(mx[:], logits[:], AX_X, ALU.max))
            done(nc.vector.tensor_tensor(ex[:], logits[:], wide(mx), ALU.subtract))
            dve.wait_ge(s_exp, 1)
            done(nc.vector.tensor_reduce(tmp[:], ex[:], AX_X, ALU.add))
            done(nc.vector.reciprocal(rec[:], tmp[:]))
            done(nc.vector.tensor_reduce(mx[:], ex[:], AX_X, ALU.max))
            done(nc.vector.tensor_tensor(gate[:], mx[:], rec[:], ALU.mult))
            done(nc.vector.tensor_tensor(hot[:], ex[:], wide(mx), ALU.is_ge))
            dve.wait_ge(s_cst, 16)
            done(nc.vector.tensor_tensor(rank[:], hot[:], cst[:, C_IOTA:C_IOTA + E].unsqueeze(1).to_broadcast(n), ALU.mult))
            done(nc.vector.tensor_reduce(mx[:], rank[:], AX_X, ALU.max))
            nc.vector.tensor_tensor(hot[:], cst[:, C_IOTA:C_IOTA + E].unsqueeze(1).to_broadcast(n), wide(mx),
                                    ALU.is_equal).then_inc(s_hot, 1)
            dve.wait_ge(s_cum, 1)
            done(nc.vector.tensor_copy(pre[:], pp[:]))
            done(nc.vector.memset(tot[:], 0.0))
            done(nc.vector.memset(tot2[:], 0.0))
            done(nc.vector.tensor_copy(tot[:, :, NT + 1:2 * NT], pt[:, 0:NT - 1, :].rearrange("p t e -> p e t")))
            a, b = tot, tot2
            d = 1
            while d < NT:
                done(nc.vector.tensor_tensor(b[:, :, NT:2 * NT], a[:, :, NT:2 * NT], a[:, :, NT - d:2 * NT - d], ALU.add))
                a, b = b, a
                d *= 2
            done(nc.vector.tensor_tensor(pre[:], pre[:], a[:, :, NT:2 * NT].rearrange("p e t -> p t e"), ALU.add))
            done(nc.vector.tensor_tensor(pre[:], pre[:], hot[:], ALU.mult))
            done(nc.vector.tensor_reduce(loc[:], pre[:], AX_X, ALU.add))
            done(nc.vector.tensor_scalar(keep[:], loc[:], float(CAP), None, ALU.is_lt))
            done(nc.vector.tensor_tensor(pre[:], hot[:], cst[:, C_CAPE:C_CAPE + E].unsqueeze(1).to_broadcast(n), ALU.mult))
            done(nc.vector.tensor_reduce(idx[:], pre[:], AX_X, ALU.add))
            done(nc.vector.tensor_tensor(slot[:], idx[:], loc[:], ALU.add))
            done(nc.vector.tensor_scalar(tmp[:], keep[:], -1.0, -float(2 * TOK), ALU.add, ALU.mult))
            done(nc.vector.tensor_tensor(gate[:], gate[:], keep[:], ALU.mult))
            done(nc.vector.tensor_tensor(loc[:], slot[:], tmp[:], ALU.add))
            done(nc.vector.tensor_copy(slot_u[:], loc[:]))
            done(nc.vector.tensor_scalar(loc[:], slot[:], float(TOK - 1), None, ALU.min))
            nc.vector.tensor_copy(back_u[:], loc[:]).then_inc(s_slot, 1)

        @block.gpsimd
        def _(pool):
            pool.wait_ge(s_slot, 1)
            for t in range(NT):
                nc.gpsimd.indirect_dma_start(dr["disp"], bass.IndirectOffsetOnAxis(ap=slot_u[:, t:t + 1], axis=0),
                                             y1_all[:, t, :], None, bounds_check=TOK - 1, oob_is_err=False).then_inc(s_sc, 16)
            pool.wait_ge(s_sc, 16 * NT)


def phase_experts(nc, ins, dr, sem, sb, ps):
    CK = FF // P
    w1 = sb("w1e", [P, 2, CK, D])
    w2 = sb("w2e", [P, 2, CK, D])
    b1 = sb("b1e", [P, 2, CK])
    b2 = sb("b2e", [1, 2, D])
    ones = sb("ones", [1, P])
    ident = sb("ident4", [P, P])
    x = sb("xe", [P, 2, CH, D])
    xT = sb("xeT", [P, 2, CAP])
    w = sb("we", [P, 2, D])
    bb = sb("be", [1, D])
    y = sb("ye", [P, CH, D])
    pw, pb, tp, py = ps("pw", [P, 2, 512]), ps("pb", [1, 512]), ps("tpe", [P, 2, CAP]), ps("pye", [P, 2, 512])
    S = {n: sem("d_" + n) for n in "load0 load1 const ones wmm bmm wout bout tp xT ymm yout stored".split()}

    with nc.Block() as block:
        @block.sync
        def _(sp):
            sp.dma_start(ident[:], ins["consts"][:, C_ID:C_ID + P]).then_inc(S["const"], 16)
            for e in range(E):
                u = e % 2
                if e >= 2:
                    sp.wait_ge(S["wout"], e - 1)
                    sp.wait_ge(S["bout"], e - 1)
                    sp.wait_ge(S["tp"], e - 1)
                sp.dma_start(w1[:, u], ins["w1T"][e].rearrange("(c p) n -> p c n", p=P)).then_inc(S[f"load{u}"], 16)
                sp.dma_start(w2[:, u], ins["w2"][e].rearrange("(c p) n -> p c n", p=P)).then_inc(S[f"load{u}"], 16)
                sp.dma_start(b1[:, u, :], ins["b1e"][e]).then_inc(S[f"load{u}"], 16)
                sp.dma_start(b2[:, u, :], ins["b2e"][e:e + 1, :]).then_inc(S[f"load{u}"], 16)
                sp.dma_start(x[:, u], dr["disp"][e * CAP:(e + 1) * CAP, :].rearrange("(a p) n -> p a n", p=P)).then_inc(S[f"load{u}"], 16)

        @block.tensor
        def _(pe):
            pe.wait_ge(S["const"], 16)
            pe.wait_ge(S["ones"], 1)
            for e in range(E):
                u = e % 2
                pe.wait_ge(S[f"load{u}"], 80 * (e // 2 + 1))
                if e:
                    pe.wait_ge(S["xT"], 2 * e)
                    pe.wait_ge(S["wout"], e)
                    pe.wait_ge(S["bout"], e)
                for k in range(2):
                    for a in range(CH):
                        last = nc.tensor.transpose(tp[:, k, a * P:(a + 1) * P], x[:, u, a, k * P:(k + 1) * P], ident[:])
                last.then_inc(S["tp"], 1)
                for c in range(CK):
                    last = nc.tensor.matmul(pb[0:1, 0:D], b1[:, u, c:c + 1], w2[:, u, c, :], start=(c == 0), stop=(c == CK - 1))
                last.then_inc(S["bmm"], 1)
                for k in range(2):
                    for c in range(CK):
                        last = nc.tensor.matmul(pw[:, k, 0:D], w1[:, u, c, k * P:(k + 1) * P], w2[:, u, c, :],
                                                start=(c == 0), stop=(c == CK - 1))
                last.then_inc(S["wmm"], 1)
                pe.wait_ge(S["xT"], 2 * e + 2)
                pe.wait_ge(S["wout"], e + 1)
                pe.wait_ge(S["bout"], e + 1)
                for a in range(CH):
                    n = e * CH + a
                    if n >= 2:
                        pe.wait_ge(S["yout"], n - 1)
                    for k in range(2):
                        nc.tensor.matmul(py[:, a % 2, 0:D], xT[:, k, a * P:(a + 1) * P], w[:, k, :], start=(k == 0), stop=False)
                    nc.tensor.matmul(py[:, a % 2, 0:D], ones[:], bb[:], start=False, stop=True).then_inc(S["ymm"], 1)

        @block.vector
        def _(dve):
            nc.vector.memset(ones[:], 1.0).then_inc(S["ones"], 1)
            for e in range(E):
                dve.wait_ge(S["bmm"], e + 1)
                if e:
                    dve.wait_ge(S["ymm"], e * CH)
                nc.vector.tensor_tensor(bb[:], pb[0:1, 0:D], b2[:, e % 2, :], ALU.add).then_inc(S["bout"], 1)
                dve.wait_ge(S["wmm"], e + 1)
                nc.vector.tensor_copy(w[:], pw[:, :, 0:D]).then_inc(S["wout"], 1)

        @block.scalar
        def _(act):
            for e in range(E):
                act.wait_ge(S["tp"], e + 1)
                if e:
                    act.wait_ge(S["ymm"], e * CH)
                for k in range(2):
                    nc.scalar.activation(xT[:, k, :], tp[:, k, :], ACT.Copy).then_inc(S["xT"], 1)
                if e:
                    act.wait_ge(S["stored"], 16 * e)
                for a in range(CH):
                    act.wait_ge(S["ymm"], e * CH + a + 1)
                    nc.scalar.activation(y[:, a, :], py[:, a % 2, 0:D], ACT.Copy).then_inc(S["yout"], 1)
                act.wait_ge(S["yout"], e * CH + CH)
                act.dma_start(dr["yexp"][e * CAP:(e + 1) * CAP, :].rearrange("(a p) n -> p a n", p=P), y[:]).then_inc(S["stored"], 16)
            act.wait_ge(S["stored"], 16 * E)


def phase_gate(nc, ins, dr, sem, sb, ps):
    y1_all, gate, back_u = dr["y1_all"], dr["gate"], dr["back_u"]
    yg = sb("yg", [P, NT, D])
    g2, b2 = sb("g2", [P, D]), sb("b2ln", [P, D])
    stat, mv = sb("stat5", [P, 4, 6]), sb("mv5", [P, 4, 2])
    std, rstd = sb("std5", [P, 4]), sb("rstd5", [P, 4])
    z, ez = sb("z5", [P, 4, D]), sb("ez", [P, 4, D])
    S = {n: sem("e_" + n) for n in "weights gathered z stats aggr eps std rstd n0 n1 n2 exp one rec out stored".split()}

    with nc.Block() as block:
        @block.sync
        def _(sp):
            sp.dma_start(g2[:], ins["g2"].partition_broadcast(P)).then_inc(S["weights"], 16)
            sp.dma_start(b2[:], ins["b2ln"].partition_broadcast(P)).then_inc(S["weights"], 16)
            for h in range(NT // 4):
                sp.wait_ge(S["out"], h + 1)
                sp.dma_start(dr["g"].rearrange("(t p) n -> p t n", p=P)[:, 4 * h:4 * h + 4, :], ez[:]).then_inc(S["stored"], 16)
            sp.wait_ge(S["stored"], 16 * (NT // 4))

        @block.gpsimd
        def _(pool):
            for t in range(NT):
                nc.gpsimd.indirect_dma_start(yg[:, t, :], None, dr["yexp"],
                                             bass.IndirectOffsetOnAxis(ap=back_u[:, t:t + 1], axis=0)).then_inc(S["gathered"], 16)

        @block.vector
        def _(dve):
            dve.wait_ge(S["weights"], 32)
            dve.wait_ge(S["gathered"], 16 * NT)
            for h in range(NT // 4):
                if h:
                    dve.wait_ge(S["out"], h)
                for a in range(4):
                    t = 4 * h + a
                    nc.vector.scalar_tensor_tensor(z[:, a, :], yg[:, t, :], gate[:, t:t + 1], y1_all[:, t, :],
                                                   ALU.mult, ALU.add).then_inc(S["z"], 1)
                for a in range(4):
                    dve.wait_ge(S["z"], 4 * h + a + 1)
                    nc.vector.bn_stats(stat[:, a, :], z[:, a, :]).then_inc(S["stats"], 1)
                for a in range(4):
                    dve.wait_ge(S["stats"], 4 * h + a + 1)
                    nc.vector.bn_aggr(mv[:, a, :], stat[:, a, :]).then_inc(S["aggr"], 1)
                dve.wait_ge(S["aggr"], 4 * h + 4)
                nc.vector.tensor_scalar(std[:], mv[:, :, 1], EPS, None, ALU.add).then_inc(S["eps"], 1)
                dve.wait_ge(S["std"], h + 1)
                nc.vector.reciprocal(rstd[:], std[:]).then_inc(S["rstd"], 1)
                dve.wait_ge(S["rstd"], h + 1)
                for a in range(4):
                    nc.vector.tensor_scalar(z[:, a, :], z[:, a, :], mv[:, a, 0:1], rstd[:, a:a + 1],
                                            ALU.subtract, ALU.mult).then_inc(S["n0"], 1)
                dve.wait_ge(S["n0"], 4 * h + 4)
                nc.vector.tensor_tensor(z[:], z[:], g2[:].unsqueeze(1).to_broadcast([P, 4, D]), ALU.mult).then_inc(S["n1"], 1)
                dve.wait_ge(S["n1"], h + 1)
                nc.vector.tensor_tensor(z[:], z[:], b2[:].unsqueeze(1).to_broadcast([P, 4, D]), ALU.add).then_inc(S["n2"], 1)
                dve.wait_ge(S["exp"], h + 1)
                nc.vector.tensor_scalar(ez[:], ez[:], 1.0, None, ALU.add).then_inc(S["one"], 1)
                dve.wait_ge(S["one"], h + 1)
                nc.vector.reciprocal(ez[:], ez[:]).then_inc(S["rec"], 1)
                dve.wait_ge(S["rec"], h + 1)
                nc.vector.tensor_tensor(ez[:], z[:], ez[:], ALU.mult).then_inc(S["out"], 1)

        @block.scalar
        def _(act):
            for h in range(NT // 4):
                act.wait_ge(S["eps"], h + 1)
                nc.scalar.activation(std[:], std[:], ACT.Sqrt).then_inc(S["std"], 1)
                act.wait_ge(S["n2"], h + 1)
                if h:
                    act.wait_ge(S["stored"], 16 * h)
                nc.scalar.activation(ez[:], z[:], ACT.Exp, scale=-1.0).then_inc(S["exp"], 1)


def tile_at(i, k):
    if k >= 0:
        over = (i + k) // NI
        return (i + k) % NI, (2 * over if k < 3 else over + 1)
    inside = (i + k + NI) // NI
    return (i + k + NI) % NI, 1 - inside


def phase_attend(nc, ins, dr, sem, sb, ps):
    kst = sb("kst", [ROWS, NI, W], BF16)
    slots = sb("slots", [P, NI, 2, HH, 64])
    qst = sb("qst", [ROWS, 3, W], BF16)
    qbd = sb("qbd", [P, 2, HH, P], FP16)
    tks = sb("tks", [P, 2, TSW], FP16)
    tvs = sb("tvs", [P, 2, TVU * DK], FP16)
    pp2 = sb("prob_parts", [P, 2, 2, 2, HH, 64], FP16)
    vrow = sb("vrow", [P, 4, HH * DK])
    vt = sb("vt", [P, 2, HH, 32])
    rc = sb("rc", [P, 3, DK])
    mx = sb("mxr", [P, 2, HH, 64])
    mb = sb("mb", [P, 2, HH, 64])
    mcol = sb("mcol", [P, 8])
    pvs = sb("pvs", [P, 2, P])
    otn = sb("otn", [P, P])
    cst = sb("cst6", [P, C_TRI])
    spp = ps("spp", [P, 2, 2, HH, 64])
    ro = ps("ro", [P, 2, 8, HH, 8])
    pvp = ps("pvps", [P, 2, P])
    otp = ps("otp", [P, 2, P])
    rom = mx[:].rearrange("p a h l -> p (a h l)").rearrange("p (b h l) -> p b h l", b=16, h=HH)
    mask = cst[:, C_MASK:C_MASK + 8]
    flat = slots[:].rearrange("p n a h l -> p (n a h l)")
    half_table = TVU * DK // 2
    tk_whole = flat[:, 0:TSW]
    tv_whole = [flat[:, 2048:2048 + half_table]] * 2

    S = {n: sem("f_" + n) for n in (
        "tables preset kst q qbd_load qbd vrow0 vrow1 vrow2 vrow3 vt prob_hi prob_lo scored stored mxd turned mcol mbp mb sub prob used "
        "split tables2 rom pvs folded rden normed otout").split()}

    def scores(pe, gg, i, n, k, first):
        if n == 0:
            pe.wait_ge(S["q"], START + (gg + 1) * 16 * 4)
            pe.wait_ge(S["qbd"], START + gg + 1)
        if n < 2:
            pe.wait_ge(S["mb"], START + gg)
        else:
            pe.wait_ge(S["stored"], START + gg * NI + n - 1)
        j, cls = tile_at(i, k)
        out = spp[:, n % 2]

        def product(h):
            for half in range(2):
                last = nc.tensor.matmul(out[:, half, h, :], kst[:, ds(j, 1), h * P:(h + 1) * P].rearrange("p a r -> p (a r)"),
                                        qst[:, ds(cls, 1), h * P + half * 64:h * P + half * 64 + 64].rearrange("p a l -> p (a l)"),
                                        start=(h == 0), stop=(h == HH - 1), skip_group_check=True)
            return last

        def relative():
            for q in range(16):
                x0 = k * P - 8 * q - LOWEST - 7
                for a, b in PAIRS:
                    nc.tensor.matmul(out[:, q // 8, :, (q % 8) * 8:(q % 8) * 8 + 8], tks[:, a, x0:x0 + P],
                                     qbd[:, b, :, 8 * q:8 * q + 8], start=False, stop=False, skip_group_check=True)

        for h in range(HH - 1):
            product(h)
        if k == 0:
            relative()
        elif -7 < k < 0:
            with pe.If(i > -k - 1):
                relative()
        elif k < 3:
            with pe.If(i < NI - k):
                relative()
        product(HH - 1).then_inc(S["scored"], 1)

    def values(pe, gg, i, n, k):
        pe.wait_ge(S["prob"], START + gg * NI + n + 1)
        pe.wait_ge(S["vt"], START + gg * NI + n + 1)
        if n < NB:
            pe.wait_ge(S["prob_lo"], START + gg * NB + n + 1)
        if n == 0:
            pe.wait_ge(S["rom"], START + gg)
            pe.wait_ge(S["pvs"], START + gg)

        def relative():
            for q in range(16):
                u0 = k * P - 8 * q - 7 - LOWEST
                for t, (a, b) in enumerate(PAIRS):
                    nc.tensor.matmul(ro[:, q // 8, q % 8, :, :], tvs[:, a, u0 * DK:(u0 + 8) * DK],
                                     pp2[:, n % 2, b, q // 8, :, (q % 8) * 8:(q % 8) * 8 + 8],
                                     start=(n == 0 and q % 8 == 0 and t == 0), stop=False, skip_group_check=True)

        if k == 0:
            relative()
        elif -7 < k < 0:
            with pe.If(i > -k - 1):
                relative()
        elif k < 3:
            with pe.If(i < NI - k):
                relative()
        for h in range(HH):
            c, q = h % 4, h // 4
            last = nc.tensor.matmul(pvp[32 * c:32 * c + 32, q, :].rearrange("p (a l) -> p a l", a=2), vt[:, n % 2, h, :],
                                    slots[:, n, :, h, :], start=(n == 0 and q == 0), stop=(n == NI - 1),
                                    skip_group_check=True)
        last.then_inc(S["used"], 1)

    def turn_max(pe, gg):
        pe.wait_ge(S["mxd"], START + (gg + 1) * NI)
        pe.wait_ge(S["stored"], START + (gg + 1) * NI)
        flat = mx[:].rearrange("p a h l -> p (a h l)")
        tp = spp[:, 0].rearrange("p a h l -> p (a h l)")
        for c in range(8):
            last = nc.tensor.transpose(tp[:, c * P:(c + 1) * P], flat[:, c * P:(c + 1) * P], cst[:, C_ID:C_ID + P])
        last.then_inc(S["turned"], 1)
        pe.wait_ge(S["mcol"], START + gg + 1)
        bc = spp[:, 1].rearrange("p a h l -> p (a h l)")
        for c in range(8):
            last = nc.tensor.matmul(bc[:, c * P:(c + 1) * P], mcol[:, c:c + 1].to_broadcast([P, P]), cst[:, C_ID:C_ID + P],
                                    start=True, stop=True)
        last.then_inc(S["mbp"], 1)

    def fold(pe, gg):
        pe.wait_ge(S["rom"], START + gg + 1)
        pe.wait_ge(S["pvs"], START + gg + 1)
        pe.wait_ge(S["normed"], START + gg)
        for h in range(HH):
            nc.tensor.matmul(otp[:, 0, :].rearrange("p (b l) -> p b l", b=16), cst[:, C_FOLD + 112 - 16 * h:C_FOLD + 240 - 16 * h],
                             rom[:, :, h, :], start=(h == 0), stop=False)
        for q in range(2):
            nc.tensor.matmul(otp[:, 0, :], cst[:, C_PICK + 64 - 64 * q:C_PICK + 192 - 64 * q], pvs[:, q, :],
                             start=False, stop=(q == 1))
        for q in range(2):
            last = nc.tensor.matmul(otp[:, 1, :], cst[:, C_DEN + 64 - 64 * q:C_DEN + 192 - 64 * q], pvs[:, q, :],
                                    start=(q == 0), stop=(q == 1))
        last.then_inc(S["folded"], 1)

    start_counts(nc, S)
    with nc.Block() as block:
        @block.sync
        def _(sp):
            sp.dma_start(cst[:], ins["consts"][:, 0:C_TRI]).then_inc(S["tables"], 16)
            tk, tv = dr["tk"], dr["tv"]
            for l in range(8):
                sp.dma_start(tk_whole[16 * l:16 * l + 16, :], tk[:, 7 - l:7 - l + TSW]).then_inc(S["tables"], 16)
            sp.dma_start(tv_whole[0], bass.AP(tv.tensor, 0, [[DK, P], [1, TVU * DK // 2]])).then_inc(S["tables"], 16)
            for n, row in ((1, REL - 1), (2, 0)):
                src = bass.AP(ins["rv"].tensor, row * DK, [[0, P], [1, DK]])
                sp.dma_start(rc[:, n, :], src).then_inc(S["tables"], 16)
            sp.wait_ge(S["split"], START + 4)
            sp.dma_start(tv_whole[1], bass.AP(tv.tensor, TVU * DK // 2, [[DK, P], [1, TVU * DK // 2]])).then_inc(S["tables2"], 16)

            def load_q(gg):
                row = dr["qs"][ds(gg, 1), :]
                at = 0
                for parts in (3, 2, 1):
                    rows = parts * DK
                    src = row[:, 0:rows * W].rearrange("a (p n) -> p a n", n=W)
                    sp.dma_start(qst[at:at + rows, :, :], src.to_broadcast([rows, 3, W])).then_inc(S["q"], 16)
                    at += rows
                sp.dma_start(qst[QROWS:ROWS, 1:3, :], dr["cs"][ds(gg, 1)].rearrange("a c q h l -> q (a c) (h l)")).then_inc(S["q"], 16)
                for q in range(2):
                    src = bass.AP(dr["qp"].tensor, (gg * 2 + q) * (DK * W), [[0, 8], [W, DK], [1, W]])
                    sp.dma_start(qbd[:, q], src).then_inc(S["qbd_load"], 16)

            def load_values(gg, i, c):
                for n, k in enumerate(KS):
                    j, _ = tile_at(i, k)
                    if n < 4:
                        sp.wait_ge(S["vt"], START + gg * NI)
                    else:
                        sp.wait_ge(S["vt"], START + gg * NI + n - 3)
                    src = bass.AP(dr["v"].tensor, (c // 2) * (L * D) + (c % 2) * P + j * (P * D), [[D, P], [1, P]])
                    sp.dma_start(vrow[:, n % 4, :], src).then_inc(S[f"vrow{n % 4}"], 16)

            def store(gg):
                sp.wait_ge(S["normed"], START + gg + 1)
                sp.dma_start(dr["ot"][ds(gg, 1)].rearrange("g p l -> p (g l)"), otn[:]).then_inc(S["otout"], 16)

            with sp.Fori(0, NC) as c:
                sp.wait_ge(S["scored"], START + c * (NI * NI))
                sp.wait_ge(S["preset"], START + 4)
                at = 0
                for u, parts in enumerate((1, 1, 1, 2, 2, 3)):
                    src = dr["ks"][ds(c * NI, NI), (parts - 1) * DK * W:parts * DK * W].rearrange("j (p n) -> p j n", n=W)
                    sp.dma_start(kst[at:at + DK, :, :], src).then_inc(S["kst"], 16)
                    at += DK
                load_q(c * NI)
                sp.wait_ge(S["scored"], START + c * (NI * NI) + NI)
                load_q(c * NI + 1)
                load_values(c * NI, c * 0, c)
                with sp.Fori(1, NI - 1) as i:
                    gg = c * NI + i
                    sp.wait_ge(S["scored"], START + gg * NI + NI)
                    load_q(gg + 1)
                    store(gg - 1)
                    load_values(gg, i, c)
                store(c * NI + NI - 2)
                load_values(c * NI + NI - 1, c * 0 + NI - 1, c)
                store(c * NI + NI - 1)
            sp.wait_ge(S["otout"], START + 16 * NC * NI)

        @block.gpsimd
        def _(pool):
            pool.wait_ge(S["preset"], START + 5)
            pool.wait_ge(S["tables"], START + 16 * 12)

            def diagonal(gg):
                pool.wait_ge(S["qbd_load"], START + (gg + 1) * 32)
                q = qbd[:].rearrange("p q h (b l) -> p (q h b) l", l=8)
                nc.gpsimd.tensor_tensor(q, q, mask.unsqueeze(1).to_broadcast([P, 2 * HH * 16, 8]), ALU.mult).then_inc(S["qbd"], 1)

            def value_tiles(gg, i):
                for n, k in enumerate(KS):
                    j, cls = tile_at(i, k)
                    pool.wait_ge(S["used"], START + gg * NI + (n - 1 if n else 0))
                    pool.wait_ge(S[f"vrow{n % 4}"], START + (gg * 4 + n // 4 + 1) * 16)
                    nc.gpsimd.tensor_tensor(vt[:, n % 2, :, 0:DK], vrow[:, n % 4, :].rearrange("p (h d) -> p h d", d=DK),
                                            rc[:, ds(cls, 1), :].to_broadcast([P, HH, DK]), ALU.add).then_inc(S["vt"], 1)

            with pool.Fori(0, NC) as c:
                diagonal(c * NI)
                with pool.Fori(0, NI - 1) as i:
                    diagonal(c * NI + i + 1)
                    value_tiles(c * NI + i, i)
                value_tiles(c * NI + NI - 1, NI - 1)

        @block.tensor
        def _(pe):
            pe.wait_ge(S["tables"], START + 16 * 12)
            pe.wait_ge(S["preset"], START + 5)
            pe.wait_ge(S["split"], START + 6)
            with pe.Fori(0, NC) as c:
                pe.wait_ge(S["kst"], START + c * 96 + 96)
                for n, k in enumerate(KS):
                    scores(pe, c * NI, c * 0, n, k, True)
                turn_max(pe, c * NI)
                with pe.Fori(0, NI - 1) as i:
                    gg = c * NI + i
                    for n, k in enumerate(KS):
                        values(pe, gg, i, n, k)
                        scores(pe, gg + 1, i + 1, n, k, False)
                    turn_max(pe, gg + 1)
                    fold(pe, gg)
                for n, k in enumerate(KS):
                    values(pe, c * NI + NI - 1, i * 0 + NI - 1, n, k)
                fold(pe, c * NI + NI - 1)

        @block.scalar
        def _(act):
            def store_scores(gg, n, used):
                act.wait_ge(S["scored"], START + gg * NI + n + 1)
                act.wait_ge(S["used"], START + used)
                nc.scalar.activation(slots[:, n], spp[:, n % 2], ACT.Copy).then_inc(S["stored"], 1)

            def exps(gg, n):
                act.wait_ge(S["sub"], START + gg * NI + n + 1)
                if n < NB:
                    act.wait_ge(S["used"], START + gg * NI + max(n - 1, 0))
                    nc.scalar.activation(pp2[:, n % 2, 0], slots[:, n], ACT.Exp).then_inc(S["prob_hi"], 1)
                nc.scalar.activation(slots[:, n], slots[:, n], ACT.Exp).then_inc(S["prob"], 1)

            def max_out(gg):
                act.wait_ge(S["mbp"], START + gg + 1)
                act.wait_ge(S["sub"], START + gg * NI)
                nc.scalar.activation(mb[:], spp[:, 1], ACT.Copy).then_inc(S["mb"], 1)

            def values_out(gg):
                act.wait_ge(S["used"], START + (gg + 1) * NI)
                act.wait_ge(S["folded"], START + gg)
                nc.scalar.activation(pvs[:], pvp[:], ACT.Copy).then_inc(S["pvs"], 1)

            act.wait_ge(S["split"], START + 6)
            with act.Fori(0, NC) as c:
                for n in range(NI):
                    store_scores(c * NI, n, c * NI * NI)
                max_out(c * NI)
                with act.Fori(0, NI - 1) as i:
                    gg = c * NI + i
                    exps(gg, 0)
                    exps(gg, 1)
                    for n in range(NI):
                        store_scores(gg + 1, n, gg * NI + n + 1)
                        if n + 2 < NI:
                            exps(gg, n + 2)
                    max_out(gg + 1)
                    values_out(gg)
                for n in range(NI):
                    exps(c * NI + NI - 1, n)
                values_out(c * NI + NI - 1)

        @block.vector
        def _(dve):
            def running_max(gg, n, folded=None):
                dve.wait_ge(S["stored"], START + gg * NI + n + 1)
                if n == 0:
                    dve.wait_ge(S["folded"], START + folded)
                    nc.vector.tensor_copy(mx[:], slots[:, 0]).then_inc(S["mxd"], 1)
                else:
                    dve.wait_ge(S["mxd"], START + gg * NI + n)
                    nc.vector.tensor_tensor(mx[:], mx[:], slots[:, n], ALU.max).then_inc(S["mxd"], 1)

            def subtract(gg, n):
                if n == 0:
                    dve.wait_ge(S["mb"], START + gg + 1)
                nc.vector.tensor_tensor(slots[:, n], slots[:, n], mb[:], ALU.subtract).then_inc(S["sub"], 1)

            def low_part(gg, n):
                dve.wait_ge(S["prob"], START + gg * NI + n + 1)
                dve.wait_ge(S["used"], START + gg * NI + max(n - 1, 0))
                nc.vector.tensor_tensor(pp2[:, n % 2, 1], slots[:, n], pp2[:, n % 2, 0], ALU.subtract).then_inc(S["prob_lo"], 1)

            def query_max(gg):
                dve.wait_ge(S["turned"], START + gg + 1)
                nc.vector.tensor_reduce(mcol[:], spp[:, 0].rearrange("p a h l -> p (a h l)").rearrange("p (c r) -> p c r", c=8),
                                        AX_X, ALU.max).then_inc(S["mcol"], 1)

            def masked(gg):
                dve.wait_ge(S["used"], START + (gg + 1) * NI)
                nc.vector.tensor_tensor(rom.rearrange("p b h l -> p (b h) l"), ro[:].rearrange("p a b h l -> p (a b h) l"),
                                        mask_l.to_broadcast([P, P, 8]), ALU.mult).then_inc(S["rom"], 1)

            def normalise(gg):
                dve.wait_ge(S["folded"], START + gg + 1)
                dve.wait_ge(S["otout"], START + gg * 16)
                nc.vector.reciprocal(otn[:], otp[:, 1, :]).then_inc(S["rden"], 1)
                dve.wait_ge(S["rden"], START + gg + 1)
                nc.vector.tensor_tensor(otn[:], otp[:, 0, :], otn[:], ALU.mult).then_inc(S["normed"], 1)

            nc.vector.memset(kst[QROWS:ROWS, :, :], 1.0).then_inc(S["preset"], 1)
            nc.vector.memset(qst[QROWS:ROWS, 0, :], 0.0).then_inc(S["preset"], 1)
            nc.vector.memset(rc[:, 0, :], 0.0).then_inc(S["preset"], 1)
            nc.vector.memset(vt[:], 0.0).then_inc(S["preset"], 1)
            dve.wait_ge(S["preset"], START + 4)
            nc.vector.memset(vt[:, :, :, DK:DK + 1], 1.0).then_inc(S["preset"], 1)
            dve.wait_ge(S["tables"], START + 16 * 12)
            step = [START]

            def split(dst, src):
                for q, op in enumerate((None, ALU.subtract)):
                    if op is None:
                        ins_ = nc.vector.tensor_copy(dst[:, 0], src)
                    else:
                        ins_ = nc.vector.tensor_tensor(dst[:, 1], src, dst[:, 0], op)
                    ins_.then_inc(S["split"], 1)
                    step[0] += 1
                    dve.wait_ge(S["split"], step[0])

            split(tks[:], tk_whole)
            split(tvs[:, :, 0:half_table], tv_whole[0])
            dve.wait_ge(S["tables2"], START + 16)
            split(tvs[:, :, half_table:], tv_whole[1])
            mask_l = cst[:, C_MASKV:C_MASKV + 8].unsqueeze(1)
            dve.wait_ge(S["tables"], START + 16 * 12)
            with dve.Fori(0, NC) as c:
                for n in range(NI):
                    running_max(c * NI, n, c * NI)
                query_max(c * NI)
                with dve.Fori(0, NI - 1) as i:
                    gg = c * NI + i
                    subtract(gg, 0)
                    subtract(gg, 1)
                    low_part(gg, 0)
                    for n in range(NI):
                        if n + 2 < NI:
                            subtract(gg, n + 2)
                        if n + 1 < NB:
                            low_part(gg, n + 1)
                        running_max(gg + 1, n, gg)
                    query_max(gg + 1)
                    masked(gg)
                    normalise(gg)
                for n in range(NI):
                    subtract(c * NI + NI - 1, n)
                    if n < NB:
                        low_part(c * NI + NI - 1, n)
                masked(c * NI + NI - 1)
                normalise(c * NI + NI - 1)


def phase_out(nc, ins, dr, sem, sb, ps):
    wo, bo = sb("woA", [P, 2, D]), sb("boA", [P, D])
    ot = sb("ot", [P, 2, 2, CH, P])
    x, g, y = sb("x6", [P, 2, CH, D]), sb("g6", [P, 2, CH, D]), sb("y6", [P, 2, CH, D])
    pp = ps("p6", [P, CH, 512])
    S = {n: sem("g_" + n) for n in "weights load0 load1 proj biased gated out store0 store1".split()}
    xv, gv, ov = (t.rearrange("(c a p) n -> p c a n", a=CH, p=P) for t in (ins["x"], dr["g"], ins["out"]))

    with nc.Block() as block:
        @block.sync
        def _(sp):
            sp.dma_start(wo[:], ins["woAT"].rearrange("(k p) n -> p k n", p=P)).then_inc(S["weights"], 16)
            sp.dma_start(bo[:], ins["boA"].partition_broadcast(P)).then_inc(S["weights"], 16)
            for ch in range(NCH):
                u = ch % 2
                if ch >= 2:
                    sp.wait_ge(S["out"], ch - 1)
                b, i0 = ch // 4, (ch % 4) * CH
                for half in range(2):
                    r = (2 * b + half) * NI + i0
                    sp.dma_start(ot[:, u, half], dr["ot"][r:r + CH].rearrange("g p l -> p g l")).then_inc(S[f"load{u}"], 16)
                sp.dma_start(x[:, u], xv[:, ch]).then_inc(S[f"load{u}"], 16)
                sp.dma_start(g[:, u], gv[:, ch]).then_inc(S[f"load{u}"], 16)

        @block.tensor
        def _(pe):
            pe.wait_ge(S["weights"], 32)
            for ch in range(NCH):
                u = ch % 2
                pe.wait_ge(S[f"load{u}"], 64 * (ch // 2 + 1))
                if ch:
                    pe.wait_ge(S["biased"], ch)
                for a in range(CH):
                    for half in range(2):
                        last = nc.tensor.matmul(pp[:, a, 0:D], ot[:, u, half, a, :], wo[:, half, :], start=(half == 0), stop=(half == 1))
                last.then_inc(S["proj"], 1)

        @block.vector
        def _(dve):
            dve.wait_ge(S["weights"], 32)
            for ch in range(NCH):
                u = ch % 2
                dve.wait_ge(S["proj"], ch + 1)
                if ch >= 2:
                    dve.wait_ge(S[f"store{u}"], 16 * (ch // 2))
                nc.vector.tensor_tensor(y[:, u], pp[:, :, 0:D], bo[:].unsqueeze(1).to_broadcast([P, CH, D]), ALU.add).then_inc(S["biased"], 1)
                dve.wait_ge(S["biased"], ch + 1)
                nc.vector.tensor_tensor(y[:, u], y[:, u], g[:, u], ALU.mult).then_inc(S["gated"], 1)
                dve.wait_ge(S["gated"], ch + 1)
                nc.vector.tensor_tensor(y[:, u], y[:, u], x[:, u], ALU.add).then_inc(S["out"], 1)

        @block.scalar
        def _(act):
            for ch in range(NCH):
                act.wait_ge(S["out"], ch + 1)
                act.dma_start(ov[:, ch], y[:, ch % 2]).then_inc(S[f"store{ch % 2}"], 16)
            for u in range(2):
                act.wait_ge(S[f"store{u}"], 16 * (NCH // 2))


def build(nc, ins):
    def dram(name, shape, dt=F32):
        return nc.dram_tensor(name, shape, dt, kind="Internal").ap()

    def scoped(ctx):
        def sb(name, shape, dt=F32):
            return ctx.enter_context(nc.sbuf_tensor(name, shape, dt))

        def ps(name, shape, dt=F32):
            return ctx.enter_context(nc.psum_tensor(name, shape, dt))

        return sb, ps

    dr = {
        "qs": dram("q_parts", [NC * NI, PARTS * DK * W], BF16),
        "ks": dram("k_parts", [NC * NI, PARTS * DK * W], BF16),
        "qp": dram("q_pair", [NC * NI, 2, DK * W], FP16),
        "cs": dram("class_constants", [NC * NI, 2, PARTS, HH, P], BF16),
        "v": dram("v_rows", [TOK, D]),
        "tk": dram("key_table", [DK, SPAN]),
        "tv": dram("value_table", [SPAN, DK]),
        "disp": dram("dispatched", [TOK, D]),
        "yexp": dram("expert_rows", [TOK, D]),
        "g": dram("gate_rows", [TOK, D]),
        "ot": dram("attention_out", [NC * NI, P, P]),
    }
    with ExitStack() as whole:
        def sem(name):
            return whole.enter_context(nc.semaphore(name))

        with ExitStack() as gate_scope:
            sb, _ = scoped(gate_scope)
            dr["xn_all"] = dr["y1_all"] = sb("xn_all", [P, NT, D])
            dr["logits"] = sb("logits", [P, NT, E])
            dr["gate"] = sb("gate", [P, NT])
            dr["slot_u"], dr["back_u"] = sb("slot_u", [P, NT], U32), sb("back_u", [P, NT], U32)
            with ExitStack() as first:
                sb, _ = scoped(first)
                dr["qkv_all"] = sb("qkv_all", [P, NT, 3 * D])
                with ExitStack() as c:
                    phase_project(nc, ins, dr, sem, *scoped(c))
                with ExitStack() as c:
                    phase_pairs(nc, ins, dr, sem, *scoped(c))
            for phase in (phase_route, phase_experts, phase_gate):
                with ExitStack() as c:
                    phase(nc, ins, dr, sem, *scoped(c))
        for phase in (phase_attend, phase_out):
            with ExitStack() as c:
                phase(nc, ins, dr, sem, *scoped(c))


def kernel(**inputs):
    import numpy as np
    import concourse.bacc as bacc
    from concourse.bass_utils import run_bass_kernel_spmd

    a = {k: np.asarray(v) for k, v in inputs.items()}

    def half_heads(w):
        return w.reshape(-1, 2, HH, DK).transpose(0, 1, 3, 2).reshape(-1, D)

    def columns(b):
        return half_heads(b[None, :]).reshape(2, P).T

    consts = np.zeros((P, C_N), np.float32)
    p = np.arange(P)
    consts[p, C_ID + p] = 1
    consts[p, C_FOLD + 112 + p % 16] = 1
    for c in range(4):
        for d in range(DK):
            consts[32 * c + d, C_PICK + 64 + 16 * c + d] = 1
            consts[32 * c + DK, C_DEN + 64 + 16 * c + d] = 1
    consts[p, C_MASK + p // 16] = 1
    consts[p, C_MASKV + 7 - p // 16] = 1
    consts[:, C_TRI:C_TRI + P] = p[:, None] < p[None, :]
    consts[:, C_ONE:C_ONE + P] = 1
    consts[p, C_HEAD + p % HH] = 1
    consts[:, C_IOTA:C_IOTA + E] = E - np.arange(E)
    consts[:, C_CAPE:C_CAPE + E] = CAP * np.arange(E)

    host = {
        "x": a["L0_attn_x"].reshape(TOK, D),
        "wqT": half_heads(a["L0_attn_Wq"].T), "wkT": half_heads(a["L0_attn_Wk"].T), "wvT": a["L0_attn_Wv"].T,
        "wiT": a["L0_ffn_in_proj_w"].T, "woT": a["L0_ffn_out_proj_w"].T, "woAT": a["L0_attn_Wo"].T,
        "bqk": np.concatenate([columns(a["L0_attn_bq"]), columns(a["L0_attn_bk"])], 1),
        "bv": a["L0_attn_bv"], "bi": a["L0_ffn_in_proj_b"], "bo_f": a["L0_ffn_out_proj_b"], "boA": a["L0_attn_bo"],
        "rk": a["L0_attn_relative_k"], "rkT": a["L0_attn_relative_k"].T,
        "rv": a["L0_attn_relative_v"],
        "g1": a["L0_ffn_ln1_g"], "b1ln": a["L0_ffn_ln1_b"], "g2": a["L0_ffn_ln2_g"], "b2ln": a["L0_ffn_ln2_b"],
        "wg": a["L0_ffn_wg"], "w1T": a["L0_ffn_w1"].transpose(0, 2, 1), "w2": a["L0_ffn_w2"],
        "b1e": a["L0_ffn_b1"].reshape(E, FF // P, P).transpose(0, 2, 1), "b2e": a["L0_ffn_b2"], "consts": consts,
    }
    nc = bacc.Bacc("TRN2", target_bir_lowering=False, num_devices=1)
    arrays, ins = {}, {}
    for name, v in host.items():
        arrays["in_" + name] = np.ascontiguousarray(v)
        ins[name] = nc.dram_tensor("in_" + name, v.shape, mybir.dt.from_np(v.dtype), kind="ExternalInput").ap()
    ins["out"] = nc.dram_tensor("out", (TOK, D), F32, kind="ExternalOutput").ap()
    build(nc, ins)
    r = run_bass_kernel_spmd(nc, [arrays], core_ids=[0])
    return r.results[0]["out"].reshape(B, L, D)
```

```python
from contextlib import ExitStack

import concourse.bass as bass
from concourse import mybir

F32 = mybir.dt.float32
BF16 = mybir.dt.bfloat16
FP16 = mybir.dt.float16
U32 = mybir.dt.uint32
U16 = mybir.dt.uint16
I32 = mybir.dt.int32
ALU = mybir.AluOpType
ACT = mybir.ActivationFunctionType
AX_X = mybir.AxisListType.X
ds = bass.ds

P = 128
B, L, D = 2, 2048, 256
TOK = B * L
NT = TOK // P
H, DK = 16, 16
HH = H // 2
NC = B * 2
NI = L // P
W = HH * P
MAXLEN = 256
REL = 2 * MAXLEN - 1
EPS = 1e-5
FH, FHD = 4, 64
E, FF, CAP = 8, 1024, TOK // 8
CH = 4
NCH = NT // CH

BAND, HI, LO = 0, 1, 2
USE = [0, 3, 1, 4, 2, 5, -1, 6, -2, 7, -3, 8, 9, -4, -5, -6]
NX = 3
LAST = USE[-NX:]
SCORE = LAST + USE[:-NX]
BANDS = [k for k in USE if k < 3]
NB = len(BANDS)
LOWEST = -6 * P - (P - 1)
HIGHEST = 2 * P + (P - 1)
SPAN = HIGHEST - LOWEST + 1
TSW = SPAN - 7
TVU = SPAN - P + 1
TERMS = 6
PARTS = 3
QROWS = TERMS * DK
ROWS = QROWS + 2 * PARTS
K_PARTS = (0, 0, 0, 1, 1, 2)
Q_PARTS = (0, 1, 2, 0, 1, 0)
PAIRS = [(0, 0), (0, 1), (1, 0)]

C_ID, C_FOLD, C_PICK, C_DEN, C_MASK, C_MASKV, C_TRI, C_ONE, C_HEAD, C_IOTA, C_CAPE = 0, 128, 368, 560, 752, 760, 768, 896, 1024, 1032, 1040
C_N = 1048

START = 1


def start_counts(nc, sems):
    with nc.Block() as block:
        @block.sync
        def _(sp):
            for s in sems.values():
                sp.sem_inc(s, START)


def phase_project(nc, ins, dr, sem, sb, ps):
    xn_all, qkv_all = dr["xn_all"], dr["qkv_all"]
    wq, wk, wv, wi = sb("wq", [P, 2, D]), sb("wk", [P, 2, D]), sb("wv", [P, 2, D]), sb("wi", [P, 2, 3 * D])
    bqk = sb("bqk", [P, 4])
    bv, bi = sb("bv", [P, D]), sb("bi", [P, 3 * D])
    cst = sb("cst1", [P, C_N])
    tc2 = sb("tc2", [P, 2])
    selc = sb("selc", [P, 2, HH])
    xc = sb("xc", [P, 2, CH, D])
    stat, mv = sb("stat", [P, CH, 6]), sb("mv", [P, CH, 2])
    std, rstd = sb("std", [P, CH]), sb("rstd", [P, CH])
    xnc = sb("xnc", [P, CH, D])
    pause = sb("pause", [P, 1])
    xT = sb("xT", [P, 2, CH * P])
    qf = sb("qf", [P, 2, CH * P])
    res = sb("res", [P, CH * P])
    pair = sb("pair", [P, 2, 2, CH * P], FP16)
    part = sb("part", [P, 2, PARTS, CH * P], BF16)
    cres = sb("cres", [2 * HH, CH * P])
    cf = sb("cf", [2 * HH, CH * P])
    cpart = sb("cpart", [2 * HH, PARTS, CH * P], BF16)
    vs = sb("vs", [P, CH, D])
    tp = ps("tp", [P, 2, CH * P])
    pq = ps("pq", [P, 2, CH * P])
    pc = ps("pc", [P, CH * P])
    pv = ps("pv", [P, D])
    pi = ps("pi", [P, 2, 512])

    S = {n: sem("a_" + n) for n in (
        "weights xload stats aggr eps std rstd normed kept tp_done xT proj qf p0 r1 p1 p2 hi lo cmm cf c0 cr1 c1 c2 vmm vout "
        "imm iout qstore0 qstore1 cstore vstore selc tabl tabl2").split()}

    start_counts(nc, S)
    with nc.Block() as block:
        @block.sync
        def _(sp):
            for t, s in ((wq, "wqT"), (wk, "wkT"), (wv, "wvT"), (wi, "wiT")):
                sp.dma_start(t[:], ins[s].rearrange("(k p) n -> p k n", p=P)).then_inc(S["weights"], 16)
            sp.dma_start(bqk[:], ins["bqk"]).then_inc(S["weights"], 16)
            sp.dma_start(bv[:], ins["bv"].partition_broadcast(P)).then_inc(S["weights"], 16)
            sp.dma_start(bi[:], ins["bi"].partition_broadcast(P)).then_inc(S["weights"], 16)
            sp.dma_start(cst[:], ins["consts"]).then_inc(S["weights"], 16)
            for n, row in ((0, REL - 1), (1, 0)):
                src = bass.AP(ins["rk"].tensor, row * DK, [[1, DK], [0, HH], [1, 1]])
                sp.dma_start(tc2[:, n:n + 1], src).then_inc(S["weights"], 16)
            tk, rkT = dr["tk"], ins["rkT"]
            lo, mid = 129, 129 + REL
            sp.dma_start(tk[:, lo:mid], rkT).then_inc(S["tabl"], 16)
            sp.dma_start(tk[:, mid:mid + REL], rkT).then_inc(S["tabl"], 16)
            sp.dma_start(tk[:, 0:lo], bass.AP(rkT.tensor, 0, [[REL, DK], [0, lo], [1, 1]])).then_inc(S["tabl"], 16)
            sp.dma_start(tk[:, mid + REL:SPAN],
                         bass.AP(rkT.tensor, REL - 1, [[REL, DK], [0, P], [1, 1]])).then_inc(S["tabl"], 16)
            tv, rv = dr["tv"], ins["rv"]
            sp.dma_start(tv[0:lo, :], bass.AP(rv.tensor, 0, [[0, lo], [1, DK]])).then_inc(S["tabl"], 16)
            sp.dma_start(tv[lo:mid, :], rv).then_inc(S["tabl"], 16)
            sp.dma_start(tv[mid:mid + REL, :], rv).then_inc(S["tabl"], 16)
            sp.dma_start(tv[mid + REL:SPAN, :],
                         bass.AP(rv.tensor, (REL - 1) * DK, [[0, P], [1, DK]])).then_inc(S["tabl"], 16)
            xv = ins["x"].rearrange("(c a p) n -> p c a n", a=CH, p=P)
            with sp.Fori(0, NCH // 2) as h:
                for u in range(2):
                    ch = h * 2 + u
                    sp.wait_ge(S["kept"], START + h * 2)
                    sp.dma_start(xc[:, u], xv[:, ds(ch, 1)].rearrange("p c a n -> p (c a) n")).then_inc(S["xload"], 16)
                    for n in range(4):
                        ready = ch * 4 + n + 1
                        sp.wait_ge(S["p2"], START + ready)
                        dst = dr["qs"] if n < 2 else dr["ks"]
                        row = (ch // 4) * (2 * NI) + (n % 2) * NI + (ch % 4) * CH
                        for u6, q in enumerate(Q_PARTS if n < 2 else K_PARTS):
                            d = dst[ds(row, CH), u6 * W * DK:(u6 + 1) * W * DK].rearrange("i (p l) -> p i l", l=P)
                            sp.dma_start(d, part[:, n % 2, q, :].rearrange("p (i l) -> p i l", l=P)).then_inc(S[f"qstore{n % 2}"], 16)
                        if n < 2:
                            for q in range(2):
                                d = dr["qp"][ds(row, CH), q, :].rearrange("i (p l) -> p i l", l=P)
                                sp.dma_start(d, pair[:, n, q, :].rearrange("p (i l) -> p i l", l=P)).then_inc(S[f"qstore{n % 2}"], 16)
                            sp.wait_ge(S["c2"], START + ch * 2 + n + 1)
                            for q in range(PARTS):
                                for cl in range(2):
                                    d = dr["cs"][ds(row, CH), cl, q, :, :].rearrange("i h l -> h i l")
                                    sp.dma_start(d, cpart[cl * HH:(cl + 1) * HH, q, :].rearrange("h (i l) -> h i l", l=P)).then_inc(S["cstore"], 16)
                    sp.wait_ge(S["vout"], START + ch * CH + CH)
                    sp.dma_start(dr["v"].rearrange("(c a p) n -> p c a n", a=CH, p=P)[:, ds(ch, 1)].rearrange("p c a n -> p (c a) n"),
                                 vs[:]).then_inc(S["vstore"], 16)
            sp.wait_ge(S["tabl"], START + 16 * 8)
            for n in range(2):
                sp.wait_ge(S[f"qstore{n}"], START + 224 * NCH)
            sp.wait_ge(S["cstore"], START + 16 * 12 * NCH)
            sp.wait_ge(S["vstore"], START + 16 * NCH)

        @block.vector
        def _(dve):
            dve.wait_ge(S["weights"], START + 16 * 10)
            for n in range(2):
                nc.vector.tensor_scalar(selc[:, n, :], cst[:, C_HEAD:C_HEAD + HH], tc2[:, n:n + 1], None, ALU.mult).then_inc(S["selc"], 1)
            with dve.Fori(0, NCH // 2) as h:
                for u in range(2):
                    ch = h * 2 + u
                    dve.wait_ge(S["xload"], START + ch * 16 + 16)
                    for a in range(CH):
                        nc.vector.bn_stats(stat[:, a, :], xc[:, u, a, :]).then_inc(S["stats"], 1)
                    dve.wait_ge(S["stats"], START + ch * CH + CH)
                    nc.vector.memset(pause[:], 0.0)
                    for a in range(CH):
                        nc.vector.bn_aggr(mv[:, a, :], stat[:, a, :]).then_inc(S["aggr"], 1)
                    dve.wait_ge(S["aggr"], START + ch * CH + CH)
                    nc.vector.tensor_scalar(std[:], mv[:, :, 1], EPS, None, ALU.add).then_inc(S["eps"], 1)
                    dve.wait_ge(S["std"], START + ch + 1)
                    nc.vector.reciprocal(rstd[:], std[:]).then_inc(S["rstd"], 1)
                    dve.wait_ge(S["rstd"], START + ch + 1)
                    dve.wait_ge(S["tp_done"], START + ch)
                    dve.wait_ge(S["kept"], START + ch)
                    for a in range(CH):
                        nc.vector.tensor_scalar(xnc[:, a, :], xc[:, u, a, :], mv[:, a, 0:1], rstd[:, a:a + 1],
                                                ALU.subtract, ALU.mult).then_inc(S["normed"], 1)
                    for n in range(4):
                        k = ch * 4 + n
                        dve.wait_ge(S["proj"], START + k + 1)
                        dve.wait_ge(S[f"qstore{n % 2}"], START + ch * 224 + (128 if n >= 2 else 0))
                        dve.wait_ge(S["p2"], START + k)
                        if n < 2:
                            nc.vector.tensor_scalar(qf[:, n % 2, :], pq[:, n % 2, :], bqk[:, n:n + 1], None, ALU.add).then_inc(S["qf"], 1)
                        else:
                            nc.vector.tensor_scalar(qf[:, n % 2, :], pq[:, n % 2, :], bqk[:, n:n + 1], DK ** -0.5,
                                                    ALU.add, ALU.mult).then_inc(S["qf"], 1)
                        dve.wait_ge(S["p0"], START + k + 1)
                        nc.vector.tensor_tensor(res[:], qf[:, n % 2, :], part[:, n % 2, 0, :], ALU.subtract).then_inc(S["r1"], 1)
                        if n < 2:
                            dve.wait_ge(S["hi"], START + ch * 2 + n + 1)
                            nc.vector.tensor_tensor(pair[:, n, 1, :], qf[:, n, :], pair[:, n, 0, :], ALU.subtract).then_inc(S["lo"], 1)
                        dve.wait_ge(S["p1"], START + k + 1)
                        nc.vector.tensor_tensor(part[:, n % 2, 2, :], res[:], part[:, n % 2, 1, :], ALU.subtract).then_inc(S["p2"], 1)
                        if n < 2:
                            k = ch * 2 + n
                            dve.wait_ge(S["cmm"], START + k + 1)
                            dve.wait_ge(S["cstore"], START + k * 96)
                            dve.wait_ge(S["c2"], START + k)
                            nc.vector.tensor_copy(cf[:], pc[0:2 * HH, :]).then_inc(S["cf"], 1)
                            dve.wait_ge(S["cf"], START + k + 1)
                            nc.vector.tensor_copy(cpart[:, 0, :], cf[:]).then_inc(S["c0"], 1)
                            dve.wait_ge(S["c0"], START + k + 1)
                            nc.vector.tensor_tensor(cres[:], cf[:], cpart[:, 0, :], ALU.subtract).then_inc(S["cr1"], 1)
                            dve.wait_ge(S["cr1"], START + k + 1)
                            nc.vector.tensor_copy(cpart[:, 1, :], cres[:]).then_inc(S["c1"], 1)
                            dve.wait_ge(S["c1"], START + k + 1)
                            nc.vector.tensor_tensor(cpart[:, 2, :], cres[:], cpart[:, 1, :], ALU.subtract).then_inc(S["c2"], 1)
                    dve.wait_ge(S["vstore"], START + ch * 16)
                    for a in range(CH):
                        dve.wait_ge(S["vmm"], START + ch * CH + a + 1)
                        nc.vector.tensor_tensor(vs[:, a, :], pv[:], bv[:], ALU.add).then_inc(S["vout"], 1)
                        dve.wait_ge(S["imm"], START + ch * CH + a + 1)
                        out = qkv_all[:, ds(ch * CH + a, 1), :].rearrange("p a n -> p (a n)")
                        nc.vector.tensor_tensor(out[:, 0:512], pi[:, 0, :], bi[:, 0:512], ALU.add)
                        nc.vector.tensor_tensor(out[:, 512:768], pi[:, 1, 0:256], bi[:, 512:768], ALU.add).then_inc(S["iout"], 1)

        @block.scalar
        def _(act):
            with act.Fori(0, NCH) as ch:
                act.wait_ge(S["eps"], START + ch + 1)
                nc.scalar.activation(std[:], std[:], ACT.Sqrt).then_inc(S["std"], 1)
                act.wait_ge(S["tp_done"], START + ch + 1)
                act.wait_ge(S["imm"], START + ch * CH)
                for k in range(2):
                    nc.scalar.activation(xT[:, k, :], tp[:, k, :], ACT.Copy).then_inc(S["xT"], 1)
                for n in range(4):
                    act.wait_ge(S["qf"], START + ch * 4 + n + 1)
                    nc.scalar.activation(part[:, n % 2, 0, :], qf[:, n % 2, :], ACT.Copy).then_inc(S["p0"], 1)
                    if n < 2:
                        nc.scalar.activation(pair[:, n, 0, :], qf[:, n, :], ACT.Copy).then_inc(S["hi"], 1)
                    act.wait_ge(S["r1"], START + ch * 4 + n + 1)
                    nc.scalar.activation(part[:, n % 2, 1, :], res[:], ACT.Copy).then_inc(S["p1"], 1)

        @block.gpsimd
        def _(pool):
            with pool.Fori(0, NCH) as ch:
                pool.wait_ge(S["normed"], START + ch * CH + CH)
                nc.gpsimd.tensor_copy(xn_all[:, ds(ch * CH, CH), :], xnc[:]).then_inc(S["kept"], 1)

        @block.tensor
        def _(pe):
            pe.wait_ge(S["weights"], START + 16 * 10)
            pe.wait_ge(S["selc"], START + 2)
            ident = cst[:, C_ID:C_ID + P]
            with pe.Fori(0, NCH) as ch:
                pe.wait_ge(S["normed"], START + ch * CH + CH)
                pe.wait_ge(S["xT"], START + ch * 2)
                for k in range(2):
                    for a in range(CH):
                        last = nc.tensor.transpose(tp[:, k, a * P:(a + 1) * P], xnc[:, a, k * P:(k + 1) * P], ident)
                last.then_inc(S["tp_done"], 1)
                pe.wait_ge(S["xT"], START + ch * 2 + 2)
                for n in range(4):
                    w, half = (wq, n) if n < 2 else (wk, n - 2)
                    pe.wait_ge(S["qf"], START + ch * 4 + (n - 1 if n > 1 else 0))
                    for k in range(2):
                        last = nc.tensor.matmul(pq[:, n % 2, :], w[:, k, half * P:(half + 1) * P], xT[:, k, :],
                                                start=(k == 0), stop=(k == 1))
                    last.then_inc(S["proj"], 1)
                    if n < 2:
                        pe.wait_ge(S["qf"], START + ch * 4 + n + 1)
                        pe.wait_ge(S["cf"], START + ch * 2 + n)
                        nc.tensor.matmul(pc[0:2 * HH, :], selc[:].rearrange("p c h -> p (c h)"), qf[:, n % 2, :],
                                         start=True, stop=True).then_inc(S["cmm"], 1)
                for a in range(CH):
                    pe.wait_ge(S["vout"], START + ch * CH + a)
                    for k in range(2):
                        last = nc.tensor.matmul(pv[:], xT[:, k, a * P:(a + 1) * P], wv[:, k, :], start=(k == 0), stop=(k == 1))
                    last.then_inc(S["vmm"], 1)
                    pe.wait_ge(S["iout"], START + ch * CH + a)
                    for c in range(2):
                        n = 512 if c == 0 else 256
                        for k in range(2):
                            last = nc.tensor.matmul(pi[:, c, 0:n], xT[:, k, a * P:(a + 1) * P], wi[:, k, c * 512:c * 512 + n],
                                                    start=(k == 0), stop=(k == 1))
                    last.then_inc(S["imm"], 1)


def phase_pairs(nc, ins, dr, sem, sb, ps):
    xn_all, qkv_all, y1_all, logits = dr["xn_all"], dr["qkv_all"], dr["y1_all"], dr["logits"]
    wo, wg = sb("wo2", [P, 2, D]), sb("wg2", [P, 2, E])
    bo, g1, b1 = sb("bo2", [P, D]), sb("g1", [P, D]), sb("b1_", [P, D])
    cst = sb("cst2", [P, P])
    zero = sb("zero", [P, D])
    prod = sb("prod", [P, 2, 2, D])
    s = sb("s", [P, 2, 2, FH])
    m = sb("m", [P, 2, FH])
    r = sb("r", [P, 2, FH])
    pv_ = sb("pvp", [P, 2, 2, D])
    o = sb("o", [P, 2, D])
    oT = sb("oT", [P, 2, 2, P])
    z = sb("z", [P, 2, D])
    stat, mv = sb("stat2", [P, 2, 6]), sb("mv2", [P, 2, 2])
    std, rstd = sb("std2", [P, 2]), sb("rstd2", [P, 2])
    y1 = sb("y1", [P, 2, D])
    pause = sb("pause2", [P, 1])
    y1T = sb("y1T", [P, 2, 2, P])
    tp = ps("tp2", [P, 2, 2, P])
    po = ps("po", [P, 2, D])
    ty = ps("ty", [P, 2, 2, P])
    pl = ps("pl", [P, 2, E])

    S = {n: sem("b_" + n) for n in (
        "weights prod0 prod1 s0 s1 max diff exp sum rec prob vprod o tp oT proj z0 z1 stats aggr eps std rstd n0 n1 y1 kept "
        "ty y1T logit lout zset zeroed").split()}

    start_counts(nc, S)
    with nc.Block() as block:
        @block.sync
        def _(sp):
            sp.dma_start(wo[:], ins["woT"].rearrange("(k p) n -> p k n", p=P)).then_inc(S["weights"], 16)
            sp.dma_start(wg[:], ins["wg"].rearrange("(k p) n -> p k n", p=P)).then_inc(S["weights"], 16)
            for t, n in ((bo, "bo_f"), (g1, "g1"), (b1, "b1ln")):
                sp.dma_start(t[:], ins[n].partition_broadcast(P)).then_inc(S["weights"], 16)
            sp.dma_start(cst[:], ins["consts"][:, C_ID:C_ID + P]).then_inc(S["weights"], 16)
            sp.wait_ge(S["zset"], START + 1)
            for t in range(NT):
                sp.dma_start(dr["disp"][t * P:(t + 1) * P, :], zero[:]).then_inc(S["zeroed"], 16)
            sp.wait_ge(S["zeroed"], START + 16 * NT)

        @block.vector
        def _(dve):
            nc.vector.memset(zero[:], 0.0).then_inc(S["zset"], 1)
            dve.wait_ge(S["weights"], START + 16 * 6)
            kv = qkv_all[:].rearrange("p (b t) n -> p b t n", b=2)
            with dve.Fori(0, NI) as t:
                for b in range(2):
                    q = kv[:, b, ds(t, 1), 0:D]
                    for c in range(2):
                        nc.vector.tensor_tensor(prod[:, b, c, :].unsqueeze(1), q, kv[:, c, ds(t, 1), D:2 * D], ALU.mult).then_inc(S[f"prod{b}"], 1)
                for b in range(2):
                    dve.wait_ge(S[f"prod{b}"], START + t * 2 + 2)
                    dve.wait_ge(S["vprod"], START + t * 4)
                    nc.vector.tensor_reduce(s[:, b].rearrange("p c h -> p (c h)"),
                                            prod[:, b].rearrange("p c (h d) -> p (c h) d", h=FH), AX_X, ALU.add).then_inc(S[f"s{b}"], 1)
                for b in range(2):
                    dve.wait_ge(S[f"s{b}"], START + t + 1)
                nc.vector.tensor_tensor(m[:], s[:, :, 0, :], s[:, :, 1, :], ALU.max).then_inc(S["max"], 1)
                dve.wait_ge(S["max"], START + t + 1)
                for c in range(2):
                    nc.vector.tensor_tensor(s[:, :, c, :], s[:, :, c, :], m[:], ALU.subtract).then_inc(S["diff"], 1)
                dve.wait_ge(S["exp"], START + t + 1)
                nc.vector.tensor_tensor(m[:], s[:, :, 0, :], s[:, :, 1, :], ALU.add).then_inc(S["sum"], 1)
                dve.wait_ge(S["sum"], START + t + 1)
                nc.vector.reciprocal(r[:], m[:]).then_inc(S["rec"], 1)
                dve.wait_ge(S["rec"], START + t + 1)
                for c in range(2):
                    nc.vector.tensor_tensor(s[:, :, c, :], s[:, :, c, :], r[:], ALU.mult).then_inc(S["prob"], 1)
                dve.wait_ge(S["proj"], START + t + 1)
                nc.vector.tensor_tensor(z[:], po[:], bo[:].unsqueeze(1).to_broadcast([P, 2, D]), ALU.add).then_inc(S["z0"], 1)
                dve.wait_ge(S["z0"], START + t + 1)
                xv = xn_all[:].rearrange("p (b t) n -> p b t n", b=2)
                for b in range(2):
                    nc.vector.tensor_tensor(z[:, b:b + 1, :], z[:, b:b + 1, :], xv[:, b, ds(t, 1), :], ALU.add).then_inc(S["z1"], 1)
                for b in range(2):
                    dve.wait_ge(S["z1"], START + t * 2 + b + 1)
                    nc.vector.bn_stats(stat[:, b, :], z[:, b, :]).then_inc(S["stats"], 1)
                dve.wait_ge(S["stats"], START + t * 2 + 2)
                nc.vector.memset(pause[:], 0.0)
                for b in range(2):
                    nc.vector.bn_aggr(mv[:, b, :], stat[:, b, :]).then_inc(S["aggr"], 1)
                dve.wait_ge(S["aggr"], START + t * 2 + 2)
                nc.vector.tensor_scalar(std[:], mv[:, :, 1], EPS, None, ALU.add).then_inc(S["eps"], 1)
                dve.wait_ge(S["std"], START + t + 1)
                nc.vector.reciprocal(rstd[:], std[:]).then_inc(S["rstd"], 1)
                dve.wait_ge(S["rstd"], START + t + 1)
                for b in range(2):
                    nc.vector.tensor_scalar(z[:, b, :], z[:, b, :], mv[:, b, 0:1], rstd[:, b:b + 1],
                                            ALU.subtract, ALU.mult).then_inc(S["n0"], 1)
                dve.wait_ge(S["n0"], START + t * 2 + 2)
                nc.vector.tensor_tensor(z[:], z[:], g1[:].unsqueeze(1).to_broadcast([P, 2, D]), ALU.mult).then_inc(S["n1"], 1)
                dve.wait_ge(S["n1"], START + t + 1)
                dve.wait_ge(S["kept"], START + t * 2)
                dve.wait_ge(S["ty"], START + t)
                nc.vector.tensor_tensor(y1[:], z[:], b1[:].unsqueeze(1).to_broadcast([P, 2, D]), ALU.add).then_inc(S["y1"], 1)
                dve.wait_ge(S["logit"], START + t + 1)
                lv = logits[:].rearrange("p (b t) e -> p b t e", b=2)
                for b in range(2):
                    nc.vector.tensor_copy(lv[:, b, ds(t, 1), :], pl[:, b:b + 1, :]).then_inc(S["lout"], 1)

        @block.gpsimd
        def _(pool):
            kv = qkv_all[:].rearrange("p (b t) n -> p b t n", b=2)
            with pool.Fori(0, NI) as t:
                pool.wait_ge(S["prob"], START + t * 2 + 2)
                for b in range(2):
                    for c in range(2):
                        nc.gpsimd.tensor_tensor(pv_[:, b, c, :].rearrange("p (h d) -> p h d", h=FH),
                                                kv[:, c, ds(t, 1), 2 * D:3 * D].rearrange("p t (h d) -> p (t h) d", h=FH),
                                                s[:, b, c, :].unsqueeze(2).to_broadcast([P, FH, FHD]), ALU.mult).then_inc(S["vprod"], 1)
                pool.wait_ge(S["vprod"], START + t * 4 + 4)
                pool.wait_ge(S["tp"], START + t)
                nc.gpsimd.tensor_tensor(o[:], pv_[:, :, 0, :], pv_[:, :, 1, :], ALU.add).then_inc(S["o"], 1)
                pool.wait_ge(S["y1"], START + t + 1)
                yv = y1_all[:].rearrange("p (b t) n -> p b t n", b=2)
                for b in range(2):
                    nc.gpsimd.tensor_copy(yv[:, b, ds(t, 1), :], y1[:, b:b + 1, :]).then_inc(S["kept"], 1)

        @block.scalar
        def _(act):
            with act.Fori(0, NI) as t:
                act.wait_ge(S["diff"], START + t * 2 + 2)
                nc.scalar.activation(s[:], s[:], ACT.Exp, scale=FHD ** -0.5).then_inc(S["exp"], 1)
                act.wait_ge(S["tp"], START + t + 1)
                act.wait_ge(S["proj"], START + t)
                nc.scalar.activation(oT[:], tp[:], ACT.Copy).then_inc(S["oT"], 1)
                act.wait_ge(S["eps"], START + t + 1)
                nc.scalar.activation(std[:], std[:], ACT.Sqrt).then_inc(S["std"], 1)
                act.wait_ge(S["ty"], START + t + 1)
                act.wait_ge(S["logit"], START + t)
                nc.scalar.activation(y1T[:], ty[:], ACT.Copy).then_inc(S["y1T"], 1)

        @block.tensor
        def _(pe):
            pe.wait_ge(S["weights"], START + 16 * 6)
            with pe.Fori(0, NI) as t:
                pe.wait_ge(S["o"], START + t + 1)
                pe.wait_ge(S["oT"], START + t)
                for b in range(2):
                    for k in range(2):
                        last = nc.tensor.transpose(tp[:, b, k, :], o[:, b, k * P:(k + 1) * P], cst[:])
                last.then_inc(S["tp"], 1)
                pe.wait_ge(S["oT"], START + t + 1)
                pe.wait_ge(S["z0"], START + t)
                for b in range(2):
                    for k in range(2):
                        last = nc.tensor.matmul(po[:, b, :], oT[:, b, k, :], wo[:, k, :], start=(k == 0), stop=(k == 1))
                last.then_inc(S["proj"], 1)
                pe.wait_ge(S["y1"], START + t + 1)
                pe.wait_ge(S["y1T"], START + t)
                for b in range(2):
                    for k in range(2):
                        last = nc.tensor.transpose(ty[:, b, k, :], y1[:, b, k * P:(k + 1) * P], cst[:])
                last.then_inc(S["ty"], 1)
                pe.wait_ge(S["y1T"], START + t + 1)
                pe.wait_ge(S["lout"], START + t * 2)
                for b in range(2):
                    for k in range(2):
                        last = nc.tensor.matmul(pl[:, b, :], y1T[:, b, k, :], wg[:, k, :], start=(k == 0), stop=(k == 1))
                last.then_inc(S["logit"], 1)


def phase_route(nc, ins, dr, sem, sb, ps):
    y1_all, logits, gate, slot_u, back_u = dr["y1_all"], dr["logits"], dr["gate"], dr["slot_u"], dr["back_u"]
    n = [P, NT, E]
    cst = sb("cst3", [P, C_N])
    mx, rec = sb("mx", [P, NT]), sb("rec", [P, NT])
    ex, hot, rank = sb("ex", n), sb("hot", n), sb("rank", n)
    pre, tot = sb("pre", n), sb("tot", [P, E, 2 * NT])
    tot2 = sb("tot2", [P, E, 2 * NT])
    loc, idx, keep, slot = sb("loc", [P, NT]), sb("idx", [P, NT]), sb("keep", [P, NT]), sb("slot", [P, NT])
    tmp = sb("tmp", [P, NT])
    pp, pt = ps("pp", n), ps("pt", n)
    s_cst, s_v, s_exp, s_hot, s_cum, s_sc = sem("c_cst"), sem("c_steps"), sem("c_exp"), sem("c_hot"), sem("c_cum"), sem("c_scattered")
    s_slot = sem("c_slots")

    with nc.Block() as block:
        @block.sync
        def _(sp):
            sp.dma_start(cst[:], ins["consts"]).then_inc(s_cst, 16)

        @block.scalar
        def _(act):
            act.wait_ge(s_v, 2)
            nc.scalar.activation(ex[:], ex[:], ACT.Exp).then_inc(s_exp, 1)

        @block.tensor
        def _(pe):
            pe.wait_ge(s_cst, 16)
            pe.wait_ge(s_hot, 1)
            nc.tensor.matmul(pp[:], cst[:, C_TRI:C_TRI + P], hot[:], start=True, stop=True)
            nc.tensor.matmul(pt[:], cst[:, C_ONE:C_ONE + P], hot[:], start=True, stop=True).then_inc(s_cum, 1)

        @block.vector
        def _(dve):
            step = [0]

            def done(ins_):
                step[0] += 1
                ins_.then_inc(s_v, 1)
                dve.wait_ge(s_v, step[0])

            def wide(t):
                return t[:].unsqueeze(2).to_broadcast(n)

            done(nc.vector.tensor_reduce(mx[:], logits[:], AX_X, ALU.max))
            done(nc.vector.tensor_tensor(ex[:], logits[:], wide(mx), ALU.subtract))
            dve.wait_ge(s_exp, 1)
            done(nc.vector.tensor_reduce(tmp[:], ex[:], AX_X, ALU.add))
            done(nc.vector.reciprocal(rec[:], tmp[:]))
            done(nc.vector.tensor_reduce(mx[:], ex[:], AX_X, ALU.max))
            done(nc.vector.tensor_tensor(gate[:], mx[:], rec[:], ALU.mult))
            done(nc.vector.tensor_tensor(hot[:], ex[:], wide(mx), ALU.is_ge))
            dve.wait_ge(s_cst, 16)
            done(nc.vector.tensor_tensor(rank[:], hot[:], cst[:, C_IOTA:C_IOTA + E].unsqueeze(1).to_broadcast(n), ALU.mult))
            done(nc.vector.tensor_reduce(mx[:], rank[:], AX_X, ALU.max))
            nc.vector.tensor_tensor(hot[:], cst[:, C_IOTA:C_IOTA + E].unsqueeze(1).to_broadcast(n), wide(mx),
                                    ALU.is_equal).then_inc(s_hot, 1)
            dve.wait_ge(s_cum, 1)
            done(nc.vector.tensor_copy(pre[:], pp[:]))
            done(nc.vector.memset(tot[:], 0.0))
            done(nc.vector.memset(tot2[:], 0.0))
            done(nc.vector.tensor_copy(tot[:, :, NT + 1:2 * NT], pt[:, 0:NT - 1, :].rearrange("p t e -> p e t")))
            a, b = tot, tot2
            d = 1
            while d < NT:
                done(nc.vector.tensor_tensor(b[:, :, NT:2 * NT], a[:, :, NT:2 * NT], a[:, :, NT - d:2 * NT - d], ALU.add))
                a, b = b, a
                d *= 2
            done(nc.vector.tensor_tensor(pre[:], pre[:], a[:, :, NT:2 * NT].rearrange("p e t -> p t e"), ALU.add))
            done(nc.vector.tensor_tensor(pre[:], pre[:], hot[:], ALU.mult))
            done(nc.vector.tensor_reduce(loc[:], pre[:], AX_X, ALU.add))
            done(nc.vector.tensor_scalar(keep[:], loc[:], float(CAP), None, ALU.is_lt))
            done(nc.vector.tensor_tensor(pre[:], hot[:], cst[:, C_CAPE:C_CAPE + E].unsqueeze(1).to_broadcast(n), ALU.mult))
            done(nc.vector.tensor_reduce(idx[:], pre[:], AX_X, ALU.add))
            done(nc.vector.tensor_tensor(slot[:], idx[:], loc[:], ALU.add))
            done(nc.vector.tensor_scalar(tmp[:], keep[:], -1.0, -float(2 * TOK), ALU.add, ALU.mult))
            done(nc.vector.tensor_tensor(gate[:], gate[:], keep[:], ALU.mult))
            done(nc.vector.tensor_tensor(loc[:], slot[:], tmp[:], ALU.add))
            done(nc.vector.tensor_copy(slot_u[:], loc[:]))
            done(nc.vector.tensor_scalar(loc[:], slot[:], float(TOK - 1), None, ALU.min))
            nc.vector.tensor_copy(back_u[:], loc[:]).then_inc(s_slot, 1)

        @block.gpsimd
        def _(pool):
            pool.wait_ge(s_slot, 1)
            for t in range(NT):
                nc.gpsimd.indirect_dma_start(dr["disp"], bass.IndirectOffsetOnAxis(ap=slot_u[:, t:t + 1], axis=0),
                                             y1_all[:, t, :], None, bounds_check=TOK - 1, oob_is_err=False).then_inc(s_sc, 16)
            pool.wait_ge(s_sc, 16 * NT)


def phase_experts(nc, ins, dr, sem, sb, ps):
    CK = FF // P
    w1 = sb("w1e", [P, 2, CK, D])
    w2 = sb("w2e", [P, 2, CK, D])
    b1 = sb("b1e", [P, 2, CK])
    b2 = sb("b2e", [1, 2, D])
    ones = sb("ones", [1, P])
    ident = sb("ident4", [P, P])
    x = sb("xe", [P, 2, CH, D])
    xT = sb("xeT", [P, 2, CAP])
    w = sb("we", [P, 2, D])
    bb = sb("be", [1, D])
    y = sb("ye", [P, CH, D])
    pw, pb, tp, py = ps("pw", [P, 2, 512]), ps("pb", [1, 512]), ps("tpe", [P, 2, CAP]), ps("pye", [P, 2, 512])
    S = {n: sem("d_" + n) for n in "load0 load1 const ones wmm bmm wout bout tp xT ymm yout stored".split()}

    with nc.Block() as block:
        @block.sync
        def _(sp):
            sp.dma_start(ident[:], ins["consts"][:, C_ID:C_ID + P]).then_inc(S["const"], 16)
            for e in range(E):
                u = e % 2
                if e >= 2:
                    sp.wait_ge(S["wout"], e - 1)
                    sp.wait_ge(S["bout"], e - 1)
                    sp.wait_ge(S["tp"], e - 1)
                sp.dma_start(w1[:, u], ins["w1T"][e].rearrange("(c p) n -> p c n", p=P)).then_inc(S[f"load{u}"], 16)
                sp.dma_start(w2[:, u], ins["w2"][e].rearrange("(c p) n -> p c n", p=P)).then_inc(S[f"load{u}"], 16)
                sp.dma_start(b1[:, u, :], ins["b1e"][e]).then_inc(S[f"load{u}"], 16)
                sp.dma_start(b2[:, u, :], ins["b2e"][e:e + 1, :]).then_inc(S[f"load{u}"], 16)
                sp.dma_start(x[:, u], dr["disp"][e * CAP:(e + 1) * CAP, :].rearrange("(a p) n -> p a n", p=P)).then_inc(S[f"load{u}"], 16)

        @block.tensor
        def _(pe):
            pe.wait_ge(S["const"], 16)
            pe.wait_ge(S["ones"], 1)
            for e in range(E):
                u = e % 2
                pe.wait_ge(S[f"load{u}"], 80 * (e // 2 + 1))
                if e:
                    pe.wait_ge(S["xT"], 2 * e)
                    pe.wait_ge(S["wout"], e)
                    pe.wait_ge(S["bout"], e)
                for k in range(2):
                    for a in range(CH):
                        last = nc.tensor.transpose(tp[:, k, a * P:(a + 1) * P], x[:, u, a, k * P:(k + 1) * P], ident[:])
                last.then_inc(S["tp"], 1)
                for c in range(CK):
                    last = nc.tensor.matmul(pb[0:1, 0:D], b1[:, u, c:c + 1], w2[:, u, c, :], start=(c == 0), stop=(c == CK - 1))
                last.then_inc(S["bmm"], 1)
                for k in range(2):
                    for c in range(CK):
                        last = nc.tensor.matmul(pw[:, k, 0:D], w1[:, u, c, k * P:(k + 1) * P], w2[:, u, c, :],
                                                start=(c == 0), stop=(c == CK - 1))
                last.then_inc(S["wmm"], 1)
                pe.wait_ge(S["xT"], 2 * e + 2)
                pe.wait_ge(S["wout"], e + 1)
                pe.wait_ge(S["bout"], e + 1)
                for a in range(CH):
                    n = e * CH + a
                    if n >= 2:
                        pe.wait_ge(S["yout"], n - 1)
                    for k in range(2):
                        nc.tensor.matmul(py[:, a % 2, 0:D], xT[:, k, a * P:(a + 1) * P], w[:, k, :], start=(k == 0), stop=False)
                    nc.tensor.matmul(py[:, a % 2, 0:D], ones[:], bb[:], start=False, stop=True).then_inc(S["ymm"], 1)

        @block.vector
        def _(dve):
            nc.vector.memset(ones[:], 1.0).then_inc(S["ones"], 1)
            for e in range(E):
                dve.wait_ge(S["bmm"], e + 1)
                if e:
                    dve.wait_ge(S["ymm"], e * CH)
                nc.vector.tensor_tensor(bb[:], pb[0:1, 0:D], b2[:, e % 2, :], ALU.add).then_inc(S["bout"], 1)
                dve.wait_ge(S["wmm"], e + 1)
                nc.vector.tensor_copy(w[:], pw[:, :, 0:D]).then_inc(S["wout"], 1)

        @block.scalar
        def _(act):
            for e in range(E):
                act.wait_ge(S["tp"], e + 1)
                if e:
                    act.wait_ge(S["ymm"], e * CH)
                for k in range(2):
                    nc.scalar.activation(xT[:, k, :], tp[:, k, :], ACT.Copy).then_inc(S["xT"], 1)
                if e:
                    act.wait_ge(S["stored"], 16 * e)
                for a in range(CH):
                    act.wait_ge(S["ymm"], e * CH + a + 1)
                    nc.scalar.activation(y[:, a, :], py[:, a % 2, 0:D], ACT.Copy).then_inc(S["yout"], 1)
                act.wait_ge(S["yout"], e * CH + CH)
                act.dma_start(dr["yexp"][e * CAP:(e + 1) * CAP, :].rearrange("(a p) n -> p a n", p=P), y[:]).then_inc(S["stored"], 16)
            act.wait_ge(S["stored"], 16 * E)


def phase_gate(nc, ins, dr, sem, sb, ps):
    y1_all, gate, back_u = dr["y1_all"], dr["gate"], dr["back_u"]
    yg = sb("yg", [P, NT, D])
    g2, b2 = sb("g2", [P, D]), sb("b2ln", [P, D])
    stat, mv = sb("stat5", [P, 4, 6]), sb("mv5", [P, 4, 2])
    std, rstd = sb("std5", [P, 4]), sb("rstd5", [P, 4])
    z, ez = sb("z5", [P, 4, D]), sb("ez", [P, 4, D])
    S = {n: sem("e_" + n) for n in "weights gathered z stats aggr eps std rstd n0 n1 n2 exp one rec out stored".split()}

    with nc.Block() as block:
        @block.sync
        def _(sp):
            sp.dma_start(g2[:], ins["g2"].partition_broadcast(P)).then_inc(S["weights"], 16)
            sp.dma_start(b2[:], ins["b2ln"].partition_broadcast(P)).then_inc(S["weights"], 16)
            for h in range(NT // 4):
                sp.wait_ge(S["out"], h + 1)
                sp.dma_start(dr["g"].rearrange("(t p) n -> p t n", p=P)[:, 4 * h:4 * h + 4, :], ez[:]).then_inc(S["stored"], 16)
            sp.wait_ge(S["stored"], 16 * (NT // 4))

        @block.gpsimd
        def _(pool):
            for t in range(NT):
                nc.gpsimd.indirect_dma_start(yg[:, t, :], None, dr["yexp"],
                                             bass.IndirectOffsetOnAxis(ap=back_u[:, t:t + 1], axis=0)).then_inc(S["gathered"], 16)

        @block.vector
        def _(dve):
            dve.wait_ge(S["weights"], 32)
            dve.wait_ge(S["gathered"], 16 * NT)
            for h in range(NT // 4):
                if h:
                    dve.wait_ge(S["out"], h)
                for a in range(4):
                    t = 4 * h + a
                    nc.vector.scalar_tensor_tensor(z[:, a, :], yg[:, t, :], gate[:, t:t + 1], y1_all[:, t, :],
                                                   ALU.mult, ALU.add).then_inc(S["z"], 1)
                for a in range(4):
                    dve.wait_ge(S["z"], 4 * h + a + 1)
                    nc.vector.bn_stats(stat[:, a, :], z[:, a, :]).then_inc(S["stats"], 1)
                for a in range(4):
                    dve.wait_ge(S["stats"], 4 * h + a + 1)
                    nc.vector.bn_aggr(mv[:, a, :], stat[:, a, :]).then_inc(S["aggr"], 1)
                dve.wait_ge(S["aggr"], 4 * h + 4)
                nc.vector.tensor_scalar(std[:], mv[:, :, 1], EPS, None, ALU.add).then_inc(S["eps"], 1)
                dve.wait_ge(S["std"], h + 1)
                nc.vector.reciprocal(rstd[:], std[:]).then_inc(S["rstd"], 1)
                dve.wait_ge(S["rstd"], h + 1)
                for a in range(4):
                    nc.vector.tensor_scalar(z[:, a, :], z[:, a, :], mv[:, a, 0:1], rstd[:, a:a + 1],
                                            ALU.subtract, ALU.mult).then_inc(S["n0"], 1)
                dve.wait_ge(S["n0"], 4 * h + 4)
                nc.vector.tensor_tensor(z[:], z[:], g2[:].unsqueeze(1).to_broadcast([P, 4, D]), ALU.mult).then_inc(S["n1"], 1)
                dve.wait_ge(S["n1"], h + 1)
                nc.vector.tensor_tensor(z[:], z[:], b2[:].unsqueeze(1).to_broadcast([P, 4, D]), ALU.add).then_inc(S["n2"], 1)
                dve.wait_ge(S["exp"], h + 1)
                nc.vector.tensor_scalar(ez[:], ez[:], 1.0, None, ALU.add).then_inc(S["one"], 1)
                dve.wait_ge(S["one"], h + 1)
                nc.vector.reciprocal(ez[:], ez[:]).then_inc(S["rec"], 1)
                dve.wait_ge(S["rec"], h + 1)
                nc.vector.tensor_tensor(ez[:], z[:], ez[:], ALU.mult).then_inc(S["out"], 1)

        @block.scalar
        def _(act):
            for h in range(NT // 4):
                act.wait_ge(S["eps"], h + 1)
                nc.scalar.activation(std[:], std[:], ACT.Sqrt).then_inc(S["std"], 1)
                act.wait_ge(S["n2"], h + 1)
                if h:
                    act.wait_ge(S["stored"], 16 * h)
                nc.scalar.activation(ez[:], z[:], ACT.Exp, scale=-1.0).then_inc(S["exp"], 1)


def tile_at(i, k):
    if k >= 0:
        over = (i + k) // NI
        return (i + k) % NI, (2 * over if k < 3 else over + 1)
    inside = (i + k + NI) // NI
    return (i + k + NI) % NI, 1 - inside


def phase_attend(nc, ins, dr, sem, sb, ps):
    kt = sb("kt", [ROWS, 4, W], BF16)
    slots = sb("slots", [P, NI + NX, 2, HH, 64])
    qst = sb("qst", [ROWS, 2, W], BF16)
    qbd = sb("qbd", [P, 2, 2, HH, P], FP16)
    tks = sb("tks", [P, 2, TSW], FP16)
    tvs = sb("tvs", [P, 2, TVU * DK], FP16)
    pp2 = sb("prob_parts", [P, 3, 2, 2, HH, 64], FP16)
    vrow = sb("vrow", [P, 4, HH * DK])
    vt = sb("vt", [P, 2, HH, 32])
    rc = sb("rc", [P, 3, DK])
    mx = sb("mxr", [P, 2, HH, 64])
    mb = sb("mb", [P, 2, HH, 64])
    rom = sb("rom", [P, 16, HH, 8])
    mcol = sb("mcol", [P, 8])
    pvs = sb("pvs", [P, 2, P])
    otn = sb("otn", [P, P])
    cst = sb("cst6", [P, C_TRI])
    spp = ps("spp", [P, 2, 2, HH, 64])
    ro = ps("ro", [P, 2, 8, HH, 8])
    pvp = ps("pvps", [P, 2, P])
    otp = ps("otp", [P, 2, P])
    mask = cst[:, C_MASK:C_MASK + 8]
    flat = slots[:].rearrange("p n a h l -> p (n a h l)")
    half_table = TVU * DK // 2
    tk_whole = flat[:, 0:TSW]
    tv_whole = flat[:, 2048:2048 + half_table]
    NG = NC * NI

    S = {n: sem("f_" + n) for n in (
        "tables tables2 split preset k0 k1 k2 k3 q0 q1 qbd_load0 qbd_load1 qbd vrow0 vrow1 vrow2 vrow3 vt scored stored "
        "mxd turned mcol mbp mb sub prob prob_hi prob_lo used rom pvs folded rden normed otout").split()}

    def slot(g2, k):
        if k in LAST:
            return slots[:, LAST.index(k) * 2 + g2]
        return slots[:, 2 * NX + USE.index(k)]

    def used_before(gg, band):
        return gg * NI + (USE.index(BANDS[band - 3]) + 1 if band >= 3 else 0)

    def scores(pe, g, i, g2, m):
        k = SCORE[m]
        if m == 0:
            pe.wait_ge(S[f"q{g2}"], START + (g // 2 + 1) * 48)
            pe.wait_ge(S["qbd"], START + g * 2 + 2)
        pe.wait_ge(S[f"k{m % 4}"], START + (g * 4 + m // 4 + 1) * 32)
        if m < 2:
            pe.wait_ge(S["mb"], START + g)
        else:
            pe.wait_ge(S["stored"], START + g * NI + m - 1)
        out = spp[:, m % 2]

        def product(h):
            for half in range(2):
                last = nc.tensor.matmul(out[:, half, h, :], kt[:, m % 4, h * P:(h + 1) * P],
                                        qst[:, g2, h * P + half * 64:h * P + half * 64 + 64],
                                        start=(h == 0), stop=(h == HH - 1), skip_group_check=True)
            return last

        def relative():
            for q in range(16):
                x0 = k * P - 8 * q - LOWEST - 7
                for a, b in PAIRS:
                    nc.tensor.matmul(out[:, q // 8, :, (q % 8) * 8:(q % 8) * 8 + 8], tks[:, a, x0:x0 + P],
                                     qbd[:, g2, b, :, 8 * q:8 * q + 8], start=False, stop=False, skip_group_check=True)

        for h in range(HH - 1):
            product(h)
        where_in_band(pe, i, k, relative)
        product(HH - 1).then_inc(S["scored"], 1)

    def where_in_band(pe, i, k, relative):
        if k == 0:
            relative()
        elif k in BANDS:
            with pe.If(i > -k - 1 if k < 0 else i < NI - k):
                relative()

    def values(pe, gg, i, g2, m):
        k = USE[m]
        pe.wait_ge(S["vt"], START + gg * NI + m + 1)
        if k in BANDS:
            pe.wait_ge(S["prob_lo"], START + gg * NB + BANDS.index(k) + 1)
        else:
            pe.wait_ge(S["prob"], START + gg * NI + m + 1)
        if m == 0:
            pe.wait_ge(S["rom"], START + gg)
            pe.wait_ge(S["pvs"], START + gg)

        def relative():
            parts = pp2[:, BANDS.index(k) % 3]
            for q in range(16):
                u0 = k * P - 8 * q - 7 - LOWEST
                for t, (a, b) in enumerate(PAIRS):
                    nc.tensor.matmul(ro[:, q // 8, q % 8, :, :], tvs[:, a, u0 * DK:(u0 + 8) * DK],
                                     parts[:, b, q // 8, :, (q % 8) * 8:(q % 8) * 8 + 8],
                                     start=(m == 0 and q % 8 == 0 and t == 0), stop=False, skip_group_check=True)

        where_in_band(pe, i, k, relative)
        for h in range(HH):
            c, q = h % 4, h // 4
            last = nc.tensor.matmul(pvp[32 * c:32 * c + 32, q, :].rearrange("p (a l) -> p a l", a=2), vt[:, m % 2, h, :],
                                    slot(g2, k)[:, :, h, :], start=(m == 0 and q == 0), stop=(m == NI - 1),
                                    skip_group_check=True)
        last.then_inc(S["used"], 1)

    def turn_max(pe, g):
        pe.wait_ge(S["mxd"], START + (g + 1) * NI)
        pe.wait_ge(S["stored"], START + (g + 1) * NI)
        lanes = mx[:].rearrange("p a h l -> p (a h l)")
        tp = spp[:, 0].rearrange("p a h l -> p (a h l)")
        for c in range(8):
            last = nc.tensor.transpose(tp[:, c * P:(c + 1) * P], lanes[:, c * P:(c + 1) * P], cst[:, C_ID:C_ID + P])
        last.then_inc(S["turned"], 1)

    def spread_max(pe, g):
        pe.wait_ge(S["mcol"], START + g + 1)
        bc = spp[:, 1].rearrange("p a h l -> p (a h l)")
        for c in range(8):
            last = nc.tensor.matmul(bc[:, c * P:(c + 1) * P], mcol[:, c:c + 1].to_broadcast([P, P]), cst[:, C_ID:C_ID + P],
                                    start=True, stop=True)
        last.then_inc(S["mbp"], 1)

    def fold(pe, gg):
        pe.wait_ge(S["rom"], START + gg + 1)
        pe.wait_ge(S["pvs"], START + gg + 1)
        pe.wait_ge(S["normed"], START + gg)
        for h in range(HH):
            nc.tensor.matmul(otp[:, 0, :].rearrange("p (b l) -> p b l", b=16), cst[:, C_FOLD + 112 - 16 * h:C_FOLD + 240 - 16 * h],
                             rom[:, :, h, :], start=(h == 0), stop=False)
        for q in range(2):
            nc.tensor.matmul(otp[:, 0, :], cst[:, C_PICK + 64 - 64 * q:C_PICK + 192 - 64 * q], pvs[:, q, :],
                             start=False, stop=(q == 1))
        for q in range(2):
            last = nc.tensor.matmul(otp[:, 1, :], cst[:, C_DEN + 64 - 64 * q:C_DEN + 192 - 64 * q], pvs[:, q, :],
                                    start=(q == 0), stop=(q == 1))
        last.then_inc(S["folded"], 1)

    def over_groups(eng, body):
        with eng.Fori(0, NG // 2 - 1) as t:
            body(t * 2, 0, 2)
            body(t * 2 + 1, 1, 2)
        body(NG - 2, 0, 1)
        body(NG - 1, 1, 0)

    start_counts(nc, S)
    with nc.Block() as block:
        @block.sync
        def _(sp):
            sp.dma_start(cst[:], ins["consts"][:, 0:C_TRI]).then_inc(S["tables"], 16)
            tk, tv = dr["tk"], dr["tv"]
            for l in range(8):
                sp.dma_start(tk_whole[16 * l:16 * l + 16, :], tk[:, 7 - l:7 - l + TSW]).then_inc(S["tables"], 16)
            sp.dma_start(tv_whole, bass.AP(tv.tensor, 0, [[DK, P], [1, half_table]])).then_inc(S["tables"], 16)
            for n, row in ((1, REL - 1), (2, 0)):
                sp.dma_start(rc[:, n, :], bass.AP(ins["rv"].tensor, row * DK, [[0, P], [1, DK]])).then_inc(S["tables"], 16)
            sp.wait_ge(S["split"], START + 4)
            sp.dma_start(tv_whole, bass.AP(tv.tensor, half_table, [[DK, P], [1, half_table]])).then_inc(S["tables2"], 16)

            def load_q(g, g2):
                row = dr["qs"][ds(g, 1), :].rearrange("a (p n) -> (a p) n", n=W)
                sp.dma_start(qst[0:QROWS, g2, :], row).then_inc(S[f"q{g2}"], 16)
                for cl in range(2):
                    at = QROWS + cl * PARTS
                    src = dr["cs"][ds(g, 1), cl].rearrange("a q h l -> (a q) (h l)")
                    sp.dma_start(qst[at:at + PARTS, g2, :], src).then_inc(S[f"q{g2}"], 16)
                for q in range(2):
                    src = bass.AP(dr["qp"].tensor, (g * 2 + q) * (DK * W), [[0, 8], [W, DK], [1, W]])
                    sp.dma_start(qbd[:, g2, q], src).then_inc(S[f"qbd_load{g2}"], 16)

            def load_key(g, i, m, scored):
                j, cls = tile_at(i, SCORE[m])
                if scored is not None:
                    sp.wait_ge(S["scored"], scored)
                row = dr["ks"][ds((g // NI) * NI + j, 1), :].rearrange("a (p n) -> (a p) n", n=W)
                sp.dma_start(kt[0:QROWS, m % 4, :], row).then_inc(S[f"k{m % 4}"], 16)
                src = ins["sel"][ds(cls, 1)].rearrange("a p n -> (a p) n")
                sp.dma_start(kt[QROWS:ROWS, m % 4, :].bitcast(U16), src).then_inc(S[f"k{m % 4}"], 16)

            def load_value(gg, i, m):
                j, _ = tile_at(i, USE[m])
                sp.wait_ge(S["vt"], START + gg * NI + max(m - 3, 0))
                src = bass.AP(dr["v"].tensor, (gg // 32) * (L * D) + ((gg // NI) % 2) * P + j * (P * D), [[D, P], [1, P]])
                sp.dma_start(vrow[:, m % 4, :], src).then_inc(S[f"vrow{m % 4}"], 16)

            def store(gg):
                sp.wait_ge(S["normed"], START + gg + 1)
                sp.dma_start(dr["ot"][ds(gg, 1)].rearrange("g p l -> p (g l)"), otn[:]).then_inc(S["otout"], 16)

            def load_tile(gg, m, more):
                load_value(gg, gg % NI, m)
                if more:
                    load_key(gg + 1, (gg + 1) % NI, m, START + (gg + 1) * NI + max(m - 3, 0))

            def body(gg, g2, ahead):
                for m in range(HEAD, NI):
                    load_tile(gg, m, ahead)
                    if m == HEAD and ahead == 2:
                        load_q(gg + 2, g2)
                if ahead:
                    for m in range(HEAD):
                        load_tile(gg + 1, m, ahead == 2)
                store(gg)

            HEAD = 7
            load_q(0, 0)
            for m in range(NI):
                load_key(0, 0, m, START + m - 3 if m > 3 else None)
            load_q(1, 1)
            for m in range(HEAD):
                load_tile(0, m, True)
            over_groups(sp, body)
            sp.wait_ge(S["otout"], START + 16 * NG)

        @block.gpsimd
        def _(pool):
            pool.wait_ge(S["preset"], START + 3)
            pool.wait_ge(S["tables"], START + 16 * 12)

            def diagonal(g, g2, part):
                if part == 0:
                    pool.wait_ge(S[f"qbd_load{g2}"], START + (g // 2 + 1) * 32)
                q = qbd[:, g2, part].rearrange("p h (b l) -> p (h b) l", l=8)
                nc.gpsimd.tensor_tensor(q, q, mask.unsqueeze(1).to_broadcast([P, HH * 16, 8]), ALU.mult).then_inc(S["qbd"], 1)

            def body(gg, g2, ahead):
                for m in range(NI):
                    _, cls = tile_at(gg % NI, USE[m])
                    pool.wait_ge(S[f"vrow{m % 4}"], START + (gg * 4 + m // 4 + 1) * 16)
                    pool.wait_ge(S["used"], START + gg * NI + max(m - 1, 0))
                    nc.gpsimd.tensor_tensor(vt[:, m % 2, :, 0:DK], vrow[:, m % 4, :].rearrange("p (h d) -> p h d", d=DK),
                                            rc[:, ds(cls, 1), :].to_broadcast([P, HH, DK]), ALU.add).then_inc(S["vt"], 1)
                    if ahead == 2 and m in (9, 11):
                        diagonal(gg + 2, g2, (m - 9) // 2)

            for g in range(2):
                for part in range(2):
                    diagonal(g, g, part)
            over_groups(pool, body)

        @block.tensor
        def _(pe):
            pe.wait_ge(S["tables"], START + 16 * 12)
            pe.wait_ge(S["preset"], START + 3)
            pe.wait_ge(S["split"], START + 6)

            def body(gg, g2, ahead):
                i, g, j2 = gg % NI, gg + 1, 1 - g2
                for m in range(NI - NX):
                    if ahead and m:
                        scores(pe, g, g % NI, j2, m)
                    values(pe, gg, i, g2, m)
                if ahead:
                    for m in range(NI - NX, NI):
                        scores(pe, g, g % NI, j2, m)
                values(pe, gg, i, g2, NI - 3)
                if ahead:
                    turn_max(pe, g)
                values(pe, gg, i, g2, NI - 2)
                if ahead:
                    spread_max(pe, g)
                values(pe, gg, i, g2, NI - 1)
                if ahead == 2:
                    scores(pe, gg + 2, (gg + 2) % NI, g2, 0)
                fold(pe, gg)

            for m in range(NI):
                scores(pe, 0, 0, 0, m)
            turn_max(pe, 0)
            spread_max(pe, 0)
            scores(pe, 1, 1, 1, 0)
            over_groups(pe, body)

        @block.scalar
        def _(act):
            def store_scores(g, g2, m, used):
                act.wait_ge(S["scored"], START + g * NI + m + 1)
                act.wait_ge(S["used"], START + used)
                nc.scalar.activation(slot(g2, SCORE[m]), spp[:, m % 2], ACT.Copy).then_inc(S["stored"], 1)

            def exps(gg, g2, m):
                k = USE[m]
                act.wait_ge(S["sub"], START + gg * NI + m + 1)
                if k in BANDS:
                    band = BANDS.index(k)
                    act.wait_ge(S["used"], START + used_before(gg, band))
                    nc.scalar.activation(pp2[:, band % 3, 0], slot(g2, k), ACT.Exp).then_inc(S["prob_hi"], 1)
                nc.scalar.activation(slot(g2, k), slot(g2, k), ACT.Exp).then_inc(S["prob"], 1)

            def max_out(g):
                act.wait_ge(S["mbp"], START + g + 1)
                act.wait_ge(S["sub"], START + g * NI)
                nc.scalar.activation(mb[:], spp[:, 1], ACT.Copy).then_inc(S["mb"], 1)

            def body(gg, g2, ahead):
                exps(gg, g2, 0)
                exps(gg, g2, 1)
                for m in range(NI - NX):
                    if ahead:
                        k = SCORE[m]
                        store_scores(gg + 1, 1 - g2, m, gg * NI + (0 if k in LAST else USE.index(k) + 1))
                    if m == 0:
                        exps(gg, g2, 2)
                    if m + 3 < NI:
                        exps(gg, g2, m + 3)
                if ahead:
                    for m in range(NI - NX, NI):
                        store_scores(gg + 1, 1 - g2, m, gg * NI + USE.index(SCORE[m]) + 1)
                    max_out(gg + 1)
                act.wait_ge(S["used"], START + (gg + 1) * NI)
                act.wait_ge(S["folded"], START + gg)
                nc.scalar.activation(pvs[:], pvp[:], ACT.Copy).then_inc(S["pvs"], 1)

            act.wait_ge(S["split"], START + 6)
            for m in range(NI):
                store_scores(0, 0, m, 0)
            max_out(0)
            over_groups(act, body)

        @block.vector
        def _(dve):
            def running_max(g, g2, m):
                dve.wait_ge(S["stored"], START + g * NI + m + 1)
                if m == 0:
                    dve.wait_ge(S["turned"], START + g)
                    nc.vector.tensor_copy(mx[:], slot(g2, SCORE[m])).then_inc(S["mxd"], 1)
                else:
                    dve.wait_ge(S["mxd"], START + g * NI + m)
                    nc.vector.tensor_tensor(mx[:], mx[:], slot(g2, SCORE[m]), ALU.max).then_inc(S["mxd"], 1)

            def subtract(gg, g2, m):
                if m == 0:
                    dve.wait_ge(S["mb"], START + gg + 1)
                nc.vector.tensor_tensor(slot(g2, USE[m]), slot(g2, USE[m]), mb[:], ALU.subtract).then_inc(S["sub"], 1)

            def low_part(gg, g2, m):
                k = USE[m]
                if k in BANDS:
                    band = BANDS.index(k)
                    dve.wait_ge(S["prob"], START + gg * NI + m + 1)
                    dve.wait_ge(S["used"], START + used_before(gg, band))
                    nc.vector.tensor_tensor(pp2[:, band % 3, 1], slot(g2, k), pp2[:, band % 3, 0],
                                            ALU.subtract).then_inc(S["prob_lo"], 1)

            def query_max(g):
                dve.wait_ge(S["turned"], START + g + 1)
                nc.vector.tensor_reduce(mcol[:], spp[:, 0].rearrange("p a h l -> p (a h l)").rearrange("p (c r) -> p c r", c=8),
                                        AX_X, ALU.max).then_inc(S["mcol"], 1)

            def head(gg, g2):
                for m in range(3):
                    subtract(gg, g2, m)
                low_part(gg, g2, 0)

            def body(gg, g2, ahead):
                g, j2 = gg + 1, 1 - g2
                for m in range(NI - 3):
                    subtract(gg, g2, m + 3)
                    low_part(gg, g2, m + 1)
                    if ahead and m:
                        running_max(g, j2, m - 1)
                low_part(gg, g2, NI - 2)
                if ahead:
                    running_max(g, j2, NI - 4)
                low_part(gg, g2, NI - 1)
                if ahead:
                    for m in range(NI - 3, NI):
                        running_max(g, j2, m)
                    query_max(g)
                dve.wait_ge(S["used"], START + (gg + 1) * NI)
                dve.wait_ge(S["folded"], START + gg)
                nc.vector.tensor_tensor(rom[:].rearrange("p b h l -> p (b h) l"), ro[:].rearrange("p a b h l -> p (a b h) l"),
                                        own.to_broadcast([P, P, 8]), ALU.mult).then_inc(S["rom"], 1)
                if ahead:
                    head(g, j2)
                dve.wait_ge(S["folded"], START + gg + 1)
                dve.wait_ge(S["otout"], START + gg * 16)
                nc.vector.reciprocal(otn[:], otp[:, 1, :]).then_inc(S["rden"], 1)
                dve.wait_ge(S["rden"], START + gg + 1)
                nc.vector.tensor_tensor(otn[:], otp[:, 0, :], otn[:], ALU.mult).then_inc(S["normed"], 1)

            nc.vector.memset(rc[:, 0, :], 0.0).then_inc(S["preset"], 1)
            nc.vector.memset(vt[:], 0.0).then_inc(S["preset"], 1)
            dve.wait_ge(S["preset"], START + 2)
            nc.vector.memset(vt[:, :, :, DK:DK + 1], 1.0).then_inc(S["preset"], 1)
            dve.wait_ge(S["tables"], START + 16 * 12)
            step = START
            for dst, src in ((tks[:], tk_whole), (tvs[:, :, 0:half_table], tv_whole), (tvs[:, :, half_table:], tv_whole)):
                if step == START + 4:
                    dve.wait_ge(S["tables2"], START + 16)
                nc.vector.tensor_copy(dst[:, 0], src).then_inc(S["split"], 1)
                dve.wait_ge(S["split"], step + 1)
                nc.vector.tensor_tensor(dst[:, 1], src, dst[:, 0], ALU.subtract).then_inc(S["split"], 1)
                step += 2
                dve.wait_ge(S["split"], step)
            own = cst[:, C_MASKV:C_MASKV + 8].unsqueeze(1)
            for m in range(NI):
                running_max(0, 0, m)
            query_max(0)
            head(0, 0)
            over_groups(dve, body)


def phase_out(nc, ins, dr, sem, sb, ps):
    wo, bo = sb("woA", [P, 2, D]), sb("boA", [P, D])
    ot = sb("ot", [P, 2, 2, CH, P])
    x, g, y = sb("x6", [P, 2, CH, D]), sb("g6", [P, 2, CH, D]), sb("y6", [P, 2, CH, D])
    pp = ps("p6", [P, CH, 512])
    S = {n: sem("g_" + n) for n in "weights load0 load1 proj biased gated out store0 store1".split()}
    xv, gv, ov = (t.rearrange("(c a p) n -> p c a n", a=CH, p=P) for t in (ins["x"], dr["g"], ins["out"]))

    with nc.Block() as block:
        @block.sync
        def _(sp):
            sp.dma_start(wo[:], ins["woAT"].rearrange("(k p) n -> p k n", p=P)).then_inc(S["weights"], 16)
            sp.dma_start(bo[:], ins["boA"].partition_broadcast(P)).then_inc(S["weights"], 16)
            for ch in range(NCH):
                u = ch % 2
                if ch >= 2:
                    sp.wait_ge(S["out"], ch - 1)
                b, i0 = ch // 4, (ch % 4) * CH
                for half in range(2):
                    r = (2 * b + half) * NI + i0
                    sp.dma_start(ot[:, u, half], dr["ot"][r:r + CH].rearrange("g p l -> p g l")).then_inc(S[f"load{u}"], 16)
                sp.dma_start(x[:, u], xv[:, ch]).then_inc(S[f"load{u}"], 16)
                sp.dma_start(g[:, u], gv[:, ch]).then_inc(S[f"load{u}"], 16)

        @block.tensor
        def _(pe):
            pe.wait_ge(S["weights"], 32)
            for ch in range(NCH):
                u = ch % 2
                pe.wait_ge(S[f"load{u}"], 64 * (ch // 2 + 1))
                if ch:
                    pe.wait_ge(S["biased"], ch)
                for a in range(CH):
                    for half in range(2):
                        last = nc.tensor.matmul(pp[:, a, 0:D], ot[:, u, half, a, :], wo[:, half, :], start=(half == 0), stop=(half == 1))
                last.then_inc(S["proj"], 1)

        @block.vector
        def _(dve):
            dve.wait_ge(S["weights"], 32)
            for ch in range(NCH):
                u = ch % 2
                dve.wait_ge(S["proj"], ch + 1)
                if ch >= 2:
                    dve.wait_ge(S[f"store{u}"], 16 * (ch // 2))
                nc.vector.tensor_tensor(y[:, u], pp[:, :, 0:D], bo[:].unsqueeze(1).to_broadcast([P, CH, D]), ALU.add).then_inc(S["biased"], 1)
                dve.wait_ge(S["biased"], ch + 1)
                nc.vector.tensor_tensor(y[:, u], y[:, u], g[:, u], ALU.mult).then_inc(S["gated"], 1)
                dve.wait_ge(S["gated"], ch + 1)
                nc.vector.tensor_tensor(y[:, u], y[:, u], x[:, u], ALU.add).then_inc(S["out"], 1)

        @block.scalar
        def _(act):
            for ch in range(NCH):
                act.wait_ge(S["out"], ch + 1)
                act.dma_start(ov[:, ch], y[:, ch % 2]).then_inc(S[f"store{ch % 2}"], 16)
            for u in range(2):
                act.wait_ge(S[f"store{u}"], 16 * (NCH // 2))


def build(nc, ins):
    def dram(name, shape, dt=F32):
        return nc.dram_tensor(name, shape, dt, kind="Internal").ap()

    def scoped(ctx):
        def sb(name, shape, dt=F32):
            return ctx.enter_context(nc.sbuf_tensor(name, shape, dt))

        def ps(name, shape, dt=F32):
            return ctx.enter_context(nc.psum_tensor(name, shape, dt))

        return sb, ps

    dr = {
        "qs": dram("q_parts", [NC * NI, TERMS * DK * W], BF16),
        "ks": dram("k_parts", [NC * NI, TERMS * DK * W], BF16),
        "qp": dram("q_pair", [NC * NI, 2, DK * W], FP16),
        "cs": dram("class_constants", [NC * NI, 2, PARTS, HH, P], BF16),
        "v": dram("v_rows", [TOK, D]),
        "tk": dram("key_table", [DK, SPAN]),
        "tv": dram("value_table", [SPAN, DK]),
        "disp": dram("dispatched", [TOK, D]),
        "yexp": dram("expert_rows", [TOK, D]),
        "g": dram("gate_rows", [TOK, D]),
        "ot": dram("attention_out", [NC * NI, P, P]),
    }
    with ExitStack() as whole:
        def sem(name):
            return whole.enter_context(nc.semaphore(name))

        with ExitStack() as gate_scope:
            sb, _ = scoped(gate_scope)
            dr["xn_all"] = dr["y1_all"] = sb("xn_all", [P, NT, D])
            dr["logits"] = sb("logits", [P, NT, E])
            dr["gate"] = sb("gate", [P, NT])
            dr["slot_u"], dr["back_u"] = sb("slot_u", [P, NT], U32), sb("back_u", [P, NT], U32)
            with ExitStack() as first:
                sb, _ = scoped(first)
                dr["qkv_all"] = sb("qkv_all", [P, NT, 3 * D])
                with ExitStack() as c:
                    phase_project(nc, ins, dr, sem, *scoped(c))
                with ExitStack() as c:
                    phase_pairs(nc, ins, dr, sem, *scoped(c))
            for phase in (phase_route, phase_experts, phase_gate):
                with ExitStack() as c:
                    phase(nc, ins, dr, sem, *scoped(c))
        for phase in (phase_attend, phase_out):
            with ExitStack() as c:
                phase(nc, ins, dr, sem, *scoped(c))


def kernel(**inputs):
    import numpy as np
    import concourse.bacc as bacc
    from concourse.bass_utils import run_bass_kernel_spmd

    a = {k: np.asarray(v) for k, v in inputs.items()}

    def half_heads(w):
        return w.reshape(-1, 2, HH, DK).transpose(0, 1, 3, 2).reshape(-1, D)

    def columns(b):
        return half_heads(b[None, :]).reshape(2, P).T

    consts = np.zeros((P, C_N), np.float32)
    p = np.arange(P)
    consts[p, C_ID + p] = 1
    consts[p, C_FOLD + 112 + p % 16] = 1
    for c in range(4):
        for d in range(DK):
            consts[32 * c + d, C_PICK + 64 + 16 * c + d] = 1
            consts[32 * c + DK, C_DEN + 64 + 16 * c + d] = 1
    consts[p, C_MASK + p // 16] = 1
    consts[p, C_MASKV + 7 - p // 16] = 1
    consts[:, C_TRI:C_TRI + P] = p[:, None] < p[None, :]
    consts[:, C_ONE:C_ONE + P] = 1
    consts[p, C_HEAD + p % HH] = 1
    consts[:, C_IOTA:C_IOTA + E] = E - np.arange(E)
    consts[:, C_CAPE:C_CAPE + E] = CAP * np.arange(E)

    sel = np.zeros((3, 2 * PARTS, W), np.uint16)
    sel[HI, :PARTS] = sel[LO, PARTS:] = 0x3F80

    host = {
        "x": a["L0_attn_x"].reshape(TOK, D),
        "wqT": half_heads(a["L0_attn_Wq"].T), "wkT": half_heads(a["L0_attn_Wk"].T), "wvT": a["L0_attn_Wv"].T,
        "wiT": a["L0_ffn_in_proj_w"].T, "woT": a["L0_ffn_out_proj_w"].T, "woAT": a["L0_attn_Wo"].T,
        "bqk": np.concatenate([columns(a["L0_attn_bq"]), columns(a["L0_attn_bk"])], 1),
        "bv": a["L0_attn_bv"], "bi": a["L0_ffn_in_proj_b"], "bo_f": a["L0_ffn_out_proj_b"], "boA": a["L0_attn_bo"],
        "rk": a["L0_attn_relative_k"], "rkT": a["L0_attn_relative_k"].T,
        "rv": a["L0_attn_relative_v"],
        "g1": a["L0_ffn_ln1_g"], "b1ln": a["L0_ffn_ln1_b"], "g2": a["L0_ffn_ln2_g"], "b2ln": a["L0_ffn_ln2_b"],
        "wg": a["L0_ffn_wg"], "w1T": a["L0_ffn_w1"].transpose(0, 2, 1), "w2": a["L0_ffn_w2"],
        "b1e": a["L0_ffn_b1"].reshape(E, FF // P, P).transpose(0, 2, 1), "b2e": a["L0_ffn_b2"], "consts": consts, "sel": sel,
    }
    nc = bacc.Bacc("TRN2", target_bir_lowering=False, num_devices=1)
    arrays, ins = {}, {}
    for name, v in host.items():
        arrays["in_" + name] = np.ascontiguousarray(v)
        ins[name] = nc.dram_tensor("in_" + name, v.shape, mybir.dt.from_np(v.dtype), kind="ExternalInput").ap()
    ins["out"] = nc.dram_tensor("out", (TOK, D), F32, kind="ExternalOutput").ap()
    build(nc, ins)
    r = run_bass_kernel_spmd(nc, [arrays], core_ids=[0])
    return r.results[0]["out"].reshape(B, L, D)
```

```python
from contextlib import ExitStack

import concourse.bass as bass
from concourse import mybir

F32 = mybir.dt.float32
BF16 = mybir.dt.bfloat16
FP16 = mybir.dt.float16
U32 = mybir.dt.uint32
U16 = mybir.dt.uint16
I32 = mybir.dt.int32
ALU = mybir.AluOpType
ACT = mybir.ActivationFunctionType
AX_X = mybir.AxisListType.X
ds = bass.ds

P = 128
B, L, D = 2, 2048, 256
TOK = B * L
NT = TOK // P
H, DK = 16, 16
HH = H // 2
NC = B * 2
NI = L // P
W = HH * P
MAXLEN = 256
REL = 2 * MAXLEN - 1
EPS = 1e-5
FH, FHD = 4, 64
E, FF, CAP = 8, 1024, TOK // 8
HK = FF // P // 4
CH = 4
NCH = NT // CH

BAND, HI, LO = 0, 1, 2
USE = [0, 3, 1, 4, 2, 5, -1, 6, -2, 7, -3, 8, 9, -4, -5, -6]
NX = 3
LAST = USE[-NX:]
SCORE = LAST + USE[:-NX]
BANDS = [k for k in USE if k < 3]
NB = len(BANDS)
LOWEST = -6 * P - (P - 1)
HIGHEST = 2 * P + (P - 1)
SPAN = HIGHEST - LOWEST + 1
TSW = SPAN - 7
TVU = SPAN - P + 1
TERMS = 6
PARTS = 3
VW = DK + 1
QROWS = TERMS * DK
ROWS = QROWS + 2 * PARTS
K_PARTS = (0, 0, 0, 1, 1, 2)
Q_PARTS = (0, 1, 2, 0, 1, 0)
PAIRS = [(0, 0), (0, 1), (1, 0)]

C_ID, C_FOLD, C_PICK, C_DEN, C_MASK, C_MASKV, C_TRI, C_ONE, C_HEAD, C_IOTA, C_CAPE = 0, 128, 368, 560, 752, 760, 768, 896, 1024, 1032, 1040
C_N = 1048

START = 3


def start_counts(nc, sems):
    with nc.Block() as block:
        @block.sync
        def _(sp):
            for s in sems.values():
                sp.sem_inc(s, START)


def phase_project(nc, ins, dr, sem, sb, ps):
    xn_all, qkv_all = dr["xn_all"], dr["qkv_all"]
    wq, wk, wv, wi = sb("wq", [P, 2, D]), sb("wk", [P, 2, D]), sb("wv", [P, 2, D]), sb("wi", [P, 2, 3 * D])
    bqk = sb("bqk", [P, 4])
    bv, bi = sb("bv", [P, D]), sb("bi", [P, 3 * D])
    cst = sb("cst1", [P, C_N])
    tc2 = sb("tc2", [P, 2])
    selc = sb("selc", [P, 2, HH])
    room = dr["shared"][:].rearrange("p (r a n) -> p r a n", a=CH, n=D)
    xc, xnc = room[:, 0:2], room[:, 2]
    xT = room[:, 3].rearrange("p a n -> p (a n)").rearrange("p (k l) -> p k l", k=2)
    qf = room[:, 4].rearrange("p a n -> p (a n)").rearrange("p (k l) -> p k l", k=2)
    stat, mv = sb("stat", [P, CH, 6]), sb("mv", [P, CH, 2])
    std, rstd = sb("std", [P, CH]), sb("rstd", [P, CH])
    pause = sb("pause", [P, 1])
    res = sb("res", [P, CH * P])
    pair = sb("pair", [P, 2, 2, CH * P], FP16)
    part = sb("part", [P, 2, PARTS, CH * P], BF16)
    cres = sb("cres", [2 * HH, CH * P])
    cf = sb("cf", [2 * HH, CH * P])
    cpart = sb("cpart", [2 * HH, PARTS, CH * P], BF16)
    vs = sb("vs", [P, 3, CH, 2, HH, VW])
    vrel = sb("vrel", [P, 2, DK])
    tp = ps("tp", [P, 2, CH * P])
    pq = ps("pq", [P, 2, CH * P])
    pc = ps("pc", [P, CH * P])
    pv = ps("pv", [P, D])
    pi = ps("pi", [P, 2, 512])

    S = {n: sem("a_" + n) for n in (
        "weights vones vclass xload0 xload1 stats aggr eps std rstd normed kept tp_done xT proj qf p0 r1 p1 p2 hi lo cmm cf c0 cr1 c1 c2 vmm vout "
        "imm iout qstore0 qstore1 cstore vstore selc tabl tabl2").split()}

    start_counts(nc, S)
    with nc.Block() as block:
        @block.sync
        def _(sp):
            for t, s in ((wq, "wqT"), (wk, "wkT"), (wv, "wvT"), (wi, "wiT")):
                sp.dma_start(t[:], ins[s].rearrange("(k p) n -> p k n", p=P)).then_inc(S["weights"], 16)
            sp.dma_start(bqk[:], ins["bqk"]).then_inc(S["weights"], 16)
            sp.dma_start(bv[:], ins["bv"].partition_broadcast(P)).then_inc(S["weights"], 16)
            sp.dma_start(bi[:], ins["bi"].partition_broadcast(P)).then_inc(S["weights"], 16)
            sp.dma_start(cst[:], ins["consts"]).then_inc(S["weights"], 16)
            for n, row in ((0, REL - 1), (1, 0)):
                src = bass.AP(ins["rk"].tensor, row * DK, [[1, DK], [0, HH], [1, 1]])
                sp.dma_start(tc2[:, n:n + 1], src).then_inc(S["weights"], 16)
            for n, row in ((0, REL - 1), (1, 0)):
                sp.dma_start(vrel[:, n, :], bass.AP(ins["rv"].tensor, row * DK, [[0, P], [1, DK]])).then_inc(S["weights"], 16)
            tk, rkT = dr["tk"], ins["rkT"]
            lo, mid = 129, 129 + REL
            sp.dma_start(tk[:, lo:mid], rkT).then_inc(S["tabl"], 16)
            sp.dma_start(tk[:, mid:mid + REL], rkT).then_inc(S["tabl"], 16)
            sp.dma_start(tk[:, 0:lo], bass.AP(rkT.tensor, 0, [[REL, DK], [0, lo], [1, 1]])).then_inc(S["tabl"], 16)
            sp.dma_start(tk[:, mid + REL:SPAN],
                         bass.AP(rkT.tensor, REL - 1, [[REL, DK], [0, P], [1, 1]])).then_inc(S["tabl"], 16)
            tv, rv = dr["tv"], ins["rv"]
            sp.dma_start(tv[0:lo, :], bass.AP(rv.tensor, 0, [[0, lo], [1, DK]])).then_inc(S["tabl"], 16)
            sp.dma_start(tv[lo:mid, :], rv).then_inc(S["tabl"], 16)
            sp.dma_start(tv[mid:mid + REL, :], rv).then_inc(S["tabl"], 16)
            sp.dma_start(tv[mid + REL:SPAN, :],
                         bass.AP(rv.tensor, (REL - 1) * DK, [[0, P], [1, DK]])).then_inc(S["tabl"], 16)
            xv = ins["x"].rearrange("(c a p) n -> p c a n", a=CH, p=P)

            def load(ch, u):
                sp.wait_ge(S["kept"], START + ch - 1)
                sp.dma_start(xc[:, u], xv[:, ds(ch, 1)].rearrange("p c a n -> p (c a) n")).then_inc(S[f"xload{u}"], 16)

            def chunk(ch, u, more):
                if more:
                    load(ch + 1, 1 - u)
                for n in range(4):
                    ready = ch * 4 + n + 1
                    sp.wait_ge(S["p2"], START + ready)
                    dst = dr["qs"] if n < 2 else dr["ks"]
                    row = (ch // 4) * (2 * NI) + (n % 2) * NI + (ch % 4) * CH
                    for u6, q in enumerate(Q_PARTS if n < 2 else K_PARTS):
                        d = dst[ds(row, CH), u6 * W * DK:(u6 + 1) * W * DK].rearrange("i (p l) -> p i l", l=P)
                        sp.dma_start(d, part[:, n % 2, q, :].rearrange("p (i l) -> p i l", l=P)).then_inc(S[f"qstore{n % 2}"], 16)
                    if n < 2:
                        for q in range(2):
                            d = dr["qp"][ds(row, CH), q, :].rearrange("i (p l) -> p i l", l=P)
                            sp.dma_start(d, pair[:, n, q, :].rearrange("p (i l) -> p i l", l=P)).then_inc(S[f"qstore{n % 2}"], 16)
                        sp.wait_ge(S["c2"], START + ch * 2 + n + 1)
                        for q in range(PARTS):
                            for cl in range(2):
                                d = dr["cs"][ds(row, CH), cl, q, :, :].rearrange("i h l -> h i l")
                                sp.dma_start(d, cpart[cl * HH:(cl + 1) * HH, q, :].rearrange("h (i l) -> h i l", l=P)).then_inc(S["cstore"], 16)
                sp.wait_ge(S["vclass"], START + (ch + 1) * 2)
                for cl in range(3):
                    for half in range(2):
                        tile = (ch // 4) * (2 * NI) + half * NI + (ch % 4) * CH
                        d = dr["v"][cl, ds(tile, CH)].rearrange("a p n -> p a n")
                        sp.dma_start(d, vs[:, cl, :, half].rearrange("p a h d -> p a (h d)")).then_inc(S["vstore"], 16)

            sp.dma_start(xc[:, 0], xv[:, 0]).then_inc(S["xload0"], 16)
            with sp.Fori(0, NCH // 2 - 1) as h:
                for u in range(2):
                    chunk(h * 2 + u, u, True)
            chunk(NCH - 2, 0, True)
            chunk(NCH - 1, 1, False)
            sp.wait_ge(S["tabl"], START + 16 * 8)
            for n in range(2):
                sp.wait_ge(S[f"qstore{n}"], START + 224 * NCH)
            sp.wait_ge(S["cstore"], START + 16 * 12 * NCH)
            sp.wait_ge(S["vstore"], START + 96 * NCH)

        @block.vector
        def _(dve):
            dve.wait_ge(S["weights"], START + 16 * 12)
            for n in range(2):
                nc.vector.tensor_scalar(selc[:, n, :], cst[:, C_HEAD:C_HEAD + HH], tc2[:, n:n + 1], None, ALU.mult).then_inc(S["selc"], 1)
            def normalise(ch, u):
                dve.wait_ge(S[f"xload{u}"], START + (ch // 2) * 16 + 16)
                for a in range(CH):
                    nc.vector.bn_stats(stat[:, a, :], xc[:, u, a, :]).then_inc(S["stats"], 1)
                dve.wait_ge(S["stats"], START + ch * CH + CH)
                nc.vector.memset(pause[:], 0.0)
                for a in range(CH):
                    nc.vector.bn_aggr(mv[:, a, :], stat[:, a, :]).then_inc(S["aggr"], 1)
                dve.wait_ge(S["aggr"], START + ch * CH + CH)
                nc.vector.tensor_scalar(std[:], mv[:, :, 1], EPS, None, ALU.add).then_inc(S["eps"], 1)
                dve.wait_ge(S["std"], START + ch + 1)
                nc.vector.reciprocal(rstd[:], std[:]).then_inc(S["rstd"], 1)
                dve.wait_ge(S["rstd"], START + ch + 1)
                dve.wait_ge(S["tp_done"], START + ch)
                dve.wait_ge(S["kept"], START + ch)
                for a in range(CH):
                    nc.vector.tensor_scalar(xnc[:, a, :], xc[:, u, a, :], mv[:, a, 0:1], rstd[:, a:a + 1],
                                            ALU.subtract, ALU.mult).then_inc(S["normed"], 1)

            def split(ch, n):
                k = ch * 4 + n
                dve.wait_ge(S["proj"], START + k + 1)
                dve.wait_ge(S[f"qstore{n % 2}"], START + ch * 224 + (128 if n >= 2 else 0))
                dve.wait_ge(S["p2"], START + k)
                if n < 2:
                    nc.vector.tensor_scalar(qf[:, n % 2, :], pq[:, n % 2, :], bqk[:, n:n + 1], None, ALU.add).then_inc(S["qf"], 1)
                else:
                    nc.vector.tensor_scalar(qf[:, n % 2, :], pq[:, n % 2, :], bqk[:, n:n + 1], DK ** -0.5,
                                            ALU.add, ALU.mult).then_inc(S["qf"], 1)
                dve.wait_ge(S["p0"], START + k + 1)
                nc.vector.tensor_tensor(res[:], qf[:, n % 2, :], part[:, n % 2, 0, :], ALU.subtract).then_inc(S["r1"], 1)
                if n < 2:
                    dve.wait_ge(S["hi"], START + ch * 2 + n + 1)
                    nc.vector.tensor_tensor(pair[:, n, 1, :], qf[:, n, :], pair[:, n, 0, :], ALU.subtract).then_inc(S["lo"], 1)
                dve.wait_ge(S["p1"], START + k + 1)
                nc.vector.tensor_tensor(part[:, n % 2, 2, :], res[:], part[:, n % 2, 1, :], ALU.subtract).then_inc(S["p2"], 1)

            def classes(ch, n):
                k = ch * 2 + n
                dve.wait_ge(S["cmm"], START + k + 1)
                dve.wait_ge(S["cstore"], START + k * 96)
                dve.wait_ge(S["c2"], START + k)
                nc.vector.tensor_copy(cf[:], pc[0:2 * HH, :]).then_inc(S["cf"], 1)
                dve.wait_ge(S["cf"], START + k + 1)
                nc.vector.tensor_copy(cpart[:, 0, :], cf[:]).then_inc(S["c0"], 1)
                dve.wait_ge(S["c0"], START + k + 1)
                nc.vector.tensor_tensor(cres[:], cf[:], cpart[:, 0, :], ALU.subtract).then_inc(S["cr1"], 1)
                dve.wait_ge(S["cr1"], START + k + 1)
                nc.vector.tensor_copy(cpart[:, 1, :], cres[:]).then_inc(S["c1"], 1)
                dve.wait_ge(S["c1"], START + k + 1)
                nc.vector.tensor_tensor(cpart[:, 2, :], cres[:], cpart[:, 1, :], ALU.subtract).then_inc(S["c2"], 1)

            def rows(ch, a):
                dve.wait_ge(S["vmm"], START + ch * CH + a + 1)
                if a == 0:
                    dve.wait_ge(S["vstore"], START + ch * 96)
                nc.vector.tensor_tensor(vs[:, 0, a, :, :, 0:DK], pv[:].rearrange("p (g h d) -> p g h d", g=2, d=DK),
                                        bv[:].rearrange("p (g h d) -> p g h d", g=2, d=DK), ALU.add).then_inc(S["vout"], 1)
                dve.wait_ge(S["imm"], START + ch * CH + a + 1)
                out = qkv_all[:, ds(ch * CH + a, 1), :].rearrange("p a n -> p (a n)")
                nc.vector.tensor_tensor(out[:, 0:512], pi[:, 0, :], bi[:, 0:512], ALU.add)
                nc.vector.tensor_tensor(out[:, 512:768], pi[:, 1, 0:256], bi[:, 512:768], ALU.add).then_inc(S["iout"], 1)

            def chunk(ch, u, more):
                for n in range(4):
                    split(ch, n)
                    if n < 2:
                        classes(ch, n)
                    rows(ch, n)
                    if n == 1 and more:
                        normalise(ch + 1, 1 - u)

            nc.vector.memset(vs[:], 1.0).then_inc(S["vones"], 1)
            dve.wait_ge(S["vones"], START + 1)
            normalise(0, 0)
            with dve.Fori(0, NCH // 2 - 1) as h:
                for u in range(2):
                    chunk(h * 2 + u, u, True)
            chunk(NCH - 2, 0, True)
            chunk(NCH - 1, 1, False)

        @block.scalar
        def _(act):
            def spread(ch):
                act.wait_ge(S["eps"], START + ch + 1)
                nc.scalar.activation(std[:], std[:], ACT.Sqrt).then_inc(S["std"], 1)

            def turned(ch):
                act.wait_ge(S["tp_done"], START + ch + 1)
                act.wait_ge(S["imm"], START + ch * CH)
                for k in range(2):
                    nc.scalar.activation(xT[:, k, :], tp[:, k, :], ACT.Copy).then_inc(S["xT"], 1)

            def split(ch, n):
                act.wait_ge(S["qf"], START + ch * 4 + n + 1)
                nc.scalar.activation(part[:, n % 2, 0, :], qf[:, n % 2, :], ACT.Copy).then_inc(S["p0"], 1)
                if n < 2:
                    nc.scalar.activation(pair[:, n, 0, :], qf[:, n, :], ACT.Copy).then_inc(S["hi"], 1)
                act.wait_ge(S["r1"], START + ch * 4 + n + 1)
                nc.scalar.activation(part[:, n % 2, 1, :], res[:], ACT.Copy).then_inc(S["p1"], 1)

            def chunk(ch, more):
                for n in range(4):
                    split(ch, n)
                    if n == 1 and more:
                        spread(ch + 1)
                if more:
                    turned(ch + 1)

            spread(0)
            turned(0)
            with act.Fori(0, NCH - 1) as ch:
                chunk(ch, True)
            chunk(NCH - 1, False)

        @block.gpsimd
        def _(pool):
            def keep(ch):
                pool.wait_ge(S["normed"], START + ch * CH + CH)
                nc.gpsimd.tensor_copy(xn_all[:, ds(ch * CH, CH), :], xnc[:]).then_inc(S["kept"], 1)

            def classes(ch):
                pool.wait_ge(S["vout"], START + ch * CH + CH)
                heads = [P, CH * 2 * HH, DK]
                for n in range(2):
                    src = vs[:, 0].rearrange("p a g h d -> p (a g h) d")[:, :, 0:DK]
                    dst = vs[:, n + 1].rearrange("p a g h d -> p (a g h) d")[:, :, 0:DK]
                    nc.gpsimd.tensor_tensor(dst, src, vrel[:, n:n + 1, :].to_broadcast(heads), ALU.add).then_inc(S["vclass"], 1)

            pool.wait_ge(S["vones"], START + 1)
            pool.wait_ge(S["weights"], START + 16 * 12)
            keep(0)
            with pool.Fori(0, NCH - 1) as ch:
                keep(ch + 1)
                classes(ch)
            classes(NCH - 1)

        @block.tensor
        def _(pe):
            pe.wait_ge(S["weights"], START + 16 * 12)
            pe.wait_ge(S["selc"], START + 2)
            ident = cst[:, C_ID:C_ID + P]

            def turn(ch):
                pe.wait_ge(S["normed"], START + ch * CH + CH)
                pe.wait_ge(S["xT"], START + ch * 2)
                for k in range(2):
                    for a in range(CH):
                        last = nc.tensor.transpose(tp[:, k, a * P:(a + 1) * P], xnc[:, a, k * P:(k + 1) * P], ident)
                last.then_inc(S["tp_done"], 1)

            def project(ch, n):
                w, half = (wq, n) if n < 2 else (wk, n - 2)
                pe.wait_ge(S["qf"], START + ch * 4 + (n - 1 if n > 1 else 0))
                for k in range(2):
                    last = nc.tensor.matmul(pq[:, n % 2, :], w[:, k, half * P:(half + 1) * P], xT[:, k, :],
                                            start=(k == 0), stop=(k == 1))
                last.then_inc(S["proj"], 1)

            def classes(ch, n):
                pe.wait_ge(S["qf"], START + ch * 4 + n + 1)
                pe.wait_ge(S["cf"], START + ch * 2 + n)
                nc.tensor.matmul(pc[0:2 * HH, :], selc[:].rearrange("p c h -> p (c h)"), qf[:, n % 2, :],
                                 start=True, stop=True).then_inc(S["cmm"], 1)

            def rows(ch, a):
                pe.wait_ge(S["vout"], START + ch * CH + a)
                for k in range(2):
                    last = nc.tensor.matmul(pv[:], xT[:, k, a * P:(a + 1) * P], wv[:, k, :], start=(k == 0), stop=(k == 1))
                last.then_inc(S["vmm"], 1)
                pe.wait_ge(S["iout"], START + ch * CH + a)
                for c in range(2):
                    n = 512 if c == 0 else 256
                    for k in range(2):
                        last = nc.tensor.matmul(pi[:, c, 0:n], xT[:, k, a * P:(a + 1) * P], wi[:, k, c * 512:c * 512 + n],
                                                start=(k == 0), stop=(k == 1))
                last.then_inc(S["imm"], 1)

            def chunk(ch, more):
                pe.wait_ge(S["xT"], START + ch * 2 + 2)
                project(ch, 0)
                project(ch, 1)
                classes(ch, 0)
                rows(ch, 0)
                classes(ch, 1)
                project(ch, 2)
                rows(ch, 1)
                project(ch, 3)
                rows(ch, 2)
                if more:
                    turn(ch + 1)
                rows(ch, 3)

            turn(0)
            with pe.Fori(0, NCH - 1) as ch:
                chunk(ch, True)
            chunk(NCH - 1, False)


def phase_pairs(nc, ins, dr, sem, sb, ps):
    xn_all, qkv_all, y1_all, logits = dr["xn_all"], dr["qkv_all"], dr["y1_all"], dr["logits"]
    wo, wg = sb("wo2", [P, 2, D]), sb("wg2", [P, 2, E])
    bo, g1, b1 = sb("bo2", [P, D]), sb("g1", [P, D]), sb("b1_", [P, D])
    cst = sb("cst2", [P, P])
    zero = sb("zero", [P, D])
    prod = sb("prod", [P, 2, 2, D])
    s = sb("s", [P, 2, 2, FH])
    m = sb("m", [P, 2, FH])
    r = sb("r", [P, 2, FH])
    pv_ = sb("pvp", [P, 2, 2, D])
    o = sb("o", [P, 2, D])
    oT = sb("oT", [P, 2, 2, P])
    z = sb("z", [P, 2, D])
    stat, mv = sb("stat2", [P, 2, 6]), sb("mv2", [P, 2, 2])
    std, rstd = sb("std2", [P, 2]), sb("rstd2", [P, 2])
    y1 = sb("y1", [P, 2, D])
    pause = sb("pause2", [P, 1])
    y1T = sb("y1T", [P, 2, 2, P])
    tp = ps("tp2", [P, 2, 2, P])
    po = ps("po", [P, 2, D])
    ty = ps("ty", [P, 2, 2, P])
    pl = ps("pl", [P, 2, E])
    w_all, b_all = dr["w_all"], dr["b_all"]
    w1 = sb("w1e", [P, 2, HK, D])
    w2 = sb("w2e", [P, 2, HK, D])
    be1 = sb("b1e", [P, 2, HK])
    pw, pb = ps("pw", [P, 2, 512]), ps("pb", [1, 512])

    S = {n: sem("b_" + n) for n in (
        "weights prod0 prod1 s0 s1 max diff exp sum rec prob vprod o tp oT proj z0 z1 stats aggr eps std rstd n0 n1 y1 kept "
        "ty y1T logit lout zset zeroed w0 w1 wmm wout bout").split()}

    start_counts(nc, S)
    with nc.Block() as block:
        @block.sync
        def _(sp):
            sp.dma_start(wo[:], ins["woT"].rearrange("(k p) n -> p k n", p=P)).then_inc(S["weights"], 16)
            sp.dma_start(wg[:], ins["wg"].rearrange("(k p) n -> p k n", p=P)).then_inc(S["weights"], 16)
            for t, n in ((bo, "bo_f"), (g1, "g1"), (b1, "b1ln")):
                sp.dma_start(t[:], ins[n].partition_broadcast(P)).then_inc(S["weights"], 16)
            sp.dma_start(cst[:], ins["consts"][:, C_ID:C_ID + P]).then_inc(S["weights"], 16)
            sp.dma_start(b_all[:], ins["b2e"].rearrange("(a e) n -> a e n", a=1)).then_inc(S["weights"], 16)
            sp.wait_ge(S["zset"], START + 1)
            for t in range(NT):
                sp.dma_start(dr["disp"][t * P:(t + 1) * P, :], zero[:]).then_inc(S["zeroed"], 16)
            with sp.Fori(0, E) as e:
                for q in range(4):
                    sp.wait_ge(S["wmm"], START + e * 4 + max(q - 1, 0))
                    for t, n in ((w1, "w1T"), (w2, "w2")):
                        src = ins[n][ds(e, 1), q * HK * P:(q + 1) * HK * P, :].rearrange("e (c p) n -> p (e c) n", p=P)
                        sp.dma_start(t[:, q % 2], src).then_inc(S[f"w{q % 2}"], 16)
                    src = ins["b1e"][ds(e, 1), :, q * HK:(q + 1) * HK].rearrange("e p c -> (e p) c")
                    sp.dma_start(be1[:, q % 2], src).then_inc(S[f"w{q % 2}"], 16)
            sp.wait_ge(S["zeroed"], START + 16 * NT)

        @block.vector
        def _(dve):
            nc.vector.memset(zero[:], 0.0).then_inc(S["zset"], 1)
            dve.wait_ge(S["weights"], START + 16 * 7)
            kv = qkv_all[:].rearrange("p (b t) n -> p b t n", b=2)
            def attention(t):
                for b in range(2):
                    q = kv[:, b, ds(t, 1), 0:D]
                    for c in range(2):
                        nc.vector.tensor_tensor(prod[:, b, c, :].unsqueeze(1), q, kv[:, c, ds(t, 1), D:2 * D], ALU.mult).then_inc(S[f"prod{b}"], 1)
                for b in range(2):
                    dve.wait_ge(S[f"prod{b}"], START + t * 2 + 2)
                    dve.wait_ge(S["vprod"], START + t * 4)
                    nc.vector.tensor_reduce(s[:, b].rearrange("p c h -> p (c h)"),
                                            prod[:, b].rearrange("p c (h d) -> p (c h) d", h=FH), AX_X, ALU.add).then_inc(S[f"s{b}"], 1)
                for b in range(2):
                    dve.wait_ge(S[f"s{b}"], START + t + 1)
                nc.vector.tensor_tensor(m[:], s[:, :, 0, :], s[:, :, 1, :], ALU.max).then_inc(S["max"], 1)
                dve.wait_ge(S["max"], START + t + 1)
                for c in range(2):
                    nc.vector.tensor_tensor(s[:, :, c, :], s[:, :, c, :], m[:], ALU.subtract).then_inc(S["diff"], 1)
                dve.wait_ge(S["exp"], START + t + 1)
                nc.vector.tensor_tensor(m[:], s[:, :, 0, :], s[:, :, 1, :], ALU.add).then_inc(S["sum"], 1)
                dve.wait_ge(S["sum"], START + t + 1)
                nc.vector.reciprocal(r[:], m[:]).then_inc(S["rec"], 1)
                dve.wait_ge(S["rec"], START + t + 1)
                for c in range(2):
                    nc.vector.tensor_tensor(s[:, :, c, :], s[:, :, c, :], r[:], ALU.mult).then_inc(S["prob"], 1)

            def finish(t):
                dve.wait_ge(S["proj"], START + t + 1)
                dve.wait_ge(S["y1"], START + t)
                nc.vector.tensor_tensor(z[:], po[:], bo[:].unsqueeze(1).to_broadcast([P, 2, D]), ALU.add).then_inc(S["z0"], 1)
                dve.wait_ge(S["z0"], START + t + 1)
                xv = xn_all[:].rearrange("p (b t) n -> p b t n", b=2)
                for b in range(2):
                    nc.vector.tensor_tensor(z[:, b:b + 1, :], z[:, b:b + 1, :], xv[:, b, ds(t, 1), :], ALU.add).then_inc(S["z1"], 1)
                for b in range(2):
                    dve.wait_ge(S["z1"], START + t * 2 + b + 1)
                    nc.vector.bn_stats(stat[:, b, :], z[:, b, :]).then_inc(S["stats"], 1)
                dve.wait_ge(S["stats"], START + t * 2 + 2)
                nc.vector.memset(pause[:], 0.0)
                for b in range(2):
                    nc.vector.bn_aggr(mv[:, b, :], stat[:, b, :]).then_inc(S["aggr"], 1)
                dve.wait_ge(S["aggr"], START + t * 2 + 2)
                nc.vector.tensor_scalar(std[:], mv[:, :, 1], EPS, None, ALU.add).then_inc(S["eps"], 1)
                dve.wait_ge(S["std"], START + t + 1)
                nc.vector.reciprocal(rstd[:], std[:]).then_inc(S["rstd"], 1)
                dve.wait_ge(S["rstd"], START + t + 1)
                for b in range(2):
                    nc.vector.tensor_scalar(z[:, b, :], z[:, b, :], mv[:, b, 0:1], rstd[:, b:b + 1],
                                            ALU.subtract, ALU.mult).then_inc(S["n0"], 1)
                dve.wait_ge(S["n0"], START + t * 2 + 2)
                nc.vector.tensor_tensor(z[:], z[:], g1[:].unsqueeze(1).to_broadcast([P, 2, D]), ALU.mult).then_inc(S["n1"], 1)
                dve.wait_ge(S["n1"], START + t + 1)
                dve.wait_ge(S["kept"], START + t * 2)
                dve.wait_ge(S["ty"], START + t)
                nc.vector.tensor_tensor(y1[:], z[:], b1[:].unsqueeze(1).to_broadcast([P, 2, D]), ALU.add).then_inc(S["y1"], 1)

            def expert(e):
                dve.wait_ge(S["wmm"], START + e * 4 + 4)
                nc.vector.tensor_tensor(b_all[:, ds(e, 1), :].rearrange("p e n -> p (e n)"), pb[0:1, 0:D],
                                        b_all[:, ds(e, 1), :].rearrange("p e n -> p (e n)"), ALU.add).then_inc(S["bout"], 1)
                nc.vector.tensor_copy(w_all[:, ds(e, 1)].rearrange("p e k n -> p (e k) n"), pw[:, :, 0:D]).then_inc(S["wout"], 1)

            attention(0)
            with dve.Fori(0, NI // 2 - 1) as h:
                for u in range(2):
                    attention(h * 2 + u + 1)
                    finish(h * 2 + u)
                expert(h * 1)
            attention(NI - 1)
            finish(NI - 2)
            finish(NI - 1)
            expert(E - 1)

        @block.gpsimd
        def _(pool):
            kv = qkv_all[:].rearrange("p (b t) n -> p b t n", b=2)
            def weigh(t):
                pool.wait_ge(S["prob"], START + t * 2 + 2)
                for b in range(2):
                    for c in range(2):
                        nc.gpsimd.tensor_tensor(pv_[:, b, c, :].rearrange("p (h d) -> p h d", h=FH),
                                                kv[:, c, ds(t, 1), 2 * D:3 * D].rearrange("p t (h d) -> p (t h) d", h=FH),
                                                s[:, b, c, :].unsqueeze(2).to_broadcast([P, FH, FHD]), ALU.mult).then_inc(S["vprod"], 1)
                pool.wait_ge(S["vprod"], START + t * 4 + 4)
                pool.wait_ge(S["tp"], START + t)
                nc.gpsimd.tensor_tensor(o[:], pv_[:, :, 0, :], pv_[:, :, 1, :], ALU.add).then_inc(S["o"], 1)

            def keep(t):
                pool.wait_ge(S["y1"], START + t + 1)
                yv = y1_all[:].rearrange("p (b t) n -> p b t n", b=2)
                for b in range(2):
                    nc.gpsimd.tensor_copy(yv[:, b, ds(t, 1), :], y1[:, b:b + 1, :]).then_inc(S["kept"], 1)

            weigh(0)
            with pool.Fori(0, NI - 1) as t:
                weigh(t + 1)
                keep(t)
            keep(NI - 1)

        @block.scalar
        def _(act):
            lv = logits[:].rearrange("p (b t) e -> p b t e", b=2)

            def exps(t):
                act.wait_ge(S["diff"], START + t * 2 + 2)
                nc.scalar.activation(s[:], s[:], ACT.Exp, scale=FHD ** -0.5).then_inc(S["exp"], 1)

            def attended(t):
                act.wait_ge(S["tp"], START + t + 1)
                act.wait_ge(S["proj"], START + t)
                nc.scalar.activation(oT[:], tp[:], ACT.Copy).then_inc(S["oT"], 1)

            def spread(t):
                act.wait_ge(S["eps"], START + t + 1)
                nc.scalar.activation(std[:], std[:], ACT.Sqrt).then_inc(S["std"], 1)

            def routed(t):
                act.wait_ge(S["ty"], START + t + 1)
                act.wait_ge(S["logit"], START + t)
                nc.scalar.activation(y1T[:], ty[:], ACT.Copy).then_inc(S["y1T"], 1)
                act.wait_ge(S["logit"], START + t + 1)
                for b in range(2):
                    nc.scalar.activation(lv[:, b, ds(t, 1), :], pl[:, b:b + 1, :], ACT.Copy).then_inc(S["lout"], 1)

            exps(0)
            attended(0)
            exps(1)
            spread(0)
            attended(1)
            with act.Fori(0, NI - 2) as t:
                exps(t + 2)
                spread(t + 1)
                routed(t)
                attended(t + 2)
            spread(NI - 1)
            routed(NI - 2)
            routed(NI - 1)

        @block.tensor
        def _(pe):
            pe.wait_ge(S["weights"], START + 16 * 7)

            def project(t):
                pe.wait_ge(S["o"], START + t + 1)
                pe.wait_ge(S["oT"], START + t)
                for b in range(2):
                    for k in range(2):
                        last = nc.tensor.transpose(tp[:, b, k, :], o[:, b, k * P:(k + 1) * P], cst[:])
                last.then_inc(S["tp"], 1)
                pe.wait_ge(S["oT"], START + t + 1)
                pe.wait_ge(S["z0"], START + t)
                for b in range(2):
                    for k in range(2):
                        last = nc.tensor.matmul(po[:, b, :], oT[:, b, k, :], wo[:, k, :], start=(k == 0), stop=(k == 1))
                last.then_inc(S["proj"], 1)

            def route(t):
                pe.wait_ge(S["y1"], START + t + 1)
                pe.wait_ge(S["y1T"], START + t)
                for b in range(2):
                    for k in range(2):
                        last = nc.tensor.transpose(ty[:, b, k, :], y1[:, b, k * P:(k + 1) * P], cst[:])
                last.then_inc(S["ty"], 1)
                pe.wait_ge(S["y1T"], START + t + 1)
                pe.wait_ge(S["lout"], START + t * 2)
                for b in range(2):
                    for k in range(2):
                        last = nc.tensor.matmul(pl[:, b, :], y1T[:, b, k, :], wg[:, k, :], start=(k == 0), stop=(k == 1))
                last.then_inc(S["logit"], 1)

            def expert(e, half):
                for q in (2 * half, 2 * half + 1):
                    u = q % 2
                    pe.wait_ge(S[f"w{u}"], START + e * 96 + (q // 2) * 48 + 48)
                    if q == 0:
                        pe.wait_ge(S["bout"], START + e)
                        pe.wait_ge(S["wout"], START + e)
                    for c in range(HK):
                        first, end = q == 0 and c == 0, q == 3 and c == HK - 1
                        nc.tensor.matmul(pb[0:1, 0:D], be1[:, u, c:c + 1], w2[:, u, c, :],
                                         start=first, stop=end, skip_group_check=True)
                        for k in range(2):
                            last = nc.tensor.matmul(pw[:, k, 0:D], w1[:, u, c, k * P:(k + 1) * P], w2[:, u, c, :],
                                                    start=first, stop=end, skip_group_check=True)
                    last.then_inc(S["wmm"], 1)

            project(0)
            with pe.Fori(0, NI // 2 - 1) as h:
                for u in range(2):
                    project(h * 2 + u + 1)
                    expert(h * 1, u)
                    route(h * 2 + u)
            project(NI - 1)
            expert(E - 1, 0)
            route(NI - 2)
            expert(E - 1, 1)
            route(NI - 1)


def phase_route(nc, ins, dr, sem, sb, ps):
    y1_all, logits, gate, slot_u, back_u = dr["y1_all"], dr["logits"], dr["gate"], dr["slot_u"], dr["back_u"]
    n = [P, NT, E]
    cst = sb("cst3", [P, C_N])
    mx, rec = sb("mx", [P, NT]), sb("rec", [P, NT])
    ex, hot, rank = sb("ex", n), sb("hot", n), sb("rank", n)
    pre, tot = sb("pre", n), sb("tot", [P, E, 2 * NT])
    tot2 = sb("tot2", [P, E, 2 * NT])
    loc, idx, keep, slot = sb("loc", [P, NT]), sb("idx", [P, NT]), sb("keep", [P, NT]), sb("slot", [P, NT])
    tmp = sb("tmp", [P, NT])
    pp, pt = ps("pp", n), ps("pt", n)
    s_cst, s_v, s_exp, s_hot, s_cum, s_sc = sem("c_cst"), sem("c_steps"), sem("c_exp"), sem("c_hot"), sem("c_cum"), sem("c_scattered")
    s_slot = sem("c_slots")

    with nc.Block() as block:
        @block.sync
        def _(sp):
            sp.dma_start(cst[:], ins["consts"]).then_inc(s_cst, 16)

        @block.scalar
        def _(act):
            act.wait_ge(s_v, 2)
            nc.scalar.activation(ex[:], ex[:], ACT.Exp).then_inc(s_exp, 1)

        @block.tensor
        def _(pe):
            pe.wait_ge(s_cst, 16)
            pe.wait_ge(s_hot, 1)
            nc.tensor.matmul(pp[:], cst[:, C_TRI:C_TRI + P], hot[:], start=True, stop=True)
            nc.tensor.matmul(pt[:], cst[:, C_ONE:C_ONE + P], hot[:], start=True, stop=True).then_inc(s_cum, 1)

        @block.vector
        def _(dve):
            step = [0]

            def done(ins_):
                step[0] += 1
                ins_.then_inc(s_v, 1)
                dve.wait_ge(s_v, step[0])

            def wide(t):
                return t[:].unsqueeze(2).to_broadcast(n)

            done(nc.vector.tensor_reduce(mx[:], logits[:], AX_X, ALU.max))
            done(nc.vector.tensor_tensor(ex[:], logits[:], wide(mx), ALU.subtract))
            dve.wait_ge(s_exp, 1)
            done(nc.vector.tensor_reduce(tmp[:], ex[:], AX_X, ALU.add))
            done(nc.vector.reciprocal(rec[:], tmp[:]))
            done(nc.vector.tensor_reduce(mx[:], ex[:], AX_X, ALU.max))
            done(nc.vector.tensor_tensor(gate[:], mx[:], rec[:], ALU.mult))
            done(nc.vector.tensor_tensor(hot[:], ex[:], wide(mx), ALU.is_ge))
            dve.wait_ge(s_cst, 16)
            done(nc.vector.tensor_tensor(rank[:], hot[:], cst[:, C_IOTA:C_IOTA + E].unsqueeze(1).to_broadcast(n), ALU.mult))
            done(nc.vector.tensor_reduce(mx[:], rank[:], AX_X, ALU.max))
            nc.vector.tensor_tensor(hot[:], cst[:, C_IOTA:C_IOTA + E].unsqueeze(1).to_broadcast(n), wide(mx),
                                    ALU.is_equal).then_inc(s_hot, 1)
            dve.wait_ge(s_cum, 1)
            done(nc.vector.tensor_copy(pre[:], pp[:]))
            done(nc.vector.memset(tot[:], 0.0))
            done(nc.vector.memset(tot2[:], 0.0))
            done(nc.vector.tensor_copy(tot[:, :, NT + 1:2 * NT], pt[:, 0:NT - 1, :].rearrange("p t e -> p e t")))
            a, b = tot, tot2
            d = 1
            while d < NT:
                done(nc.vector.tensor_tensor(b[:, :, NT:2 * NT], a[:, :, NT:2 * NT], a[:, :, NT - d:2 * NT - d], ALU.add))
                a, b = b, a
                d *= 2
            done(nc.vector.tensor_tensor(pre[:], pre[:], a[:, :, NT:2 * NT].rearrange("p e t -> p t e"), ALU.add))
            done(nc.vector.tensor_tensor(pre[:], pre[:], hot[:], ALU.mult))
            done(nc.vector.tensor_reduce(loc[:], pre[:], AX_X, ALU.add))
            done(nc.vector.tensor_scalar(keep[:], loc[:], float(CAP), None, ALU.is_lt))
            done(nc.vector.tensor_tensor(pre[:], hot[:], cst[:, C_CAPE:C_CAPE + E].unsqueeze(1).to_broadcast(n), ALU.mult))
            done(nc.vector.tensor_reduce(idx[:], pre[:], AX_X, ALU.add))
            done(nc.vector.tensor_tensor(slot[:], idx[:], loc[:], ALU.add))
            done(nc.vector.tensor_scalar(tmp[:], keep[:], -1.0, -float(2 * TOK), ALU.add, ALU.mult))
            done(nc.vector.tensor_tensor(gate[:], gate[:], keep[:], ALU.mult))
            done(nc.vector.tensor_tensor(loc[:], slot[:], tmp[:], ALU.add))
            done(nc.vector.tensor_copy(slot_u[:], loc[:]))
            done(nc.vector.tensor_scalar(loc[:], slot[:], float(TOK - 1), None, ALU.min))
            nc.vector.tensor_copy(back_u[:], loc[:]).then_inc(s_slot, 1)

        @block.gpsimd
        def _(pool):
            pool.wait_ge(s_slot, 1)
            for t in range(NT):
                nc.gpsimd.indirect_dma_start(dr["disp"], bass.IndirectOffsetOnAxis(ap=slot_u[:, t:t + 1], axis=0),
                                             y1_all[:, t, :], None, bounds_check=TOK - 1, oob_is_err=False).then_inc(s_sc, 16)
            pool.wait_ge(s_sc, 16 * NT)


def phase_experts(nc, ins, dr, sem, sb, ps):
    w_all, b_all = dr["w_all"], dr["b_all"]
    ones = sb("ones", [1, P])
    ident = sb("ident4", [P, P])
    x = sb("xe", [P, E, CH, D])
    xT = sb("xeT", [P, 2, 2, CAP])
    y = sb("ye", [P, 2, CH, D])
    tp, py = ps("tpe", [P, 2, CAP]), ps("pye", [P, CH, 512])
    S = {n: sem("d_" + n) for n in "const ones load0 load1 tp xT ymm yout stored0 stored1".split()}

    with nc.Block() as block:
        @block.sync
        def _(sp):
            sp.dma_start(ident[:], ins["consts"][:, C_ID:C_ID + P]).then_inc(S["const"], 16)
            for e in range(E):
                sp.dma_start(x[:, e], dr["disp"][e * CAP:(e + 1) * CAP, :].rearrange("(a p) n -> p a n", p=P)).then_inc(S[f"load{e // (E // 2)}"], 16)
            for e in range(E):
                sp.wait_ge(S["yout"], e * CH + CH)
                sp.dma_start(dr["yexp"][e * CAP:(e + 1) * CAP, :].rearrange("(a p) n -> p a n", p=P), y[:, e % 2]).then_inc(S[f"stored{e % 2}"], 16)
            for u in range(2):
                sp.wait_ge(S[f"stored{u}"], 16 * (E // 2))

        @block.tensor
        def _(pe):
            def turn(e):
                pe.wait_ge(S[f"load{e // (E // 2)}"], 16 * (E // 2))
                if e:
                    pe.wait_ge(S["xT"], 2 * e)
                for k in range(2):
                    for a in range(CH):
                        last = nc.tensor.transpose(tp[:, k, a * P:(a + 1) * P], x[:, e, a, k * P:(k + 1) * P], ident[:])
                last.then_inc(S["tp"], 1)

            pe.wait_ge(S["const"], 16)
            pe.wait_ge(S["ones"], 1)
            turn(0)
            for e in range(E):
                if e + 1 < E:
                    turn(e + 1)
                pe.wait_ge(S["xT"], 2 * e + 2)
                for a in range(CH):
                    if e:
                        pe.wait_ge(S["yout"], (e - 1) * CH + a + 1)
                    for k in range(2):
                        nc.tensor.matmul(py[:, a, 0:D], xT[:, e % 2, k, a * P:(a + 1) * P], w_all[:, e, k, :], start=(k == 0), stop=False)
                    nc.tensor.matmul(py[:, a, 0:D], ones[:], b_all[:, e, :], start=False, stop=True).then_inc(S["ymm"], 1)

        @block.vector
        def _(dve):
            nc.vector.memset(ones[:], 1.0).then_inc(S["ones"], 1)
            for e in range(E):
                if e >= 2:
                    dve.wait_ge(S[f"stored{e % 2}"], 16 * (e // 2))
                for a in range(CH):
                    dve.wait_ge(S["ymm"], e * CH + a + 1)
                    nc.vector.tensor_copy(y[:, e % 2, a, :], py[:, a, 0:D]).then_inc(S["yout"], 1)

        @block.scalar
        def _(act):
            for e in range(E):
                act.wait_ge(S["tp"], e + 1)
                if e >= 2:
                    act.wait_ge(S["ymm"], (e - 1) * CH)
                for k in range(2):
                    nc.scalar.activation(xT[:, e % 2, k, :], tp[:, k, :], ACT.Copy).then_inc(S["xT"], 1)


def phase_gate(nc, ins, dr, sem, sb, ps):
    y1_all, gate, back_u = dr["y1_all"], dr["gate"], dr["back_u"]
    QT = NT // 4
    yg = sb("yg", [P, NT, D])
    g2, b2 = sb("g2", [P, D]), sb("b2ln", [P, D])
    stat, mv = sb("stat5", [P, 4, 6]), sb("mv5", [P, 4, 2])
    std, rstd = sb("std5", [P, 4]), sb("rstd5", [P, 4])
    z, ez = sb("z5", [P, 4, D]), sb("ez", [P, 4, D])
    S = {n: sem("e_" + n) for n in "weights gathered0 gathered1 gathered2 gathered3 z stats aggr eps std rstd n0 n1 n2 exp one rec out stored".split()}

    with nc.Block() as block:
        @block.sync
        def _(sp):
            sp.dma_start(g2[:], ins["g2"].partition_broadcast(P)).then_inc(S["weights"], 16)
            sp.dma_start(b2[:], ins["b2ln"].partition_broadcast(P)).then_inc(S["weights"], 16)
            for h in range(NT // 4):
                sp.wait_ge(S["out"], h + 1)
                sp.dma_start(dr["g"].rearrange("(t p) n -> p t n", p=P)[:, 4 * h:4 * h + 4, :], ez[:]).then_inc(S["stored"], 16)
            sp.wait_ge(S["stored"], 16 * (NT // 4))

        @block.gpsimd
        def _(pool):
            for t in range(NT):
                nc.gpsimd.indirect_dma_start(yg[:, t, :], None, dr["yexp"],
                                             bass.IndirectOffsetOnAxis(ap=back_u[:, t:t + 1], axis=0)).then_inc(S[f"gathered{t // QT}"], 16)

        @block.vector
        def _(dve):
            dve.wait_ge(S["weights"], 32)
            for h in range(NT // 4):
                if h % 2 == 0:
                    dve.wait_ge(S[f"gathered{h // 2}"], 16 * QT)
                if h:
                    dve.wait_ge(S["out"], h)
                for a in range(4):
                    t = 4 * h + a
                    nc.vector.scalar_tensor_tensor(z[:, a, :], yg[:, t, :], gate[:, t:t + 1], y1_all[:, t, :],
                                                   ALU.mult, ALU.add).then_inc(S["z"], 1)
                for a in range(4):
                    dve.wait_ge(S["z"], 4 * h + a + 1)
                    nc.vector.bn_stats(stat[:, a, :], z[:, a, :]).then_inc(S["stats"], 1)
                for a in range(4):
                    dve.wait_ge(S["stats"], 4 * h + a + 1)
                    nc.vector.bn_aggr(mv[:, a, :], stat[:, a, :]).then_inc(S["aggr"], 1)
                dve.wait_ge(S["aggr"], 4 * h + 4)
                nc.vector.tensor_scalar(std[:], mv[:, :, 1], EPS, None, ALU.add).then_inc(S["eps"], 1)
                dve.wait_ge(S["std"], h + 1)
                nc.vector.reciprocal(rstd[:], std[:]).then_inc(S["rstd"], 1)
                dve.wait_ge(S["rstd"], h + 1)
                for a in range(4):
                    nc.vector.tensor_scalar(z[:, a, :], z[:, a, :], mv[:, a, 0:1], rstd[:, a:a + 1],
                                            ALU.subtract, ALU.mult).then_inc(S["n0"], 1)
                dve.wait_ge(S["n0"], 4 * h + 4)
                nc.vector.tensor_tensor(z[:], z[:], g2[:].unsqueeze(1).to_broadcast([P, 4, D]), ALU.mult).then_inc(S["n1"], 1)
                dve.wait_ge(S["n1"], h + 1)
                nc.vector.tensor_tensor(z[:], z[:], b2[:].unsqueeze(1).to_broadcast([P, 4, D]), ALU.add).then_inc(S["n2"], 1)
                dve.wait_ge(S["exp"], h + 1)
                nc.vector.tensor_scalar(ez[:], ez[:], 1.0, None, ALU.add).then_inc(S["one"], 1)
                dve.wait_ge(S["one"], h + 1)
                nc.vector.reciprocal(ez[:], ez[:]).then_inc(S["rec"], 1)
                dve.wait_ge(S["rec"], h + 1)
                nc.vector.tensor_tensor(ez[:], z[:], ez[:], ALU.mult).then_inc(S["out"], 1)

        @block.scalar
        def _(act):
            for h in range(NT // 4):
                act.wait_ge(S["eps"], h + 1)
                nc.scalar.activation(std[:], std[:], ACT.Sqrt).then_inc(S["std"], 1)
                act.wait_ge(S["n2"], h + 1)
                if h:
                    act.wait_ge(S["stored"], 16 * h)
                nc.scalar.activation(ez[:], z[:], ACT.Exp, scale=-1.0).then_inc(S["exp"], 1)


def tile_at(i, k):
    if k >= 0:
        over = (i + k) // NI
        return (i + k) % NI, (2 * over if k < 3 else over + 1)
    inside = (i + k + NI) // NI
    return (i + k + NI) % NI, 1 - inside


def phase_attend(nc, ins, dr, sem, sb, ps):
    kt = sb("kt", [ROWS, 4, W], BF16)
    slots = sb("slots", [P, NI + NX, 2, HH, 64])
    qst = sb("qst", [ROWS, 2, W], BF16)
    qbd = sb("qbd", [P, 2, 2, HH, P], FP16)
    tks = sb("tks", [P, 2, TSW], FP16)
    tvs = sb("tvs", [P, 2, TVU * DK], FP16)
    pp2 = sb("prob_parts", [P, 3, 2, 2, HH, 64], FP16)
    vt = sb("vt", [P, 4, HH, VW])
    mx = sb("mxr", [P, 2, HH, 64])
    mb = sb("mb", [P, 2, HH, 64])
    rom = sb("rom", [P, 16, HH, 8])
    mcol = sb("mcol", [P, 8])
    pvs = sb("pvs", [P, 2, P])
    otn = sb("otn", [P, P])
    cst = sb("cst6", [P, C_TRI])
    spp = ps("spp", [P, 2, 2, HH, 64])
    ro = ps("ro", [P, 2, 8, HH, 8])
    pvp = ps("pvps", [P, 2, P])
    otp = ps("otp", [P, 2, P])
    mask = cst[:, C_MASK:C_MASK + 8]
    flat = slots[:].rearrange("p n a h l -> p (n a h l)")
    half_table = TVU * DK // 2
    tk_whole = flat[:, 0:TSW]
    tv_whole = flat[:, 2048:2048 + half_table]
    NG = NC * NI

    S = {n: sem("f_" + n) for n in (
        "tables tables2 split preset k0 k1 k2 k3 q0 q1 qbd_load0 qbd_load1 qbd v0 v1 v2 v3 scored stored "
        "mxd turned mcol mbp mb sub prob prob_hi prob_lo used rom pvs folded rden normed otout").split()}

    def slot(g2, k):
        if k in LAST:
            return slots[:, LAST.index(k) * 2 + g2]
        return slots[:, 2 * NX + USE.index(k)]

    def used_before(gg, band):
        return gg * NI + USE.index(BANDS[band - 3]) + 1 - (0 if band >= 3 else NI)

    def scores(pe, g, i, g2, m):
        k = SCORE[m]
        if m == 0:
            pe.wait_ge(S[f"q{g2}"], START + (g // 2 + 1) * 48)
            pe.wait_ge(S["qbd"], START + g * 8 + 8)
        pe.wait_ge(S[f"k{m % 4}"], START + (g * 4 + m // 4 + 1) * 32)
        if m == 0:
            pe.wait_ge(S["mcol"], START + g * 2)
        elif m == 1:
            pe.wait_ge(S["mb"], START + g * 2)
        else:
            pe.wait_ge(S["stored"], START + g * NI + m - 1)
        out = spp[:, m % 2]

        def product(h):
            for half in range(2):
                last = nc.tensor.matmul(out[:, half, h, :], kt[:, m % 4, h * P:(h + 1) * P],
                                        qst[:, g2, h * P + half * 64:h * P + half * 64 + 64],
                                        start=(h == 0), stop=(h == HH - 1), skip_group_check=True)
            return last

        def relative():
            for q in range(16):
                x0 = k * P - 8 * q - LOWEST - 7
                for a, b in PAIRS:
                    nc.tensor.matmul(out[:, q // 8, :, (q % 8) * 8:(q % 8) * 8 + 8], tks[:, a, x0:x0 + P],
                                     qbd[:, g2, b, :, 8 * q:8 * q + 8], start=False, stop=False, skip_group_check=True)

        for h in range(HH - 1):
            product(h)
        where_in_band(pe, i, k, relative)
        product(HH - 1).then_inc(S["scored"], 1)

    def where_in_band(pe, i, k, relative):
        if k == 0:
            relative()
        elif k in BANDS:
            with pe.If(i > -k - 1 if k < 0 else i < NI - k):
                relative()

    def values(pe, gg, i, g2, m):
        k = USE[m]
        pe.wait_ge(S[f"v{m % 4}"], START + (gg * 4 + m // 4 + 1) * 16)
        if k in BANDS:
            pe.wait_ge(S["prob_lo"], START + gg * NB + BANDS.index(k) + 1)
        else:
            pe.wait_ge(S["prob"], START + gg * NI + m + 1)
        if m == 0:
            pe.wait_ge(S["rom"], START + gg)
            pe.wait_ge(S["pvs"], START + gg)

        def relative():
            parts = pp2[:, BANDS.index(k) % 3]
            for q in range(16):
                u0 = k * P - 8 * q - 7 - LOWEST
                for t, (a, b) in enumerate(PAIRS):
                    nc.tensor.matmul(ro[:, q // 8, q % 8, :, :], tvs[:, a, u0 * DK:(u0 + 8) * DK],
                                     parts[:, b, q // 8, :, (q % 8) * 8:(q % 8) * 8 + 8],
                                     start=(m == 0 and q % 8 == 0 and t == 0), stop=False, skip_group_check=True)

        where_in_band(pe, i, k, relative)
        for h in range(HH):
            c, q = h % 4, h // 4
            last = nc.tensor.matmul(pvp[32 * c:32 * c + VW, q, :].rearrange("p (a l) -> p a l", a=2), vt[:, m % 4, h, :],
                                    slot(g2, k)[:, :, h, :], start=(m == 0 and q == 0), stop=(m == NI - 1),
                                    skip_group_check=True)
        last.then_inc(S["used"], 1)

    def turn_max(pe, g):
        pe.wait_ge(S["mxd"], START + (g + 1) * NI)
        pe.wait_ge(S["stored"], START + (g + 1) * NI)
        lanes = mx[:].rearrange("p a h l -> p (a h l)")
        tp = spp[:, 0].rearrange("p a h l -> p (a h l)")
        for half in range(2):
            for c in range(4 * half, 4 * half + 4):
                last = nc.tensor.transpose(tp[:, c * P:(c + 1) * P], lanes[:, c * P:(c + 1) * P], cst[:, C_ID:C_ID + P])
            last.then_inc(S["turned"], 1)

    def spread_max(pe, g):
        bc = spp[:, 1].rearrange("p a h l -> p (a h l)")
        for half in range(2):
            pe.wait_ge(S["mcol"], START + g * 2 + half + 1)
            for c in range(4 * half, 4 * half + 4):
                last = nc.tensor.matmul(bc[:, c * P:(c + 1) * P], mcol[:, c:c + 1].to_broadcast([P, P]), cst[:, C_ID:C_ID + P],
                                        start=True, stop=True)
            last.then_inc(S["mbp"], 1)

    def fold(pe, gg):
        pe.wait_ge(S["rom"], START + gg + 1)
        pe.wait_ge(S["pvs"], START + gg + 1)
        pe.wait_ge(S["normed"], START + gg)
        for h in range(HH):
            nc.tensor.matmul(otp[:, 0, :].rearrange("p (b l) -> p b l", b=16), cst[:, C_FOLD + 112 - 16 * h:C_FOLD + 240 - 16 * h],
                             rom[:, :, h, :], start=(h == 0), stop=False)
        for q in range(2):
            nc.tensor.matmul(otp[:, 0, :], cst[:, C_PICK + 64 - 64 * q:C_PICK + 192 - 64 * q], pvs[:, q, :],
                             start=False, stop=(q == 1))
        for q in range(2):
            last = nc.tensor.matmul(otp[:, 1, :], cst[:, C_DEN + 64 - 64 * q:C_DEN + 192 - 64 * q], pvs[:, q, :],
                                    start=(q == 0), stop=(q == 1))
        last.then_inc(S["folded"], 1)

    def over_groups(eng, body):
        with eng.Fori(0, NG // 2 - 1) as t:
            body(t * 2, 0, 2)
            body(t * 2 + 1, 1, 2)
        body(NG - 2, 0, 1)
        body(NG - 1, 1, 0)

    start_counts(nc, S)
    with nc.Block() as block:
        @block.sync
        def _(sp):
            sp.dma_start(cst[:], ins["consts"][:, 0:C_TRI]).then_inc(S["tables"], 16)
            tk, tv = dr["tk"], dr["tv"]
            for l in range(8):
                sp.dma_start(tk_whole[16 * l:16 * l + 16, :], tk[:, 7 - l:7 - l + TSW]).then_inc(S["tables"], 16)
            sp.dma_start(tv_whole, bass.AP(tv.tensor, 0, [[DK, P], [1, half_table]])).then_inc(S["tables"], 16)
            sp.wait_ge(S["split"], START + 4)
            sp.dma_start(tv_whole, bass.AP(tv.tensor, half_table, [[DK, P], [1, half_table]])).then_inc(S["tables2"], 16)

            def load_q(g, g2):
                row = dr["qs"][ds(g, 1), :].rearrange("a (p n) -> (a p) n", n=W)
                sp.dma_start(qst[0:QROWS, g2, :], row).then_inc(S[f"q{g2}"], 16)
                for cl in range(2):
                    at = QROWS + cl * PARTS
                    src = dr["cs"][ds(g, 1), cl].rearrange("a q h l -> (a q) (h l)")
                    sp.dma_start(qst[at:at + PARTS, g2, :], src).then_inc(S[f"q{g2}"], 16)
                for q in range(2):
                    src = bass.AP(dr["qp"].tensor, (g * 2 + q) * (DK * W), [[0, 8], [W, DK], [1, W]])
                    sp.dma_start(qbd[:, g2, q], src).then_inc(S[f"qbd_load{g2}"], 16)

            def load_key(g, i, m, scored):
                j, cls = tile_at(i, SCORE[m])
                if scored is not None:
                    sp.wait_ge(S["scored"], scored)
                row = dr["ks"][ds((g // NI) * NI + j, 1), :].rearrange("a (p n) -> (a p) n", n=W)
                sp.dma_start(kt[0:QROWS, m % 4, :], row).then_inc(S[f"k{m % 4}"], 16)
                src = ins["sel"][ds(cls, 1)].rearrange("a p n -> (a p) n")
                sp.dma_start(kt[QROWS:ROWS, m % 4, :].bitcast(U16), src).then_inc(S[f"k{m % 4}"], 16)

            def load_value(gg, i, m):
                j, cls = tile_at(i, USE[m])
                sp.wait_ge(S["used"], START + gg * NI + m - 3)
                src = dr["v"][ds(cls, 1), ds((gg // NI) * NI + j, 1)].rearrange("c a p n -> (c a p) n")
                sp.dma_start(vt[:, m % 4].rearrange("p h d -> p (h d)"), src).then_inc(S[f"v{m % 4}"], 16)

            def load_tile(gg, m, more):
                load_value(gg, gg % NI, m)
                if more:
                    load_key(gg + 1, (gg + 1) % NI, m, START + (gg + 1) * NI + max(m - 3, 0))

            def store(gg):
                sp.wait_ge(S["normed"], START + gg + 1)
                sp.dma_start(dr["ot"][ds(gg, 1)].rearrange("g p l -> p (g l)"), otn[:]).then_inc(S["otout"], 16)

            def head(gg, g2, ahead):
                for m in range(HEAD):
                    load_tile(gg, m, ahead)
                    if m == 1 and ahead > 1:
                        load_q(gg + 2, g2)

            def body(gg, g2, ahead):
                for m in range(HEAD, NI):
                    load_tile(gg, m, ahead)
                if ahead:
                    head(gg + 1, 1 - g2, ahead - 1)
                store(gg)

            HEAD = 7
            load_q(0, 0)
            load_q(1, 1)
            for m in range(NI):
                load_key(0, 0, m, START + m - 3 if m > 3 else None)
            head(0, 0, 3)
            with sp.Fori(0, NG // 2 - 2) as t:
                body(t * 2, 0, 3)
                body(t * 2 + 1, 1, 3)
            for gg in range(NG - 4, NG):
                body(gg, gg % 2, NG - 1 - gg)
            sp.wait_ge(S["otout"], START + 16 * NG)

        @block.tensor
        def _(pe):
            pe.wait_ge(S["tables"], START + 16 * 10)
            pe.wait_ge(S["preset"], START + 1)
            pe.wait_ge(S["split"], START + 6)

            def body(gg, g2, ahead):
                i, g, j2 = gg % NI, gg + 1, 1 - g2
                for m in range(NI - NX):
                    if ahead and m:
                        scores(pe, g, g % NI, j2, m)
                    values(pe, gg, i, g2, m)
                if ahead:
                    for m in range(NI - NX, NI):
                        scores(pe, g, g % NI, j2, m)
                values(pe, gg, i, g2, NI - 3)
                if ahead:
                    turn_max(pe, g)
                values(pe, gg, i, g2, NI - 2)
                if ahead:
                    spread_max(pe, g)
                if ahead == 2:
                    scores(pe, gg + 2, (gg + 2) % NI, g2, 0)
                values(pe, gg, i, g2, NI - 1)
                fold(pe, gg)

            for m in range(NI):
                scores(pe, 0, 0, 0, m)
            turn_max(pe, 0)
            spread_max(pe, 0)
            scores(pe, 1, 1, 1, 0)
            over_groups(pe, body)

        @block.scalar
        def _(act):
            def store_scores(g, g2, m, used):
                act.wait_ge(S["scored"], START + g * NI + m + 1)
                act.wait_ge(S["used"], START + used)
                nc.scalar.activation(slot(g2, SCORE[m]), spp[:, m % 2], ACT.Copy).then_inc(S["stored"], 1)

            def exps(gg, g2, m):
                k = USE[m]
                act.wait_ge(S["sub"], START + gg * NI + m + 1)
                if k in BANDS:
                    band = BANDS.index(k)
                    act.wait_ge(S["used"], START + used_before(gg, band))
                    nc.scalar.activation(pp2[:, band % 3, 0], slot(g2, k), ACT.Exp).then_inc(S["prob_hi"], 1)
                nc.scalar.activation(slot(g2, k), slot(g2, k), ACT.Exp).then_inc(S["prob"], 1)

            def diagonal(g, g2, l):
                if l == 0:
                    act.wait_ge(S[f"qbd_load{g2}"], START + (g // 2 + 1) * 32)
                q = qbd[:, g2].rearrange("p q h (b l) -> p (q h b) l", l=8)[:, :, l]
                nc.scalar.activation(q, q, ACT.Copy, scale=mask[:, l:l + 1]).then_inc(S["qbd"], 1)

            def max_out(g):
                act.wait_ge(S["sub"], START + g * NI)
                for half in range(2):
                    act.wait_ge(S["mbp"], START + g * 2 + half + 1)
                    nc.scalar.activation(mb[:, half], spp[:, 1, half], ACT.Copy).then_inc(S["mb"], 1)

            def body(gg, g2, ahead):
                exps(gg, g2, 1)
                for m in range(NI - NX):
                    if m == 0:
                        exps(gg, g2, 2)
                        exps(gg, g2, 3)
                    if m + 4 < NI - 1:
                        exps(gg, g2, m + 4)
                    if ahead:
                        k = SCORE[m]
                        store_scores(gg + 1, 1 - g2, m, gg * NI + (m + 1 - NX if k in LAST else USE.index(k) + 1))
                if ahead:
                    for m in range(NI - NX, NI):
                        store_scores(gg + 1, 1 - g2, m, gg * NI + USE.index(SCORE[m]) + 1)
                if ahead == 2:
                    for l in range(8):
                        diagonal(gg + 2, g2, l)
                exps(gg, g2, NI - 1)
                if ahead:
                    max_out(gg + 1)
                act.wait_ge(S["used"], START + (gg + 1) * NI)
                act.wait_ge(S["folded"], START + gg)
                nc.scalar.activation(pvs[:], pvp[:], ACT.Copy).then_inc(S["pvs"], 1)
                if ahead:
                    exps(gg + 1, 1 - g2, 0)

            act.wait_ge(S["tables"], START + 16 * 10)
            for g in range(2):
                for l in range(8):
                    diagonal(g, g, l)
            act.wait_ge(S["split"], START + 6)
            for m in range(NI):
                store_scores(0, 0, m, 0)
            max_out(0)
            exps(0, 0, 0)
            over_groups(act, body)

        @block.vector
        def _(dve):
            def running_max(g, g2, m):
                dve.wait_ge(S["stored"], START + g * NI + m + 1)
                if m == 1:
                    dve.wait_ge(S["turned"], START + g * 2)
                    nc.vector.tensor_tensor(mx[:], slot(g2, SCORE[0]), slot(g2, SCORE[1]), ALU.max).then_inc(S["mxd"], 2)
                elif m:
                    dve.wait_ge(S["mxd"], START + g * NI + m)
                    nc.vector.tensor_tensor(mx[:], mx[:], slot(g2, SCORE[m]), ALU.max).then_inc(S["mxd"], 1)

            def subtract(gg, g2, m):
                tile = slot(g2, USE[m])
                if m == 0:
                    dve.wait_ge(S["mb"], START + gg * 2 + 1)
                    nc.vector.tensor_tensor(tile[:, 0], tile[:, 0], mb[:, 0], ALU.subtract)
                    dve.wait_ge(S["mb"], START + gg * 2 + 2)
                    nc.vector.tensor_tensor(tile[:, 1], tile[:, 1], mb[:, 1], ALU.subtract).then_inc(S["sub"], 1)
                else:
                    nc.vector.tensor_tensor(tile, tile, mb[:], ALU.subtract).then_inc(S["sub"], 1)

            def low_part(gg, g2, m):
                k = USE[m]
                if k in BANDS:
                    band = BANDS.index(k)
                    dve.wait_ge(S["prob"], START + gg * NI + m + 1)
                    dve.wait_ge(S["used"], START + used_before(gg, band))
                    nc.vector.tensor_tensor(pp2[:, band % 3, 1], slot(g2, k), pp2[:, band % 3, 0],
                                            ALU.subtract).then_inc(S["prob_lo"], 1)

            def query_max(g):
                for half in range(2):
                    dve.wait_ge(S["turned"], START + g * 2 + half + 1)
                    nc.vector.tensor_reduce(mcol[:, 4 * half:4 * half + 4],
                                            spp[:, 0, half].rearrange("p h l -> p (h l)").rearrange("p (c r) -> p c r", c=4),
                                            AX_X, ALU.max).then_inc(S["mcol"], 1)

            def body(gg, g2, ahead):
                g, j2 = gg + 1, 1 - g2
                for m in range(NI - 3):
                    if m + 5 < NI - 1:
                        subtract(gg, g2, m + 5)
                    low_part(gg, g2, m + 1)
                    if ahead and m > 1:
                        running_max(g, j2, m - 2)
                if ahead:
                    for m in range(NI - 5, NI):
                        running_max(g, j2, m)
                low_part(gg, g2, NI - 2)
                subtract(gg, g2, NI - 1)
                if ahead:
                    query_max(g)
                low_part(gg, g2, NI - 1)
                if ahead:
                    subtract(g, j2, 0)
                    subtract(g, j2, 1)
                dve.wait_ge(S["used"], START + (gg + 1) * NI)
                dve.wait_ge(S["folded"], START + gg)
                nc.vector.tensor_tensor(rom[:].rearrange("p b h l -> p (b h) l"), ro[:].rearrange("p a b h l -> p (a b h) l"),
                                        own.to_broadcast([P, P, 8]), ALU.mult).then_inc(S["rom"], 1)
                if ahead:
                    subtract(g, j2, 2)
                    low_part(g, j2, 0)
                    subtract(g, j2, 3)
                    subtract(g, j2, 4)
                dve.wait_ge(S["folded"], START + gg + 1)
                dve.wait_ge(S["otout"], START + gg * 16)
                nc.vector.reciprocal(otn[:], otp[:, 1, :]).then_inc(S["rden"], 1)
                dve.wait_ge(S["rden"], START + gg + 1)
                nc.vector.tensor_tensor(otn[:], otp[:, 0, :], otn[:], ALU.mult).then_inc(S["normed"], 1)

            nc.vector.memset(pvp[:], 0.0).then_inc(S["preset"], 1)
            dve.wait_ge(S["tables"], START + 16 * 10)
            step = START
            for dst, src in ((tks[:], tk_whole), (tvs[:, :, 0:half_table], tv_whole), (tvs[:, :, half_table:], tv_whole)):
                if step == START + 4:
                    dve.wait_ge(S["tables2"], START + 16)
                nc.vector.tensor_copy(dst[:, 0], src).then_inc(S["split"], 1)
                dve.wait_ge(S["split"], step + 1)
                nc.vector.tensor_tensor(dst[:, 1], src, dst[:, 0], ALU.subtract).then_inc(S["split"], 1)
                step += 2
                dve.wait_ge(S["split"], step)
            own = cst[:, C_MASKV:C_MASKV + 8].unsqueeze(1)
            for m in range(NI):
                running_max(0, 0, m)
            query_max(0)
            for m in range(5):
                subtract(0, 0, m)
            low_part(0, 0, 0)
            over_groups(dve, body)


def phase_out(nc, ins, dr, sem, sb, ps):
    wo, bo = sb("woA", [P, 2, D]), sb("boA", [P, D])
    ot = sb("ot", [P, 2, 2, CH, P])
    x, g, y = sb("x6", [P, 2, CH, D]), sb("g6", [P, 2, CH, D]), sb("y6", [P, 2, CH, D])
    pp = ps("p6", [P, CH, 512])
    S = {n: sem("g_" + n) for n in "weights load0 load1 proj biased gated out store0 store1".split()}
    xv, gv, ov = (t.rearrange("(c a p) n -> p c a n", a=CH, p=P) for t in (ins["x"], dr["g"], ins["out"]))

    with nc.Block() as block:
        @block.sync
        def _(sp):
            sp.dma_start(wo[:], ins["woAT"].rearrange("(k p) n -> p k n", p=P)).then_inc(S["weights"], 16)
            sp.dma_start(bo[:], ins["boA"].partition_broadcast(P)).then_inc(S["weights"], 16)
            for ch in range(NCH):
                u = ch % 2
                if ch >= 2:
                    sp.wait_ge(S["out"], ch - 1)
                b, i0 = ch // 4, (ch % 4) * CH
                for half in range(2):
                    r = (2 * b + half) * NI + i0
                    sp.dma_start(ot[:, u, half], dr["ot"][r:r + CH].rearrange("g p l -> p g l")).then_inc(S[f"load{u}"], 16)
                sp.dma_start(x[:, u], xv[:, ch]).then_inc(S[f"load{u}"], 16)
                sp.dma_start(g[:, u], gv[:, ch]).then_inc(S[f"load{u}"], 16)

        @block.tensor
        def _(pe):
            pe.wait_ge(S["weights"], 32)
            for ch in range(NCH):
                u = ch % 2
                pe.wait_ge(S[f"load{u}"], 64 * (ch // 2 + 1))
                if ch:
                    pe.wait_ge(S["biased"], ch)
                for a in range(CH):
                    for half in range(2):
                        last = nc.tensor.matmul(pp[:, a, 0:D], ot[:, u, half, a, :], wo[:, half, :], start=(half == 0), stop=(half == 1))
                last.then_inc(S["proj"], 1)

        @block.vector
        def _(dve):
            dve.wait_ge(S["weights"], 32)
            for ch in range(NCH):
                u = ch % 2
                dve.wait_ge(S["proj"], ch + 1)
                if ch >= 2:
                    dve.wait_ge(S[f"store{u}"], 16 * (ch // 2))
                nc.vector.tensor_tensor(y[:, u], pp[:, :, 0:D], bo[:].unsqueeze(1).to_broadcast([P, CH, D]), ALU.add).then_inc(S["biased"], 1)
                dve.wait_ge(S["biased"], ch + 1)
                nc.vector.tensor_tensor(y[:, u], y[:, u], g[:, u], ALU.mult).then_inc(S["gated"], 1)
                dve.wait_ge(S["gated"], ch + 1)
                nc.vector.tensor_tensor(y[:, u], y[:, u], x[:, u], ALU.add).then_inc(S["out"], 1)

        @block.scalar
        def _(act):
            for ch in range(NCH):
                act.wait_ge(S["out"], ch + 1)
                act.dma_start(ov[:, ch], y[:, ch % 2]).then_inc(S[f"store{ch % 2}"], 16)
            for u in range(2):
                act.wait_ge(S[f"store{u}"], 16 * (NCH // 2))


def build(nc, ins):
    def dram(name, shape, dt=F32):
        return nc.dram_tensor(name, shape, dt, kind="Internal").ap()

    def scoped(ctx):
        def sb(name, shape, dt=F32):
            return ctx.enter_context(nc.sbuf_tensor(name, shape, dt))

        def ps(name, shape, dt=F32):
            return ctx.enter_context(nc.psum_tensor(name, shape, dt))

        return sb, ps

    dr = {
        "qs": dram("q_parts", [NC * NI, TERMS * DK * W], BF16),
        "ks": dram("k_parts", [NC * NI, TERMS * DK * W], BF16),
        "qp": dram("q_pair", [NC * NI, 2, DK * W], FP16),
        "cs": dram("class_constants", [NC * NI, 2, PARTS, HH, P], BF16),
        "v": dram("v_rows", [3, NC * NI, P, HH * VW]),
        "tk": dram("key_table", [DK, SPAN]),
        "tv": dram("value_table", [SPAN, DK]),
        "disp": dram("dispatched", [TOK, D]),
        "yexp": dram("expert_rows", [TOK, D]),
        "g": dram("gate_rows", [TOK, D]),
        "ot": dram("attention_out", [NC * NI, P, P]),
    }
    with ExitStack() as whole:
        def sem(name):
            return whole.enter_context(nc.semaphore(name))

        with ExitStack() as gate_scope:
            sb, _ = scoped(gate_scope)
            dr["xn_all"] = dr["y1_all"] = sb("xn_all", [P, NT, D])
            dr["logits"] = sb("logits", [P, NT, E])
            dr["gate"] = sb("gate", [P, NT])
            dr["slot_u"], dr["back_u"] = sb("slot_u", [P, NT], U32), sb("back_u", [P, NT], U32)
            shared = sb("shared", [P, E * 3 * D])
            dr["shared"] = shared
            dr["w_all"] = shared[:, 0:2 * E * D].rearrange("p (e k n) -> p e k n", e=E, k=2)
            dr["b_all"] = shared[0:1, 2 * E * D:].rearrange("p (e n) -> p e n", e=E)
            with ExitStack() as first:
                sb, _ = scoped(first)
                dr["qkv_all"] = sb("qkv_all", [P, NT, 3 * D])
                with ExitStack() as c:
                    phase_project(nc, ins, dr, sem, *scoped(c))
                with ExitStack() as c:
                    phase_pairs(nc, ins, dr, sem, *scoped(c))
            for phase in (phase_route, phase_experts, phase_gate):
                with ExitStack() as c:
                    phase(nc, ins, dr, sem, *scoped(c))
        for phase in (phase_attend, phase_out):
            with ExitStack() as c:
                phase(nc, ins, dr, sem, *scoped(c))


def kernel(**inputs):
    import numpy as np
    import concourse.bacc as bacc
    from concourse.bass_utils import run_bass_kernel_spmd

    a = {k: np.asarray(v) for k, v in inputs.items()}

    def half_heads(w):
        return w.reshape(-1, 2, HH, DK).transpose(0, 1, 3, 2).reshape(-1, D)

    def columns(b):
        return half_heads(b[None, :]).reshape(2, P).T

    consts = np.zeros((P, C_N), np.float32)
    p = np.arange(P)
    consts[p, C_ID + p] = 1
    consts[p, C_FOLD + 112 + p % 16] = 1
    for c in range(4):
        for d in range(DK):
            consts[32 * c + d, C_PICK + 64 + 16 * c + d] = 1
            consts[32 * c + DK, C_DEN + 64 + 16 * c + d] = 1
    consts[p, C_MASK + p // 16] = 1
    consts[p, C_MASKV + 7 - p // 16] = 1
    consts[:, C_TRI:C_TRI + P] = p[:, None] < p[None, :]
    consts[:, C_ONE:C_ONE + P] = 1
    consts[p, C_HEAD + p % HH] = 1
    consts[:, C_IOTA:C_IOTA + E] = E - np.arange(E)
    consts[:, C_CAPE:C_CAPE + E] = CAP * np.arange(E)

    sel = np.zeros((3, 2 * PARTS, W), np.uint16)
    sel[HI, :PARTS] = sel[LO, PARTS:] = 0x3F80

    host = {
        "x": a["L0_attn_x"].reshape(TOK, D),
        "wqT": half_heads(a["L0_attn_Wq"].T), "wkT": half_heads(a["L0_attn_Wk"].T), "wvT": a["L0_attn_Wv"].T,
        "wiT": a["L0_ffn_in_proj_w"].T, "woT": a["L0_ffn_out_proj_w"].T, "woAT": a["L0_attn_Wo"].T,
        "bqk": np.concatenate([columns(a["L0_attn_bq"]), columns(a["L0_attn_bk"])], 1),
        "bv": a["L0_attn_bv"], "bi": a["L0_ffn_in_proj_b"], "bo_f": a["L0_ffn_out_proj_b"], "boA": a["L0_attn_bo"],
        "rk": a["L0_attn_relative_k"], "rkT": a["L0_attn_relative_k"].T,
        "rv": a["L0_attn_relative_v"],
        "g1": a["L0_ffn_ln1_g"], "b1ln": a["L0_ffn_ln1_b"], "g2": a["L0_ffn_ln2_g"], "b2ln": a["L0_ffn_ln2_b"],
        "wg": a["L0_ffn_wg"], "w1T": a["L0_ffn_w1"].transpose(0, 2, 1), "w2": a["L0_ffn_w2"],
        "b1e": a["L0_ffn_b1"].reshape(E, FF // P, P).transpose(0, 2, 1), "b2e": a["L0_ffn_b2"], "consts": consts, "sel": sel,
    }
    nc = bacc.Bacc("TRN2", target_bir_lowering=False, num_devices=1)
    arrays, ins = {}, {}
    for name, v in host.items():
        arrays["in_" + name] = np.ascontiguousarray(v)
        ins[name] = nc.dram_tensor("in_" + name, v.shape, mybir.dt.from_np(v.dtype), kind="ExternalInput").ap()
    ins["out"] = nc.dram_tensor("out", (TOK, D), F32, kind="ExternalOutput").ap()
    build(nc, ins)
    r = run_bass_kernel_spmd(nc, [arrays], core_ids=[0])
    return r.results[0]["out"].reshape(B, L, D)
```
